# Optimizing a Trainium2 kernel written in Bass

```python
import numpy as np
import jax
import jax.numpy as jnp

def _softmax(x, axis=-1):
    return jax.nn.softmax(x, axis=axis)

def _gelu(x):
    return jax.nn.gelu(x, approximate=True)

def _silu(x):
    return jax.nn.silu(x)

def _sigmoid(x):
    return jax.nn.sigmoid(x)

def _layernorm(x, axis=-1, eps=1e-05):
    m = jnp.mean(x, axis=axis, keepdims=True)
    v = jnp.var(x, axis=axis, keepdims=True)
    return (x - m) / jnp.sqrt(v + eps)

def _scatter_add(tgt, idx, src, axis=0):
    return tgt.at[idx].add(src)

def _segment_sum(src, seg, n):
    return jax.ops.segment_sum(src, seg, n)
kernel_name = 'mk_gnn_resnorm_d2_gnn_r8_b3f411'

def setup_inputs(seed: int=0):
    np.random.seed(seed)
    _w = jnp.asarray

    def _rec_inputs():
        import jax
        import jax.numpy as jnp
        _gk = jax.random.key(seed)
        x = -0.000202 + 1 * jax.random.normal(jax.random.fold_in(_gk, 1), (6250, 128), jnp.float32)
        _s = jax.random.randint(jax.random.fold_in(_gk, 2), (50000,), 0, 6250, jnp.int32)
        _d = jax.random.randint(jax.random.fold_in(_gk, 3), (50000,), 0, 6250, jnp.int32)
        _loop = jnp.arange(6250, dtype=jnp.int32)
        src = jnp.concatenate([_s, _d, _loop])
        dst = jnp.concatenate([_d, _s, _loop])
        _o = jnp.argsort(dst, stable=True)
        src = src[_o]
        dst = dst[_o]
        edge_type_8 = jax.random.randint(jax.random.fold_in(_gk, 12), (106250,), 0, 8, jnp.int32)
        return (x, src, dst, edge_type_8)
    x, src, dst, edge_type_8 = _rec_inputs()

    def _L0_gnn_setup():
        import jax, jax.numpy as jnp
        import numpy as np
        N_NODES = 6250
        N_EDGES = 100000
        IN_C = 128
        OUT_C = 128
        BN_EPS = 1e-05

        def mish(x):
            return x * jnp.tanh(jax.nn.softplus(x))
        key = jax.random.key(seed)
        ks = jax.random.split(key, 7)
        x = jax.random.normal(ks[0], (N_NODES, IN_C), dtype=jnp.float32)
        edge_index = jax.random.randint(ks[1], (2, N_EDGES), 0, N_NODES, dtype=jnp.int64)
        s1 = 1.0 / np.sqrt(2 * IN_C)
        s2 = 1.0 / np.sqrt(OUT_C)
        W1 = jax.random.uniform(ks[2], (2 * IN_C, OUT_C), jnp.float32, -s1, s1)
        b1 = jax.random.uniform(ks[3], (OUT_C,), jnp.float32, -s1, s1)
        W2 = jax.random.uniform(ks[4], (OUT_C, OUT_C), jnp.float32, -s2, s2)
        b2 = jax.random.uniform(ks[5], (OUT_C,), jnp.float32, -s2, s2)
        gamma = jnp.ones((OUT_C,), jnp.float32)
        beta = jnp.zeros((OUT_C,), jnp.float32)
        return {'x': x, 'edge_index': edge_index, 'W1': W1, 'b1': b1, 'W2': W2, 'b2': b2, 'gamma': gamma, 'beta': beta}
    _L0_gnn_all = _L0_gnn_setup()
    _L0_gnn_in = {k: v for k, v in _L0_gnn_all.items() if k in ('W1', 'b1', 'W2', 'b2', 'gamma', 'beta')}
    del _L0_gnn_all

    def _L1_gnn_setup():
        import jax, jax.numpy as jnp
        import numpy as np
        N, E, D, R = (6250, 75000, 128, 8)

        def rgcn_conv(x, src, dst, etype, W, root, bias):
            n = x.shape[0]
            r = W.shape[0]
            xw = jnp.einsum('nd,rdo->rno', x, W)
            seg = etype * n + dst
            counts = jax.ops.segment_sum(jnp.ones(src.shape, dtype=x.dtype), seg, num_segments=r * n)
            norm = 1.0 / jnp.maximum(counts[seg], 1.0)
            msg = xw[etype, src] * norm[:, None]
            agg = jax.ops.segment_sum(msg, dst, num_segments=n)
            return agg + x @ root + bias
        key = jax.random.key(seed)
        ks = jax.random.split(key, 16)
        s = 1.0 / np.sqrt(D)
        inp = {'x': jax.random.normal(ks[0], (N, D), dtype=jnp.float32), 'edge_index': jax.random.randint(ks[1], (2, E), 0, N, dtype=jnp.int32), 'edge_type': jax.random.randint(ks[2], (E,), 0, R, dtype=jnp.int32), 'W1': jax.random.normal(ks[3], (R, D, D), dtype=jnp.float32) * s, 'root1': jax.random.normal(ks[4], (D, D), dtype=jnp.float32) * s, 'b1': jnp.zeros((D,), dtype=jnp.float32), 'W2': jax.random.normal(ks[5], (R, D, D), dtype=jnp.float32) * s, 'root2': jax.random.normal(ks[6], (D, D), dtype=jnp.float32) * s, 'b2': jnp.zeros((D,), dtype=jnp.float32), 'W3': jax.random.normal(ks[7], (R, D, D), dtype=jnp.float32) * s, 'root3': jax.random.normal(ks[8], (D, D), dtype=jnp.float32) * s, 'b3': jnp.zeros((D,), dtype=jnp.float32), 'res_w': jax.random.normal(ks[9], (D, D), dtype=jnp.float32) * s, 'res_b': jnp.zeros((D,), dtype=jnp.float32)}
        return inp
    _L1_gnn_all = _L1_gnn_setup()
    _L1_gnn_in = {k: v for k, v in _L1_gnn_all.items() if k in ('W1', 'root1', 'b1', 'W2', 'root2', 'b2', 'W3', 'root3', 'b3', 'res_w', 'res_b')}
    del _L1_gnn_all
    return {'x': x, 'src': src, 'dst': dst, 'edge_type_8': edge_type_8, 'L0_gnn_W1': _L0_gnn_in['W1'], 'L0_gnn_b1': _L0_gnn_in['b1'], 'L0_gnn_W2': _L0_gnn_in['W2'], 'L0_gnn_b2': _L0_gnn_in['b2'], 'L0_gnn_gamma': _L0_gnn_in['gamma'], 'L0_gnn_beta': _L0_gnn_in['beta'], 'L1_gnn_W1': _L1_gnn_in['W1'], 'L1_gnn_root1': _L1_gnn_in['root1'], 'L1_gnn_b1': _L1_gnn_in['b1'], 'L1_gnn_W2': _L1_gnn_in['W2'], 'L1_gnn_root2': _L1_gnn_in['root2'], 'L1_gnn_b2': _L1_gnn_in['b2'], 'L1_gnn_W3': _L1_gnn_in['W3'], 'L1_gnn_root3': _L1_gnn_in['root3'], 'L1_gnn_b3': _L1_gnn_in['b3'], 'L1_gnn_res_w': _L1_gnn_in['res_w'], 'L1_gnn_res_b': _L1_gnn_in['res_b']}

def reference(x, src, dst, edge_type_8, L0_gnn_W1, L0_gnn_b1, L0_gnn_W2, L0_gnn_b2, L0_gnn_gamma, L0_gnn_beta, L1_gnn_W1, L1_gnn_root1, L1_gnn_b1, L1_gnn_W2, L1_gnn_root2, L1_gnn_b2, L1_gnn_W3, L1_gnn_root3, L1_gnn_b3, L1_gnn_res_w, L1_gnn_res_b):
    import jax
    import jax.numpy as jnp

    def _L0_gnn_ref(x, edge_index, W1, b1, W2, b2, gamma, beta):
        import jax, jax.numpy as jnp
        import numpy as np
        N_NODES = 6250
        N_EDGES = 100000
        IN_C = 128
        OUT_C = 128
        BN_EPS = 1e-05

        def mish(x):
            return x * jnp.tanh(jax.nn.softplus(x))
        src, dst = (edge_index[0], edge_index[1])
        x_i = x[dst]
        x_j = x[src]
        feat = jnp.concatenate([x_i, x_j - x_i], axis=-1)
        h = mish(feat @ W1 + b1)
        m = h @ W2 + b2
        agg = jax.ops.segment_max(m, dst, num_segments=N_NODES)
        agg = jnp.where(jnp.isneginf(agg), 0.0, agg)
        mean = jnp.mean(agg, axis=0)
        var = jnp.mean(jnp.square(agg - mean), axis=0)
        y = (agg - mean) * jax.lax.rsqrt(var + BN_EPS) * gamma + beta
        return y

    def _L1_gnn_ref(x, edge_index, edge_type, W1, root1, b1, W2, root2, b2, W3, root3, b3, res_w, res_b):
        import jax, jax.numpy as jnp
        import numpy as np
        N, E, D, R = (6250, 75000, 128, 8)

        def rgcn_conv(x, src, dst, etype, W, root, bias):
            n = x.shape[0]
            r = W.shape[0]
            xw = jnp.einsum('nd,rdo->rno', x, W)
            seg = etype * n + dst
            counts = jax.ops.segment_sum(jnp.ones(src.shape, dtype=x.dtype), seg, num_segments=r * n)
            norm = 1.0 / jnp.maximum(counts[seg], 1.0)
            msg = xw[etype, src] * norm[:, None]
            agg = jax.ops.segment_sum(msg, dst, num_segments=n)
            return agg + x @ root + bias
        src, dst = (edge_index[0], edge_index[1])
        res = x @ res_w + res_b
        h = jax.nn.relu(rgcn_conv(x, src, dst, edge_type, W1, root1, b1))
        h = res + jax.nn.relu(h)
        h = jax.nn.relu(rgcn_conv(h, src, dst, edge_type, W2, root2, b2))
        h = res + jax.nn.relu(h)
        h = jax.nn.relu(rgcn_conv(h, src, dst, edge_type, W3, root3, b3))
        h = res + jax.nn.relu(h)
        return h
    edge_index = jnp.stack([src, dst])
    x = _layernorm(x + _L0_gnn_ref(x, edge_index, L0_gnn_W1, L0_gnn_b1, L0_gnn_W2, L0_gnn_b2, L0_gnn_gamma, L0_gnn_beta), axis=-1)
    x = _layernorm(x + _L1_gnn_ref(x, edge_index, edge_type_8, L1_gnn_W1, L1_gnn_root1, L1_gnn_b1, L1_gnn_W2, L1_gnn_root2, L1_gnn_b2, L1_gnn_W3, L1_gnn_root3, L1_gnn_b3, L1_gnn_res_w, L1_gnn_res_b), axis=-1)
    return x

_drawn_inputs = setup_inputs


def setup_inputs(seed=0):
    import zlib

    import numpy as np

    out = dict(_drawn_inputs(seed))
    spreads = {'L0_gnn_gamma': (1.0, 0.2),
     'L0_gnn_beta': (0.0, 0.1),
     'L1_gnn_b1': (0.0, 0.1),
     'L1_gnn_b2': (0.0, 0.282),
     'L1_gnn_b3': (0.0, 0.543),
     'L1_gnn_res_b': (0.0, 0.1)}
    factors = {'L0_gnn_b2': 8.0}
    for name, (base, spread) in spreads.items():
        noise = np.random.default_rng([zlib.crc32(name.encode()), seed]).standard_normal(out[name].shape)
        drawn = base * np.exp(spread * noise) if base else spread * noise
        out[name] = jnp.asarray(drawn.astype(out[name].dtype))
    for name, factor in factors.items():
        out[name] = (out[name] * factor).astype(out[name].dtype)
    return out
```

```python
from contextlib import ExitStack, nullcontext

import concourse.bass as bass
from concourse import mybir

ALU = mybir.AluOpType
ACT = mybir.ActivationFunctionType
AX = mybir.AxisListType
F32 = mybir.dt.float32
BF16 = mybir.dt.bfloat16
I32 = mybir.dt.int32
SP, DVE = mybir.EngineType.SP, mybir.EngineType.DVE

P = 128
WINDOW = 16
GROUP = 4
SLOTS = 4
CHUNK = 4 * P
BIG = 2.0 ** 100
SPLIT = 3
EPS = 1e-5
EXP_LIMIT = 30.0


def run_steps(engine, step, count, lag, unroll):
    first = 2 * unroll
    assert lag <= first
    stop = count - count % unroll
    for s in range(first):
        step(s, s % unroll)
    with engine.Fori(first // unroll, stop // unroll) as i:
        for phase in range(unroll):
            step(i * unroll + phase, phase)
    for s in range(stop, count + lag):
        step(s, s % unroll)


def active(s, lag, count):
    return not isinstance(s, int) or 0 <= s - lag < count


def later(s, n):
    return not isinstance(s, int) or s >= n


def build_gnn(nc, x, src, dst, edge_type, w1, b1, w2, b2, gamma, beta, conv_w, conv_root, conv_b, res_w, res_b, out):
    N, D = x.shape
    E = src.shape[0]
    R = conv_w[0].shape[0]
    LAYERS = len(conv_w)
    assert D == P and R * WINDOW == P
    UNIT = P * GROUP * SLOTS
    GROUPS = -(-E // UNIT) * SLOTS
    TILES = GROUPS * GROUP
    BLOCKS = -(-(TILES + GROUP * SLOTS) // P)
    COLS = BLOCKS * P
    CHUNKS = -(-N // CHUNK)
    NP = -(-N // P) * P
    LAST = NP - (CHUNKS - 1) * CHUNK
    assert NP >= N + WINDOW and LAST % P == 0 and CHUNKS % 2 == 1
    PAD_DST = 2 * N
    MAX_STEPS = (N - 1) // WINDOW
    STAT = next(n for n in range(512, 0, -1) if N % n == 0)
    SIDE = 16 * (2 + GROUP)

    def width(c):
        return (LAST if c == CHUNKS - 1 else CHUNK) if isinstance(c, int) else CHUNK

    with ExitStack() as ctx:
        sems = []

        def sb(name, shape, dt=F32):
            return ctx.enter_context(nc.sbuf_tensor(name, shape, dt))

        def sem(name):
            s = ctx.enter_context(nc.semaphore(name))
            sems.append(s)
            return s

        def dram(name, shape, dt=F32):
            return nc.dram_tensor(name, shape, dt).ap()

        p_tab = dram("p_tab", [NP * SPLIT, P], BF16)
        q_tab = dram("q_tab", [NP, P])
        h_tab = dram("h_tab", [NP, P])
        x1_tab = dram("x1_tab", [NP, P])
        rel_tab = dram("rel_tab", [COLS, P], BF16)
        reset_tab = dram("reset_tab", [COLS, P], BF16)
        fac_tab = dram("fac_tab", [NP, SPLIT * R], BF16)

        acc = sb("acc", [P, NP])
        res_buf = sb("res_buf", [P, max(NP, TILES * R)])
        type_hot = res_buf[:, 0:TILES * R].rearrange("p (t r) -> p t r", r=R)
        cnt = sb("cnt", [R, NP])
        ident = sb("ident", [P, P])
        iota_p = sb("iota_p", [P, 1])
        iota_split = sb("iota_split", [P, 1])
        iota_row = sb("iota_row", [P, P])
        big_mat = sb("big_mat", [P, P])
        negbig_row = sb("negbig_row", [1, P])
        ones_row = sb("ones_row", [1, P])
        wsteps = sb("wsteps", [1, MAX_STEPS])
        w_pq = sb("w_pq", [P, 2 * P])
        w1a = sb("w1a", [P, P])
        b1_rows = sb("b1_rows", [P, P])
        w2m = sb("w2m", [P, P])
        cols = sb("cols", [P, 4 + LAYERS + 1])
        w_all = sb("w_all", [P, (LAYERS + 1) * R * P])
        root_all = sb("root_all", [P, (LAYERS + 1) * P])
        w_cur = sb("w_cur", [P, R * P])
        root_cur = sb("root_cur", [P, P])
        b_cur = sb("b_cur", [P, 1])
        resw_sb = sb("resw_sb", [P, P])
        dst_f = sb("dst_f", [P, BLOCKS, P])
        lo = sb("lo", [P, BLOCKS])
        base_f = sb("base_f", [P, BLOCKS])
        src_c = sb("src_c", [P, COLS])
        type_c = sb("type_c", [P, COLS])
        last_c = sb("last_c", [P, COLS])
        keys = sb("keys", [P, COLS, 2])
        key_rn = sb("key_rn", [P, COLS])
        base_i = sb("base_i", [1, COLS], I32)
        facts = sb("facts", [P, 4])
        norm = sb("norm", [P, 2])
        facts_row = sb("facts_row", [1, 4])
        passes_i = sb("passes_i", [1, 2], I32)
        shift = sb("shift", [P, 4])
        rows = sb("rows", [P, SLOTS * GROUP, P])
        idx_stage = sb("idx_stage", [P, SLOTS * GROUP], I32)
        arena = sb("arena", [P, 9 * 1024])

        def carve():
            at = [0]

            def take(shape, dt=F32, parts=P):
                n = 1
                for k in shape:
                    n *= k
                words = n if dt != BF16 else n // 2
                v = arena[0:parts, at[0]:at[0] + words]
                at[0] += words
                assert at[0] <= 9 * 1024
                if dt != F32:
                    v = v.bitcast(dt)
                names = "abcd"[:len(shape)]
                if len(shape) > 1:
                    v = v.rearrange("p (" + " ".join(names) + ") -> p " + " ".join(names),
                                    **{names[k]: shape[k] for k in range(1, len(shape))})
                return v
            return take

        banks = [ctx.enter_context(nc.psum_tensor(f"bank{i}", [P, 512], F32)) for i in range(8)]

        chain = sem("chain")
        act_chain = sem("act_chain")
        landed = sem("landed")
        landed2 = [sem(f"landed2_{k}") for k in range(2)]
        landed3 = [sem(f"landed3_{k}") for k in range(2)]
        stored = [sem(f"stored_{k}") for k in range(2)]
        stored2 = [sem(f"stored2_{k}") for k in range(2)]
        filled = sem("filled")
        row_landed = [sem(f"row_landed{t}") for t in range(SLOTS * GROUP)]
        side_landed = [sem(f"side_landed{g}") for g in range(SLOTS)]
        idx_ready, gather_go = sem("idx_ready"), sem("gather_go")
        hot_ready, z_done, clamp_ready, recip_ready, g_ready = (sem(n) for n in (
            "hot_ready", "z_done", "clamp_ready", "recip_ready", "g_ready"))
        m_done, scan_done, turned, turned_copied, select_ready, window_done, merged = (sem(n) for n in (
            "m_done", "scan_done", "turned", "turned_copied", "select_ready", "window_done", "merged"))
        stood = sem("stood")
        spread_ready, spread_done, z_copied, scaled = (sem(n) for n in (
            "spread_ready", "spread_done", "z_copied", "scaled"))

        def block_end():
            numbers = [s.num for s in sems]
            span = range(min(numbers), max(numbers) + 1)
            assert len(span) == len(sems)
            nc.gpsimd.dma_reset(span)
            nc.gpsimd.sem_clear(span)
            nc.all_engine_barrier()

        def stand(engine):
            engine.sem_inc(stood, 1)

        def linker(engine, semaphore):
            count = [0]

            def link(instruction):
                count[0] += 1
                instruction.then_inc(semaphore, 1)
                engine.wait_ge(semaphore, count[0])
            return link

        take = carve()
        dst_i, src_i, type_i = (take([BLOCKS, P], I32) for _ in range(3))
        src_f, type_f, starts, lasts, tmp_r = (take([BLOCKS, P]) for _ in range(5))
        reset_bf = take([BLOCKS, P], BF16)
        hi, pair, top = take([BLOCKS]), take([2]), take([1, 8])
        hits = take([MAX_STEPS])
        FULL = E // P
        WHOLE = FULL // P
        TAIL = E - FULL * P
        with nc.Block() as block:
            @block.sync
            def _(sp):
                sp.wait_ge(filled, 1)
                for table, edges in ((dst_i, dst), (src_i, src), (type_i, edge_type)):
                    sp.dma_start(table[:, 0:WHOLE, :],
                                 edges[0:WHOLE * P * P].rearrange("(a q e) -> q a e", q=P, e=P)).then_inc(landed, 16)
                    sp.dma_start(table[0:FULL - WHOLE * P, WHOLE, :],
                                 edges[WHOLE * P * P:FULL * P].rearrange("(q e) -> q e", e=P)).then_inc(landed, 16)
                    sp.dma_start(table[FULL - WHOLE * P:FULL - WHOLE * P + 1, WHOLE, 0:TAIL],
                                 edges[FULL * P:E].rearrange("(a e) -> a e", a=1)).then_inc(landed, 16)
                sp.dma_start(w_pq[:, P:2 * P], w1[D:2 * D, :]).then_inc(landed2[0], 16)
                sp.dma_start(w1a[:, :], w1[0:D, :]).then_inc(landed2[0], 16)
                sp.dma_start(w2m[:, :], w2).then_inc(landed2[0], 16)
                sp.dma_start(b1_rows[:, :], b1.rearrange("(a n) -> a n", a=1).to_broadcast([P, P])).then_inc(landed3[0], 16)
                with nc.allow_non_contiguous_dma("one value per partition"):
                    for k, vec in enumerate([b2, gamma, beta, res_b] + list(conv_b)):
                        sp.dma_start(cols[:, k:k + 1], vec.rearrange("(n a) -> n a", a=1)).then_inc(landed3[0], 16)
                for k in range(LAYERS):
                    sp.dma_start(w_all[:, k * R * P:(k + 1) * R * P].rearrange("p (r n) -> p r n", n=P),
                                 conv_w[k].rearrange("r d n -> d r n")).then_inc(landed3[0], 16)
                    sp.dma_start(root_all[:, k * P:(k + 1) * P], conv_root[k]).then_inc(landed3[0], 16)
                sp.dma_start(resw_sb[:, :], res_w).then_inc(landed3[0], 16)
                sp.wait_ge(landed3[0], 16 * (6 + 3 * LAYERS))
                sp.wait_ge(scan_done, 1)
                with nc.allow_non_contiguous_dma("rows of 256 bytes"):
                    sp.dma_start(reset_tab.rearrange("(a q) e -> q a e", q=P), reset_bf).then_inc(stored[0], 16)
                sp.wait_ge(stored[0], 16)

            @block.gpsimd
            def _(pool):
                link = linker(pool, gather_go)
                link(pool.memset(ident[:, :], 0.0))
                link(pool.affine_select(out=ident[:, :], in_=ident[:, :], compare_op=ALU.not_equal, fill=1.0,
                                        base=0, pattern=[[-1, P]], channel_multiplier=1))
                link(pool.iota(iota_p[:, :], pattern=[[0, 1]], base=0, channel_multiplier=1,
                               allow_small_or_imprecise_dtypes=True))
                link(pool.iota(iota_row[:, :], pattern=[[1, P]], base=0, channel_multiplier=0,
                               allow_small_or_imprecise_dtypes=True))
                link(pool.iota(wsteps[:, :], pattern=[[WINDOW, MAX_STEPS]], base=WINDOW, channel_multiplier=0,
                               allow_small_or_imprecise_dtypes=True))
                pool.memset(ones_row[:, :], 1.0)
                pool.memset(negbig_row[:, :], -BIG)
                pool.memset(big_mat[:, :], BIG)
                pool.memset(shift[:, :], 0.0)
                pool.memset(cols[:, 4 + LAYERS:5 + LAYERS], 0.0)
                pool.memset(w_all[:, LAYERS * R * P:(LAYERS + 1) * R * P], 0.0)
                pool.memset(root_all[:, LAYERS * P:(LAYERS + 1) * P], 0.0)
                pool.drain().then_inc(idx_ready, 1)

            @block.vector
            def _(dve):
                link = linker(dve, chain)
                dve.memset(dst_i, PAD_DST)
                dve.memset(src_i, 0)
                dve.memset(type_i, 0)
                dve.drain().then_inc(filled, 1)
                dve.wait_ge(landed, 16 * 9)
                dve.wait_ge(idx_ready, 1)
                link(nc.vector.tensor_copy(dst_f[:, :, :], dst_i))
                link(nc.vector.tensor_copy(src_f, src_i))
                link(nc.vector.tensor_copy(type_f, type_i))
                link(nc.vector.tensor_tensor(starts[:, :, 1:P], dst_f[:, :, 1:P], dst_f[:, :, 0:P - 1], ALU.not_equal))
                link(nc.vector.memset(starts[:, :, 0:1], 1.0))
                link(nc.vector.tensor_scalar(reset_bf, starts, -BIG, None, ALU.mult))
                nc.vector.tensor_copy(lasts[:, :, 0:P - 1], starts[:, :, 1:P]).then_inc(scan_done, 1)
                link(nc.vector.memset(lasts[:, :, P - 1:P], 1.0))
                link(nc.vector.tensor_reduce(lo[:, :], dst_f[:, :, :], AX.X, ALU.min))
                link(nc.vector.scalar_tensor_tensor(out=tmp_r, in0=dst_f[:, :, :], scalar=float(N), in1=dst_f[:, :, :],
                                                    op0=ALU.is_lt, op1=ALU.mult))
                link(nc.vector.tensor_reduce(hi, tmp_r, AX.X, ALU.max))
                link(nc.vector.tensor_tensor(hi, hi, lo[:, :], ALU.subtract))
                link(nc.vector.tensor_reduce(pair[:, 0:1], hi, AX.X, ALU.max))
                link(nc.vector.tensor_tensor(tmp_r[:, :, 1:P], dst_f[:, :, 1:P], dst_f[:, :, 0:P - 1], ALU.is_lt))
                link(nc.vector.tensor_reduce(pair[:, 1:2], tmp_r[:, :, 1:P], AX.XY, ALU.max))
                nc.vector.tensor_scalar(iota_split[:, :], iota_p[:, :], 0.0, None, ALU.mult).then_inc(hot_ready, 1)
                dve.wait_ge(z_done, 1)
                link(nc.vector.tensor_reduce(top[0:1, 0, 0:2], banks[0][0:1, 0:2 * P].rearrange("a (k q) -> a k q", q=P),
                                             AX.X, ALU.max))
                link(nc.vector.tensor_scalar(hits[0:1, :], wsteps[:, :], top[0:1, 0, 0:1], None, ALU.is_le))
                link(nc.vector.tensor_reduce(top[0:1, 0, 2:3], hits[0:1, :], AX.X, ALU.add))
                link(nc.vector.tensor_scalar(facts_row[:, 0:1], top[0:1, 0, 2:3], 1.0, None, ALU.add))
                link(nc.vector.tensor_scalar(facts_row[:, 1:2], top[0:1, 0, 1:2], P - 1.0, 1.0, ALU.mult, ALU.add))
                link(nc.vector.tensor_copy(facts_row[:, 2:3], top[0:1, 0, 1:2]))
                link(nc.vector.reciprocal(facts_row[:, 3:4], facts_row[:, 1:2]))
                link(nc.vector.tensor_tensor(top[0:1, 0, 4:5], facts_row[:, 0:1], facts_row[:, 1:2], ALU.mult))
                link(nc.vector.tensor_copy(passes_i[:, 0:1], top[0:1, 0, 4:5]))
                nc.vector.tensor_copy(passes_i[:, 1:2], facts_row[:, 0:1]).then_inc(hot_ready, 1)
                dve.wait_ge(z_done, 2)
                nc.vector.tensor_copy(facts[:, :], banks[0][:, 0:4])
                for k in range(1, WINDOW):
                    link(nc.vector.scalar_tensor_tensor(out=iota_split[:, :], in0=iota_p[:, :], scalar=float(SPLIT * k),
                                                        in1=iota_split[:, :], op0=ALU.is_ge, op1=ALU.add))
                dve.wait_ge(landed2[0], 48)
                nc.vector.tensor_tensor(w_pq[:, 0:P], w1a[:, :], w_pq[:, P:2 * P], ALU.subtract)
                nc.vector.tensor_scalar(w2m[:, :], w2m[:, :], -2.0, None, ALU.mult)
                for n, table in enumerate((src_c, type_c, last_c)):
                    for half in range(2):
                        dve.wait_ge(m_done, 2 * n + half + 1)
                        a, b = half * GROUP * P, min((half + 1) * GROUP * P, COLS)
                        ins = nc.vector.tensor_copy(table[:, a:b], banks[1 + half + 2 * n][:, 0:b - a])
                        if (n, half) == (1, 1):
                            ins.then_inc(hot_ready, 1)
                dve.wait_ge(hot_ready, 3)
                nc.vector.tensor_tensor(type_hot, iota_row[:, None, 0:R].to_broadcast([P, TILES, R]),
                                        type_c[:, 0:TILES, None].to_broadcast([P, TILES, R]), ALU.is_equal)

            @block.tensor
            def _(pe):
                pe.wait_ge(hot_ready, 1)
                for k in range(2):
                    last = nc.tensor.transpose(banks[0][0:1, k * P:(k + 1) * P], pair[:, k:k + 1], ident[:, :])
                last.then_inc(z_done, 1)
                pe.wait_ge(hot_ready, 2)
                nc.tensor.matmul(banks[0][:, 0:4], ones_row[0:1, :], facts_row[:, :], start=True, stop=True).then_inc(z_done, 1)
                for n, table in enumerate((src_f, type_f, lasts)):
                    for a in range(BLOCKS):
                        last = nc.tensor.transpose(banks[1 + 2 * n + a // GROUP][:, (a % GROUP) * P:(a % GROUP + 1) * P],
                                                   table[:, a, :], ident[:, :])
                        if a in (GROUP - 1, BLOCKS - 1):
                            last.then_inc(m_done, 1)
        block_end()

        take = carve()
        rel = take([BLOCKS, P])
        rel_bf = take([BLOCKS, P], BF16)
        rel_c, lastw, inside, work = (take([COLS]) for _ in range(4))
        picks = take([4])

        def window_tables(sweeps=None, by_edge=False):
            def guard(engine):
                return engine.If(sweeps > 1) if sweeps is not None else nullcontext()

            with nc.Block() as block:
                @block.sync
                def _(sp):
                    with guard(sp):
                        sp.wait_ge(scan_done, 1)
                        with nc.allow_non_contiguous_dma("rows of 256 bytes"):
                            sp.dma_start(rel_tab.rearrange("(a q) e -> q a e", q=P), rel_bf).then_inc(stored[0], 16)
                        sp.wait_ge(stored[0], 16)
                        stand(sp)

                @block.vector
                def _(dve):
                    with guard(dve):
                        link = linker(dve, chain)
                        if sweeps is not None:
                            step = 1.0 if by_edge else facts[:, 1:2]
                            link(nc.vector.tensor_scalar(shift[:, 2:3], shift[:, 2:3], step, None, ALU.add))
                            link(nc.vector.tensor_tensor(shift[:, 3:4], shift[:, 2:3], facts[:, 1:2], ALU.is_ge))
                            link(nc.vector.tensor_tensor(shift[:, 1:2], shift[:, 1:2], shift[:, 3:4], ALU.add))
                            link(nc.vector.tensor_tensor(shift[:, 3:4], shift[:, 3:4], facts[:, 1:2], ALU.mult))
                            link(nc.vector.tensor_tensor(shift[:, 2:3], shift[:, 2:3], shift[:, 3:4], ALU.subtract))
                            link(nc.vector.tensor_tensor(shift[:, 3:4], shift[:, 1:2], facts[:, 0:1], ALU.is_lt))
                            link(nc.vector.tensor_tensor(shift[:, 1:2], shift[:, 1:2], shift[:, 3:4], ALU.mult))
                            link(nc.vector.tensor_scalar(shift[:, 0:1], shift[:, 1:2], float(WINDOW), None, ALU.mult))
                        link(nc.vector.tensor_scalar(base_f[:, :], lo[:, :], shift[:, 0:1], None, ALU.add))
                        link(nc.vector.tensor_scalar(base_f[:, :], base_f[:, :], float(N), None, ALU.min))
                        nc.vector.tensor_tensor(rel, dst_f[:, :, :], base_f[:, :, None].to_broadcast([P, BLOCKS, P]),
                                                ALU.subtract).then_inc(hot_ready, 1)
                        dve.wait_ge(hot_ready, 1)
                        nc.vector.tensor_scalar(rel_bf, rel, -1.0, float(WINDOW), ALU.max, ALU.min).then_inc(scan_done, 1)
                        link(nc.vector.tensor_scalar(picks[:, 0:1], facts[:, 2:3], -1.0, 1.0, ALU.mult, ALU.add))
                        link(nc.vector.tensor_tensor(picks[:, 1:2], iota_p[:, :], shift[:, 2:3], ALU.is_equal))
                        link(nc.vector.tensor_tensor(picks[:, 2:3], picks[:, 1:2], facts[:, 2:3], ALU.mult))
                        link(nc.vector.tensor_scalar(lastw, last_c[:, :], picks[:, 0:1], picks[:, 2:3], ALU.mult, ALU.add))
                        dve.wait_ge(m_done, 1)
                        for a in range(0, BLOCKS, GROUP):
                            b = min(a + GROUP, BLOCKS)
                            link(nc.vector.tensor_copy(rel_c[:, a * P:b * P], banks[a // GROUP][:, 0:(b - a) * P]))
                            nc.vector.tensor_copy(base_i[:, a * P:b * P], banks[2 + a // GROUP][0:1, 0:(b - a) * P])
                        link(nc.vector.scalar_tensor_tensor(out=work, in0=rel_c, scalar=1.0, in1=lastw,
                                                            op0=ALU.add, op1=ALU.mult))
                        nc.vector.tensor_scalar(keys[:, :, 0], work, -1.0, None, ALU.add)
                        nc.vector.tensor_copy(keys[:, :, 1], rel_c)
                        link(nc.vector.tensor_scalar(inside, rel_c, 0.0, None, ALU.is_ge))
                        link(nc.vector.scalar_tensor_tensor(out=inside, in0=rel_c, scalar=WINDOW - 1.0, in1=inside,
                                                            op0=ALU.is_le, op1=ALU.mult))
                        link(nc.vector.scalar_tensor_tensor(out=work, in0=type_c[:, :], scalar=float(WINDOW), in1=rel_c,
                                                            op0=ALU.mult, op1=ALU.add))
                        link(nc.vector.scalar_tensor_tensor(out=work, in0=work, scalar=1.0, in1=inside,
                                                            op0=ALU.add, op1=ALU.mult))
                        nc.vector.tensor_scalar(key_rn[:, :], work, -1.0, None, ALU.add)

                @block.tensor
                def _(pe):
                    with guard(pe):
                        pe.wait_ge(hot_ready, 1)
                        for a in range(BLOCKS):
                            nc.tensor.transpose(banks[a // GROUP][:, (a % GROUP) * P:(a % GROUP + 1) * P], rel[:, a, :],
                                                ident[:, :])
                            last = nc.tensor.transpose(banks[2 + a // GROUP][0:1, (a % GROUP) * P:(a % GROUP + 1) * P],
                                                       base_f[:, a:a + 1], ident[:, :])
                        last.then_inc(m_done, 1)
            block_end()

        window_tables()

        take = carve()
        x_ring = take([2, GROUP, P])
        xt = take([2, CHUNK])
        p_f = take([2, GROUP, P])
        p_parts = take([2, GROUP, SPLIT, P], BF16)
        q_rows = take([2, GROUP, P])
        with nc.Block() as block:
            @block.sync
            def _(sp):
                def step(c, k):
                    if active(c, 0, CHUNKS):
                        n = width(c) // P
                        if later(c, 2):
                            sp.wait_ge(turned, c - 1)
                        if isinstance(c, int) and c == CHUNKS - 1:
                            sp.wait_ge(filled, 1)
                            sp.dma_start(x_ring[0:N - c * CHUNK, k, 0, :], x[c * CHUNK:N, :]).then_inc(landed2[k], 16)
                        else:
                            sp.dma_start(x_ring[:, k, :, :],
                                         x[bass.ds(c * CHUNK, CHUNK), :].rearrange("(t p) d -> p t d", p=P)).then_inc(landed2[k], 16)
                    if active(c, 2, CHUNKS):
                        d = c - 2
                        n = width(d) // P
                        sp.wait_ge(m_done, d + 1)
                        sp.dma_start(p_tab[bass.ds(d * (CHUNK * SPLIT), n * P * SPLIT), :].rearrange("(t p c) d -> p t c d", p=P, c=SPLIT),
                                     p_parts[:, k, 0:n, :, :]).then_inc(stored[k], 16)
                        sp.wait_ge(z_copied, d + 1)
                        sp.dma_start(q_tab[bass.ds(d * CHUNK, n * P), :].rearrange("(t p) d -> p t d", p=P),
                                     q_rows[:, k, 0:n, :]).then_inc(stored2[k], 16)
                run_steps(sp, step, CHUNKS, 2, 2)
                for k in range(2):
                    sp.wait_ge(stored[k], 16 * ((CHUNKS + 1 - k) // 2))
                    sp.wait_ge(stored2[k], 16 * ((CHUNKS + 1 - k) // 2))

            @block.tensor
            def _(pe):
                def step(c, k):
                    if active(c, 0, CHUNKS):
                        n = width(c) // P
                        pe.wait_ge(landed2[k], (c // 2 + 1) * 16 if isinstance(c, int) else (c - k) * 8 + 16)
                        if later(c, 2):
                            pe.wait_ge(turned_copied, c - 1)
                        for t in range(n):
                            last = nc.tensor.transpose(banks[k][:, t * P:(t + 1) * P], x_ring[:, k, t, :], ident[:, :])
                        last.then_inc(turned, 1)
                    if active(c, 1, CHUNKS):
                        d, j = c - 1, (k + 1) % 2
                        n = width(d) // P
                        pe.wait_ge(turned_copied, d + 1)
                        if later(d, 2):
                            pe.wait_ge(chain, d * 5 - 9)
                            pe.wait_ge(z_copied, d - 1)
                        for t in range(n):
                            nc.tensor.matmul(banks[2 + j][:, t * P:(t + 1) * P], xt[:, j, t * P:(t + 1) * P],
                                             w_pq[:, 0:P], start=(t == 0), stop=True, skip_group_check=True)
                            last = nc.tensor.matmul(banks[4 + j][:, t * P:(t + 1) * P], xt[:, j, t * P:(t + 1) * P],
                                                    w_pq[:, P:2 * P], start=(t == 0), stop=True, skip_group_check=True)
                        last.then_inc(z_done, 1)
                run_steps(pe, step, CHUNKS, 1, 2)

            @block.scalar
            def _(act):
                def step(c, k):
                    if active(c, 0, CHUNKS):
                        w = width(c)
                        act.wait_ge(turned, c + 1)
                        if later(c, 2):
                            act.wait_ge(z_done, c - 1)
                        nc.scalar.copy(xt[:, k, 0:w], banks[k][:, 0:w]).then_inc(turned_copied, 1)
                    if active(c, 1, CHUNKS):
                        d, j = c - 1, (k + 1) % 2
                        n = width(d) // P
                        act.wait_ge(z_done, d + 1)
                        if later(d, 2):
                            act.wait_ge(stored2[j], (d // 2) * 16 if isinstance(d, int) else (d - j) * 8)
                        nc.scalar.copy(q_rows[:, j, 0:n, :], banks[4 + j][:, 0:n * P].rearrange("p (t d) -> p t d", d=P)).then_inc(z_copied, 1)
                run_steps(act, step, CHUNKS, 1, 2)

            @block.gpsimd
            def _(pool):
                pool.wait_ge(turned, CHUNKS - 2)
                pool.memset(x_ring[:, (CHUNKS - 1) % 2, 0, :], 0.0).then_inc(filled, 1)

            @block.vector
            def _(dve):
                dve.memset(acc[:, :], -BIG)
                dve.memset(cnt[:, :], 0.0)

                def step(c, k):
                    n = width(c) // P
                    left, parts = p_f[:, k, 0:n, :], p_parts[:, k, 0:n, :, :]
                    dve.wait_ge(z_done, c + 1)
                    if later(c, 2):
                        dve.wait_ge(stored[k], (c // 2) * 16 if isinstance(c, int) else (c - k) * 8)
                    link_at = c * 5
                    nc.vector.tensor_tensor(left, banks[2 + k][:, 0:n * P].rearrange("p (t d) -> p t d", d=P),
                                            b1_rows[:, None, :].to_broadcast([P, n, P]), ALU.add).then_inc(chain, 1)
                    dve.wait_ge(chain, link_at + 1)
                    nc.vector.tensor_copy(parts[:, :, 0, :], left).then_inc(chain, 1)
                    dve.wait_ge(chain, link_at + 2)
                    nc.vector.tensor_tensor(left, left, parts[:, :, 0, :], ALU.subtract).then_inc(chain, 1)
                    dve.wait_ge(chain, link_at + 3)
                    nc.vector.tensor_copy(parts[:, :, 1, :], left).then_inc(chain, 1)
                    dve.wait_ge(chain, link_at + 4)
                    nc.vector.tensor_tensor(left, left, parts[:, :, 1, :], ALU.subtract).then_inc(chain, 1)
                    dve.wait_ge(chain, link_at + 5)
                    nc.vector.tensor_copy(parts[:, :, 2, :], left).then_inc(m_done, 1)
                run_steps(dve, step, CHUNKS, 0, 2)
        block_end()

        take = carve()
        rel_ring = take([SLOTS, GROUP * P], BF16, WINDOW * SPLIT)
        reset_ring = take([SLOTS, GROUP * P], BF16)
        p_ring = take([SLOTS * GROUP, P], BF16, WINDOW * SPLIT)
        hot = take([2, GROUP * P], BF16, WINDOW * SPLIT)
        zc = take([2, GROUP * P])
        er = take([2, GROUP * P])
        g_t = take([2, GROUP * P])
        scanned = take([2, GROUP * P])
        scanned_t = take([2, GROUP, P])
        select = take([2, GROUP, 2, WINDOW])
        rel_flat = rel_tab.rearrange("t e -> (t e)")
        reset_flat = reset_tab.rearrange("t e -> (t e)")

        def gather_rows(pool, table, reader_done):
            def body(i):
                for g in range(SLOTS):
                    pool.wait_ge(idx_ready, i * SLOTS + g + 1)
                    if not isinstance(i, int):
                        pool.wait_ge(reader_done, (i - 1) * SLOTS + g + 1)
                    stand(pool)
                    for t in range(g * GROUP, (g + 1) * GROUP):
                        pool.indirect_dma_start(rows[:, t, :], None, table,
                                                bass.IndirectOffsetOnAxis(ap=idx_stage[:, t:t + 1], axis=0)
                                                ).then_inc(row_landed[t], 16)
            body(0)
            with pool.Fori(1, GROUPS // SLOTS) as i:
                body(i)

        def stage_indices(act, s, k):
            stand(act)
            nc.scalar.copy(idx_stage[:, k * GROUP:(k + 1) * GROUP],
                           src_c[:, bass.ds(s * GROUP, GROUP)]).then_inc(idx_ready, 1)

        def rows_here(pe, s, k, t):
            pe.wait_ge(row_landed[k * GROUP + t], (s // SLOTS + 1) * 16 if isinstance(s, int) else (s - k) * 4 + 16)

        def tile_bases(engine, s):
            _, values = nc.values_load_multi_w_load_instructions(
                base_i[0:1, bass.ds(s * GROUP, GROUP)], engines=[engine], min_val=0, max_val=N,
                skip_runtime_bounds_check_because="the tables hold no base above N")
            return values

        def edge_sweep():
            with nc.Block() as block:
                @block.gpsimd
                def _(pool):
                    gather_rows(pool, q_tab, z_done)

                @block.sync
                def _(sp):
                    def step(s, k):
                        if later(s, SLOTS):
                            sp.wait_ge(scan_done, s - SLOTS + 1)
                        sp.dma_start(rel_ring[:, k, :], rel_flat[None, bass.ds(s * (GROUP * P), GROUP * P)]
                                     .to_broadcast([WINDOW * SPLIT, GROUP * P])).then_inc(side_landed[k], 16)
                        sp.dma_start(reset_ring[:, k, :], reset_flat[None, bass.ds(s * (GROUP * P), GROUP * P)]
                                     .to_broadcast([P, GROUP * P])).then_inc(side_landed[k], 16)
                        for t, b in enumerate(tile_bases(SP, s)):
                            sp.dma_start(p_ring[:, k * GROUP + t, :], p_tab[bass.ds(b * SPLIT, WINDOW * SPLIT), :]
                                         ).then_inc(side_landed[k], 16)
                    run_steps(sp, step, GROUPS, 0, SLOTS)

                def side_here(engine, s, k):
                    engine.wait_ge(side_landed[k], (s // SLOTS + 1) * SIDE if isinstance(s, int) else (s - k) * (SIDE // SLOTS) + SIDE)

                @block.tensor
                def _(pe):
                    def step(s, k):
                        b = k % 2
                        if active(s, 0, GROUPS):
                            side_here(pe, s, k)
                            pe.wait_ge(hot_ready, s + 1)
                            if later(s, 2):
                                pe.wait_ge(g_ready, s - 1)
                            for t in range(GROUP):
                                rows_here(pe, s, k, t)
                                nc.tensor.matmul(banks[b][:, t * P:(t + 1) * P], rows[:, k * GROUP + t, :], ident[:, :],
                                                 start=(t == 0), stop=False, skip_group_check=True)
                                last = nc.tensor.matmul(banks[b][:, t * P:(t + 1) * P], p_ring[:, k * GROUP + t, :],
                                                        hot[:, b, t * P:(t + 1) * P], start=False, stop=True,
                                                        skip_group_check=True)
                            last.then_inc(z_done, 1)
                        if active(s, 2, GROUPS):
                            pe.wait_ge(g_ready, s - 1)
                            if later(s, 4):
                                pe.wait_ge(scan_done, s - 3)
                            nc.tensor.matmul(banks[2 + b][:, :], w2m[:, :], g_t[:, b, :], start=True, stop=True).then_inc(m_done, 1)
                        if active(s, 4, GROUPS):
                            pe.wait_ge(scan_done, s - 3)
                            if later(s, 6):
                                pe.wait_ge(turned_copied, s - 5)
                            for t in range(GROUP):
                                last = nc.tensor.transpose(banks[4 + b][:, t * P:(t + 1) * P],
                                                           scanned[:, b, t * P:(t + 1) * P], ident[:, :])
                            last.then_inc(turned, 1)
                        if active(s, 5, GROUPS):
                            c = (b + 1) % 2
                            pe.wait_ge(select_ready, s - 4)
                            pe.wait_ge(turned_copied, s - 4)
                            if later(s, 7):
                                pe.wait_ge(merged, (s - 6) * (2 * GROUP))
                            best = banks[6 + c][:, 0:GROUP * WINDOW]
                            nc.tensor.matmul(best.rearrange("p (t n) -> p t n", n=WINDOW), big_mat[:, :], select[:, c, :, 0, :], start=True, stop=False,
                                             skip_group_check=True)
                            nc.tensor.matmul(best, negbig_row[:, :], ones_row[0:1, 0:GROUP * WINDOW], start=False,
                                             stop=False, skip_group_check=True)
                            for t in range(GROUP):
                                nc.tensor.matmul(best[:, t * WINDOW:(t + 1) * WINDOW], scanned_t[:, c, t, :],
                                                 select[:, c, t, 0, :], start=False, stop=True, skip_group_check=True)
                                last = nc.tensor.matmul(
                                    banks[6 + c][0:R, (GROUP + t) * WINDOW:(GROUP + t + 1) * WINDOW],
                                    type_now[:, c, t, :], select[:, c, t, 1, :], start=False, stop=True,
                                    skip_group_check=True)
                            last.then_inc(window_done, 1)
                    run_steps(pe, step, GROUPS, 5, SLOTS)

                @block.scalar
                def _(act):
                    nc.scalar.preload_act_table_set("natural_log_exp_and_others")
                    for k in range(SLOTS):
                        stage_indices(act, k, k)

                    def step(s, k):
                        if active(s, 1, GROUPS):
                            b = (k + 1) % 2
                            act.wait_ge(clamp_ready, s)
                            if later(s, 3):
                                act.wait_ge(g_ready, s - 2)
                            now = er[:, b, :]
                            done = (s - 1) * 3
                            nc.scalar.activation(now, zc[:, b, :], ACT.Exp).then_inc(act_chain, 1)
                            act.wait_ge(act_chain, done + 1)
                            nc.scalar.activation(now, now, ACT.Square, bias=1.0).then_inc(act_chain, 1)
                            act.wait_ge(act_chain, done + 2)
                            nc.scalar.activation(now, now, ACT.Ln, bias=1.0).then_inc(act_chain, 1)
                            act.wait_ge(act_chain, done + 3)
                            nc.scalar.activation(now, now, ACT.Exp, scale=-1.0).then_inc(recip_ready, 1)
                            act.wait_ge(z_done, s)
                            stage_indices(act, s + (SLOTS - 1), (k + SLOTS - 1) % SLOTS)
                        if active(s, 4, GROUPS):
                            b = k % 2
                            act.wait_ge(turned, s - 3)
                            if later(s, 6):
                                act.wait_ge(window_done, s - 5)
                            nc.scalar.copy(scanned_t[:, b, :, :], banks[4 + b][:, :].rearrange("p (t d) -> p t d", d=P)
                                           ).then_inc(turned_copied, 1)
                    run_steps(act, step, GROUPS, 4, SLOTS)

                @block.vector
                def _(dve):
                    def step(s, k):
                        b, c = k % 2, (k + 1) % 2
                        if active(s, 0, GROUPS):
                            side_here(dve, s, k)
                            if later(s, 2):
                                dve.wait_ge(z_done, s - 1)
                            nc.vector.tensor_scalar(hot[:, b, :], rel_ring[:, k, :], iota_split[0:WINDOW * SPLIT, :], None,
                                                    ALU.is_equal).then_inc(hot_ready, 1)
                        if active(s, 3, GROUPS):
                            dve.wait_ge(m_done, s - 2)
                            if later(s, 5):
                                dve.wait_ge(turned, s - 4)
                            nc.vector.tensor_tensor_scan(scanned[:, c, :], reset_ring[:, (k + 1) % SLOTS, :], banks[2 + c][:, :],
                                                         0.0, ALU.add, ALU.max).then_inc(scan_done, 1)
                        if active(s, 1, GROUPS):
                            dve.wait_ge(z_done, s)
                            if later(s, 3):
                                dve.wait_ge(recip_ready, s - 2)
                            nc.vector.tensor_scalar(zc[:, c, :], banks[c][:, :], EXP_LIMIT, None, ALU.min).then_inc(clamp_ready, 1)
                        if active(s, 2, GROUPS):
                            dve.wait_ge(recip_ready, s - 1)
                            if later(s, 4):
                                dve.wait_ge(m_done, s - 3)
                            nc.vector.scalar_tensor_tensor(out=g_t[:, b, :], in0=er[:, b, :], scalar=-0.5, in1=banks[b][:, :],
                                                           op0=ALU.add, op1=ALU.mult).then_inc(g_ready, 1)
                        if active(s, 4, GROUPS):
                            if later(s, 6):
                                dve.wait_ge(window_done, s - 5)
                            first = (s - 4) * GROUP
                            nc.vector.tensor_copy(type_now[:, b, :, :], type_hot[:, bass.ds(first, GROUP), :])
                            nc.vector.tensor_tensor(
                                select[:, b, :, :, :],
                                iota_row[:, None, None, 0:WINDOW].to_broadcast([P, GROUP, 2, WINDOW]),
                                keys[:, bass.ds(first, GROUP), :, None].to_broadcast([P, GROUP, 2, WINDOW]),
                                ALU.is_equal).then_inc(select_ready, 1)
                        if active(s, 6, GROUPS):
                            dve.wait_ge(window_done, s - 5)
                            at = (s - 6) * (2 * GROUP)
                            for t, w in enumerate(tile_bases(DVE, s - 6)):
                                if later(s, 7) or t:
                                    dve.wait_ge(merged, at + 2 * t)
                                nc.vector.tensor_tensor(acc[:, bass.ds(w, WINDOW)], acc[:, bass.ds(w, WINDOW)],
                                                        banks[6 + b][:, t * WINDOW:(t + 1) * WINDOW], ALU.max).then_inc(merged, 1)
                                nc.vector.tensor_tensor(cnt[:, bass.ds(w, WINDOW)], cnt[:, bass.ds(w, WINDOW)],
                                                        banks[6 + b][0:R, (GROUP + t) * WINDOW:(GROUP + t + 1) * WINDOW],
                                                        ALU.add).then_inc(merged, 1)
                    run_steps(dve, step, GROUPS, 6, SLOTS)
            block_end()

        type_now = take([2, GROUP, R])
        sweeps = nc.values_load(passes_i[0:1, 0:1], min_val=1, max_val=P * (MAX_STEPS + 1),
                                skip_runtime_bounds_check_because="the kernel works it out from spans of at most N")
        with nc.Fori(0, sweeps):
            edge_sweep()
            window_tables(sweeps, True)

        take = carve()
        nodes_ok = take([STAT])
        stats = take([N // STAT, 6])
        mv = take([8])
        factor = take([NP // P, R])
        factor_parts = take([NP // P, SPLIT, R], BF16)
        with nc.Block() as block:
            @block.sync
            def _(sp):
                sp.wait_ge(spread_ready, 1)
                with nc.allow_non_contiguous_dma("rows of 48 bytes"):
                    sp.dma_start(fac_tab.rearrange("(t p) m -> p t m", p=P),
                                 factor_parts.rearrange("p t c r -> p t (c r)")).then_inc(stored[0], 16)
                sp.wait_ge(stored[0], 16)

            @block.tensor
            def _(pe):
                for t in range(NP // P):
                    last = nc.tensor.transpose(banks[0][:, t * R:(t + 1) * R], cnt[:, t * P:(t + 1) * P], ident[0:R, 0:R])
                last.then_inc(turned, 1)

            @block.vector
            def _(dve):
                link = linker(dve, chain)
                dve.wait_ge(turned, 1)
                link(nc.vector.tensor_scalar(factor, banks[0][:, 0:NP // P * R].rearrange("p (t r) -> p t r", r=R),
                                             facts[:, 3:4], 1.0, ALU.mult, ALU.max))
                link(nc.vector.reciprocal(factor, factor))
                link(nc.vector.tensor_copy(factor_parts[:, :, 0, :], factor))
                link(nc.vector.tensor_tensor(factor, factor, factor_parts[:, :, 0, :], ALU.subtract))
                link(nc.vector.tensor_copy(factor_parts[:, :, 1, :], factor))
                link(nc.vector.tensor_tensor(factor, factor, factor_parts[:, :, 1, :], ALU.subtract))
                nc.vector.tensor_copy(factor_parts[:, :, 2, :], factor).then_inc(spread_ready, 1)
                nc.vector.memset(acc[:, N:NP], 0.0)

                def part(s, k):
                    here = acc[:, bass.ds(s * STAT, STAT)]
                    at = 2 * s
                    if later(s, 1):
                        dve.wait_ge(scaled, at + s)
                    nc.vector.tensor_scalar(nodes_ok, here, -BIG / 2, None, ALU.is_gt).then_inc(scaled, 1)
                    dve.wait_ge(scaled, at + s + 1)
                    nc.vector.scalar_tensor_tensor(out=here, in0=here, scalar=cols[:, 0:1], in1=nodes_ok, op0=ALU.add,
                                                   op1=ALU.mult).then_inc(scaled, 1)
                    dve.wait_ge(scaled, at + s + 2)
                    nc.vector.bn_stats(stats[:, bass.ds(s, 1), :], here).then_inc(scaled, 1)
                part(0, 0)
                with dve.Fori(1, N // STAT) as i:
                    part(i, 0)
                dve.wait_ge(scaled, 3 * (N // STAT))
                link(nc.vector.bn_aggr(mv[:, 0:2], stats))
                nc.vector.tensor_scalar(mv[:, 2:3], mv[:, 1:2], EPS, None, ALU.add).then_inc(hot_ready, 1)
                dve.wait_ge(z_copied, 1)
                link(nc.vector.reciprocal(mv[:, 4:5], mv[:, 3:4]))
                link(nc.vector.tensor_tensor(norm[:, 0:1], mv[:, 4:5], cols[:, 1:2], ALU.mult))
                link(nc.vector.tensor_tensor(mv[:, 5:6], mv[:, 0:1], norm[:, 0:1], ALU.mult))
                nc.vector.tensor_tensor(norm[:, 1:2], cols[:, 2:3], mv[:, 5:6], ALU.subtract)

            @block.scalar
            def _(act):
                act.wait_ge(hot_ready, 1)
                nc.scalar.activation(mv[:, 3:4], mv[:, 2:3], ACT.Sqrt).then_inc(z_copied, 1)
                link = linker(act, act_chain)
                link(nc.scalar.copy(w_cur[:, :], w_all[:, 0:R * P]))
                link(nc.scalar.copy(b_cur[:, :], cols[:, 4:5]))
        block_end()

        take = carve()
        y_t = take([2, CHUNK])
        x_rows = take([2, GROUP, P])
        v_rows = take([2, GROUP, P])
        x1_rows = take([2, GROUP, P])
        x1_t = take([2, CHUNK])
        ln_stats = take([2, GROUP, 6])
        ln_mv = take([2, GROUP, 2])
        ln_sd = take([2, GROUP])
        y_rows = take([2, GROUP, P])

        def ln_stats_of(dve, k, n, at):
            for t in range(n):
                last = nc.vector.bn_stats(ln_stats[:, k, t, :], v_rows[:, k, t, :])
            last.then_inc(chain, 1)
            dve.wait_ge(chain, at + 1)
            stand(dve)
            for t in range(n):
                last = nc.vector.bn_aggr(ln_mv[:, k, t, :], ln_stats[:, k, t, :])
            last.then_inc(chain, 1)
            dve.wait_ge(chain, at + 2)
            nc.vector.tensor_scalar(ln_sd[:, k, 0:n], ln_mv[:, k, 0:n, 1], EPS, None, ALU.add).then_inc(hot_ready, 1)

        def ln_apply(dve, k, n, at):
            nc.vector.reciprocal(ln_sd[:, k, 0:n], ln_sd[:, k, 0:n]).then_inc(chain, 1)
            dve.wait_ge(chain, at)
            for t in range(n):
                last = nc.vector.tensor_scalar(x1_rows[:, k, t, :], v_rows[:, k, t, :], ln_mv[:, k, t, 0:1],
                                               ln_sd[:, k, t:t + 1], ALU.subtract, ALU.mult)
            last.then_inc(scaled, 1)

        def ln_root(act, k, n):
            nc.scalar.activation(ln_sd[:, k, 0:n], ln_sd[:, k, 0:n], ACT.Sqrt).then_inc(recip_ready, 1)

        def half16(c, k):
            return (c // 2) * 16 if isinstance(c, int) else (c - k) * 8

        with nc.Block() as block:
            @block.sync
            def _(sp):
                def step(c, k):
                    if active(c, 0, CHUNKS):
                        if later(c, 2):
                            sp.wait_ge(filled, c - 1)
                        if isinstance(c, int) and c == CHUNKS - 1:
                            sp.wait_ge(spread_ready, 1)
                            sp.dma_start(x_rows[0:N - c * CHUNK, k, 0, :], x[c * CHUNK:N, :]).then_inc(landed2[k], 16)
                        else:
                            sp.dma_start(x_rows[:, k, :, :],
                                         x[bass.ds(c * CHUNK, CHUNK), :].rearrange("(t p) d -> p t d", p=P)).then_inc(landed2[k], 16)
                    if active(c, 2, CHUNKS):
                        d = c - 2
                        n = width(d) // P
                        sp.wait_ge(scaled, d + 1)
                        for table, done in ((h_tab, stored), (x1_tab, stored2)):
                            sp.dma_start(table[bass.ds(d * CHUNK, n * P), :].rearrange("(t p) d -> p t d", p=P),
                                         x1_rows[:, k, 0:n, :]).then_inc(done[k], 16)
                run_steps(sp, step, CHUNKS, 2, 2)
                for k in range(2):
                    sp.wait_ge(stored[k], 16 * ((CHUNKS + 1 - k) // 2))
                    sp.wait_ge(stored2[k], 16 * ((CHUNKS + 1 - k) // 2))

            @block.scalar
            def _(act):
                def step(c, k):
                    if active(c, 0, CHUNKS):
                        w = width(c)
                        if later(c, 2):
                            act.wait_ge(turned, c - 1)
                        nc.scalar.activation(y_t[:, k, 0:w], acc[:, bass.ds(c * CHUNK, w)], ACT.Identity,
                                             bias=norm[:, 1:2], scale=norm[:, 0:1]).then_inc(clamp_ready, 1)
                        act.wait_ge(hot_ready, c + 1)
                        ln_root(act, k, w // P)
                    if active(c, 1, CHUNKS):
                        d, j = c - 1, (k + 1) % 2
                        w = width(d)
                        act.wait_ge(m_done, d + 1)
                        if later(d, 2):
                            act.wait_ge(window_done, d - 1)
                        nc.scalar.copy(x1_t[:, j, 0:w], banks[2 + j][:, 0:w]).then_inc(turned_copied, 1)
                        act.wait_ge(window_done, d + 1)
                        stand(act)
                        nc.scalar.copy(acc[:, bass.ds(d * CHUNK, w)], banks[4 + j][:, 0:w]).then_inc(z_copied, 1)
                        nc.scalar.activation(res_buf[:, bass.ds(d * CHUNK, w)], banks[6 + j][:, 0:w], ACT.Identity,
                                             bias=cols[:, 3:4]).then_inc(z_copied, 1)
                run_steps(act, step, CHUNKS, 1, 2)

            @block.tensor
            def _(pe):
                def step(c, k):
                    if active(c, 0, CHUNKS):
                        n = width(c) // P
                        pe.wait_ge(clamp_ready, c + 1)
                        if later(c, 2):
                            pe.wait_ge(filled, c - 1)
                        for t in range(n):
                            last = nc.tensor.transpose(banks[k][:, t * P:(t + 1) * P], y_t[:, k, t * P:(t + 1) * P], ident[:, :])
                        last.then_inc(turned, 1)
                    if active(c, 1, CHUNKS):
                        d, j = c - 1, (k + 1) % 2
                        w = width(d)
                        pe.wait_ge(scaled, d + 1)
                        if later(d, 2):
                            pe.wait_ge(turned_copied, d - 1)
                        for t in range(w // P):
                            last = nc.tensor.transpose(banks[2 + j][:, t * P:(t + 1) * P], x1_rows[:, j, t, :], ident[:, :])
                        last.then_inc(m_done, 1)
                        pe.wait_ge(turned_copied, d + 1)
                        if later(d, 2):
                            pe.wait_ge(z_copied, 2 * d - 2)
                        nc.tensor.matmul(banks[4 + j][:, 0:w], root_all[:, 0:P], x1_t[:, j, 0:w], start=True, stop=True)
                        nc.tensor.matmul(banks[6 + j][:, 0:w], resw_sb[:, :], x1_t[:, j, 0:w], start=True, stop=True
                                         ).then_inc(window_done, 1)
                run_steps(pe, step, CHUNKS, 1, 2)

            @block.vector
            def _(dve):
                def step(c, k):
                    n = width(c) // P
                    dve.wait_ge(turned, c + 1)
                    dve.wait_ge(landed2[k], half16(c, k) + 16)
                    if later(c, 2):
                        dve.wait_ge(scaled, c - 1)
                    nc.vector.tensor_tensor(v_rows[:, k, 0:n, :], banks[k][:, 0:n * P].rearrange("p (t d) -> p t d", d=P),
                                            x_rows[:, k, 0:n, :], ALU.add).then_inc(filled, 1)
                    dve.wait_ge(filled, c + 1)
                    ln_stats_of(dve, k, n, c * 3)
                    dve.wait_ge(recip_ready, c + 1)
                    if later(c, 2):
                        dve.wait_ge(stored[k], half16(c, k))
                        dve.wait_ge(stored2[k], half16(c, k))
                        dve.wait_ge(m_done, c - 1)
                    ln_apply(dve, k, n, c * 3 + 3)
                run_steps(dve, step, CHUNKS, 0, 2)

            @block.gpsimd
            def _(pool):
                pool.wait_ge(filled, CHUNKS - 2)
                pool.memset(x_rows[:, (CHUNKS - 1) % 2, 0, :], 0.0).then_inc(spread_ready, 1)
        block_end()

        take = carve()
        rel_ring16 = take([SLOTS, GROUP * P], BF16, WINDOW)
        fac_ring = take([SLOTS * GROUP, SPLIT * R], BF16, WINDOW)
        hot16 = take([2, GROUP * P], BF16, WINDOW)
        type_sel = take([2, GROUP, 1, R])
        fac_sel = take([2, GROUP, SPLIT * R])
        edge_fac = take([2, GROUP])
        onehot = take([2, GROUP, P])
        z_sb = take([2, 2 * GROUP, R, WINDOW])
        CONV_SIDE = 16 * (1 + GROUP)

        def conv_sweep():
            with nc.Block() as block:
                @block.gpsimd
                def _(pool):
                    gather_rows(pool, h_tab, z_done)

                @block.sync
                def _(sp):
                    def step(s, k):
                        if later(s, SLOTS):
                            sp.wait_ge(m_done, s - SLOTS + 1)
                        sp.dma_start(rel_ring16[:, k, :], rel_flat[None, bass.ds(s * (GROUP * P), GROUP * P)]
                                     .to_broadcast([WINDOW, GROUP * P])).then_inc(side_landed[k], 16)
                        for t, b in enumerate(tile_bases(SP, s)):
                            sp.dma_start(fac_ring[:, k * GROUP + t, :], fac_tab[bass.ds(b, WINDOW), :]
                                         ).then_inc(side_landed[k], 16)
                    run_steps(sp, step, GROUPS, 0, SLOTS)

                def side_here(engine, s, k):
                    engine.wait_ge(side_landed[k], (s // SLOTS + 1) * CONV_SIDE if isinstance(s, int)
                                   else (s - k) * (CONV_SIDE // SLOTS) + CONV_SIDE)

                @block.tensor
                def _(pe):
                    def step(s, k):
                        b = k % 2
                        if active(s, 0, GROUPS):
                            side_here(pe, s, k)
                            pe.wait_ge(hot_ready, s + 1)
                            if later(s, 2):
                                pe.wait_ge(scaled, s - 1)
                            for t in range(GROUP):
                                last = nc.tensor.matmul(banks[6 + b][:, t * SPLIT * R:(t + 1) * SPLIT * R],
                                                        hot16[:, b, t * P:(t + 1) * P], fac_ring[:, k * GROUP + t, :],
                                                        start=(t == 0), stop=True, skip_group_check=True)
                            last.then_inc(m_done, 1)
                        if active(s, 2, GROUPS):
                            j = s - 2
                            pe.wait_ge(select_ready, j + 1)
                            if later(j, 2):
                                pe.wait_ge(z_copied, j - 1)
                            for t in range(GROUP):
                                rows_here(pe, j, (k + 2) % SLOTS, t)
                                last = nc.tensor.matmul(banks[b][:, t * P:(t + 1) * P], rows[:, (k + 2) % SLOTS * GROUP + t, :],
                                                        onehot[:, b, t, :], start=(t == 0), stop=True, skip_group_check=True)
                            last.then_inc(z_done, 1)
                        if k % 2 and active(s, 4, GROUPS):
                            j, q = s - 4, k // 2
                            pe.wait_ge(z_copied, j + 1)
                            if later(j, 4):
                                pe.wait_ge(merged, (j - 3) * GROUP)
                            for r in range(R):
                                last = nc.tensor.matmul(banks[4 + q][:, 0:2 * GROUP * WINDOW].rearrange("p (t n) -> p t n", n=WINDOW),
                                                        w_cur[:, r * P:(r + 1) * P],
                                                        z_sb[:, q, :, r, :], start=(r == 0), stop=(r == R - 1))
                            last.then_inc(window_done, 2)
                    run_steps(pe, step, GROUPS, 4, SLOTS)

                @block.scalar
                def _(act):
                    for k in range(SLOTS):
                        stage_indices(act, k, k)

                    def step(s, k):
                        if active(s, 3, GROUPS):
                            j, q, half = s - 3, ((k + 1) % SLOTS) // 2, (k + 1) % 2
                            act.wait_ge(z_done, j + 1)
                            if later(j, 4):
                                act.wait_ge(window_done, j - 3 if half else j - 2)
                            nc.scalar.copy(z_sb[:, q, half * GROUP:(half + 1) * GROUP, :, :],
                                           banks[(k + 1) % 2][:, :].rearrange("p (t r n) -> p t r n", r=R, n=WINDOW)
                                           ).then_inc(z_copied, 1)
                            stage_indices(act, j + SLOTS, (k + 1) % SLOTS)
                    run_steps(act, step, GROUPS, 3, SLOTS)

                @block.vector
                def _(dve):
                    def step(s, k):
                        b, c = k % 2, (k + 1) % 2
                        if active(s, 0, GROUPS):
                            side_here(dve, s, k)
                            if later(s, 2):
                                dve.wait_ge(m_done, s - 1)
                            nc.vector.tensor_scalar(hot16[:, b, :], rel_ring16[:, k, :], iota_p[0:WINDOW, :], None,
                                                    ALU.is_equal).then_inc(hot_ready, 1)
                        if active(s, 6, GROUPS):
                            j, q = s - 6, 1 - k // 2
                            dve.wait_ge(window_done, j + 2 if k % 2 == 0 else j + 1)
                            for t, w in enumerate(tile_bases(DVE, j)):
                                if later(j, 1) or t:
                                    dve.wait_ge(merged, j * GROUP + t)
                                col = (b * GROUP + t) * WINDOW
                                nc.vector.tensor_tensor(acc[:, bass.ds(w, WINDOW)], acc[:, bass.ds(w, WINDOW)],
                                                        banks[4 + q][:, col:col + WINDOW], ALU.add).then_inc(merged, 1)
                        if active(s, 1, GROUPS):
                            j = s - 1
                            if later(j, 2):
                                dve.wait_ge(z_done, j - 1)
                            nc.vector.tensor_tensor(type_sel[:, c, :, 0, :], iota_row[:, None, 0:R].to_broadcast([P, GROUP, R]),
                                                    type_c[:, bass.ds(j * GROUP, GROUP), None].to_broadcast([P, GROUP, R]),
                                                    ALU.is_equal).then_inc(chain, 1)
                            dve.wait_ge(chain, j * 2 + 1)
                            dve.wait_ge(m_done, j + 1)
                            nc.vector.tensor_tensor(fac_sel[:, c, :, :].rearrange("p t (c r) -> p t c r", r=R),
                                                    banks[6 + c][:, 0:GROUP * SPLIT * R].rearrange("p (t c r) -> p t c r", c=SPLIT, r=R),
                                                    type_sel[:, c, :, :, :].to_broadcast([P, GROUP, SPLIT, R]),
                                                    ALU.mult).then_inc(scaled, 1)
                            dve.wait_ge(scaled, j + 1)
                            nc.vector.tensor_reduce(edge_fac[:, c, :], fac_sel[:, c, :, :], AX.X, ALU.add).then_inc(chain, 1)
                            dve.wait_ge(chain, j * 2 + 2)
                            for t in range(GROUP):
                                last = nc.vector.tensor_scalar(onehot[:, c, t, :], iota_row[:, :],
                                                               key_rn[:, bass.ds(j * GROUP + t, 1)], edge_fac[:, c, t:t + 1],
                                                               ALU.is_equal, ALU.mult)
                            last.then_inc(select_ready, 1)
                    run_steps(dve, step, GROUPS, 6, SLOTS)
            block_end()

        take = carve()
        relu_t = take([2, CHUNK])
        h_t = take([2, CHUNK])
        h_rows = take([2, GROUP, P])

        def node_update(layer):
            with nc.Block() as block:
                @block.scalar
                def _(act):
                    nc.scalar.copy(root_cur[:, :], root_all[:, bass.ds((layer + 1) * P, P)]).then_inc(act_chain, 1)

                    def step(c, k):
                        if active(c, 0, CHUNKS):
                            w = width(c)
                            if later(c, 2):
                                act.wait_ge(g_ready, c - 1)
                            nc.scalar.activation(relu_t[:, k, 0:w], acc[:, bass.ds(c * CHUNK, w)], ACT.Relu,
                                                 bias=b_cur[:, :]).then_inc(clamp_ready, 1)
                        if active(c, 1, CHUNKS):
                            d, j = c - 1, (k + 1) % 2
                            w = width(d)
                            act.wait_ge(z_done, d + 1)
                            act.wait_ge(clamp_ready, d + 1)
                            stand(act)
                            nc.scalar.copy(acc[:, bass.ds(d * CHUNK, w)], banks[2 + j][:, 0:w]).then_inc(z_copied, 1)
                    run_steps(act, step, CHUNKS, 1, 2)
                    act.wait_ge(clamp_ready, CHUNKS)
                    nc.scalar.copy(w_cur[:, :], w_all[:, bass.ds((layer + 1) * (R * P), R * P)])
                    nc.scalar.copy(b_cur[:, :], cols[:, bass.ds(layer + 5, 1)])

                @block.vector
                def _(dve):
                    def step(c, k):
                        if active(c, 0, CHUNKS):
                            w = width(c)
                            dve.wait_ge(clamp_ready, c + 1)
                            if later(c, 2):
                                dve.wait_ge(z_done, c - 1)
                            nc.vector.tensor_tensor(h_t[:, k, 0:w], relu_t[:, k, 0:w], res_buf[:, bass.ds(c * CHUNK, w)],
                                                    ALU.add).then_inc(g_ready, 1)
                        if active(c, 1, CHUNKS):
                            d, j = c - 1, (k + 1) % 2
                            n = width(d) // P
                            dve.wait_ge(turned, d + 1)
                            if later(d, 2):
                                dve.wait_ge(stored[j], half16(d, j))
                            nc.vector.tensor_copy(h_rows[:, j, 0:n, :], banks[j][:, 0:n * P].rearrange("p (t d) -> p t d", d=P)
                                                  ).then_inc(turned_copied, 1)
                    run_steps(dve, step, CHUNKS, 1, 2)

                @block.tensor
                def _(pe):
                    pe.wait_ge(act_chain, 1)

                    def step(c, k):
                        w = width(c)
                        pe.wait_ge(g_ready, c + 1)
                        if later(c, 2):
                            pe.wait_ge(turned_copied, c - 1)
                        for t in range(w // P):
                            last = nc.tensor.transpose(banks[k][:, t * P:(t + 1) * P], h_t[:, k, t * P:(t + 1) * P], ident[:, :])
                        last.then_inc(turned, 1)
                        if later(c, 2):
                            pe.wait_ge(z_copied, c - 1)
                        nc.tensor.matmul(banks[2 + k][:, 0:w], root_cur[:, :], h_t[:, k, 0:w], start=True, stop=True
                                         ).then_inc(z_done, 1)
                    run_steps(pe, step, CHUNKS, 0, 2)

                @block.sync
                def _(sp):
                    def step(c, k):
                        n = width(c) // P
                        sp.wait_ge(turned_copied, c + 1)
                        sp.dma_start(h_tab[bass.ds(c * CHUNK, n * P), :].rearrange("(t p) d -> p t d", p=P),
                                     h_rows[:, k, 0:n, :]).then_inc(stored[k], 16)
                    run_steps(sp, step, CHUNKS, 0, 2)
                    for k in range(2):
                        sp.wait_ge(stored[k], 16 * ((CHUNKS + 1 - k) // 2))
            block_end()

        with nc.Fori(0, LAYERS) as layer:
            windows = nc.values_load(passes_i[0:1, 1:2], min_val=1, max_val=MAX_STEPS + 1,
                                     skip_runtime_bounds_check_because="the kernel works it out from spans of at most N")
            with nc.Fori(0, windows):
                conv_sweep()
                window_tables(windows, False)
            node_update(layer)

        with nc.Block() as block:
            @block.sync
            def _(sp):
                def step(c, k):
                    if active(c, 0, CHUNKS):
                        n = width(c) // P
                        if later(c, 2):
                            sp.wait_ge(filled, c - 1)
                        for table, ring, done in ((x1_tab, y_rows, landed2), (h_tab, x_rows, landed3)):
                            sp.dma_start(ring[:, k, 0:n, :], table[bass.ds(c * CHUNK, n * P), :].rearrange("(t p) d -> p t d", p=P)
                                         ).then_inc(done[k], 16)
                    if active(c, 1, CHUNKS):
                        d, j = c - 1, (k + 1) % 2
                        sp.wait_ge(scaled, d + 1)
                        if isinstance(d, int) and d == CHUNKS - 1:
                            sp.dma_start(out[d * CHUNK:N, :], x1_rows[0:N - d * CHUNK, j, 0, :]).then_inc(stored[j], 16)
                        else:
                            sp.dma_start(out[bass.ds(d * CHUNK, CHUNK), :].rearrange("(t p) d -> p t d", p=P),
                                         x1_rows[:, j, :, :]).then_inc(stored[j], 16)
                run_steps(sp, step, CHUNKS, 1, 2)
                for k in range(2):
                    sp.wait_ge(stored[k], 16 * ((CHUNKS + 1 - k) // 2))

            @block.scalar
            def _(act):
                def step(c, k):
                    act.wait_ge(hot_ready, c + 1)
                    ln_root(act, k, width(c) // P)
                run_steps(act, step, CHUNKS, 0, 2)

            @block.vector
            def _(dve):
                def step(c, k):
                    n = width(c) // P
                    dve.wait_ge(landed2[k], half16(c, k) + 16)
                    dve.wait_ge(landed3[k], half16(c, k) + 16)
                    if later(c, 2):
                        dve.wait_ge(scaled, c - 1)
                    nc.vector.tensor_tensor(v_rows[:, k, 0:n, :], y_rows[:, k, 0:n, :], x_rows[:, k, 0:n, :],
                                            ALU.add).then_inc(filled, 1)
                    dve.wait_ge(filled, c + 1)
                    ln_stats_of(dve, k, n, c * 3)
                    dve.wait_ge(recip_ready, c + 1)
                    if later(c, 2):
                        dve.wait_ge(stored[k], half16(c, k))
                    ln_apply(dve, k, n, c * 3 + 3)
                run_steps(dve, step, CHUNKS, 0, 2)


_INS = ["x", "src", "dst", "edge_type_8",
        "L0_gnn_W1", "L0_gnn_b1", "L0_gnn_W2", "L0_gnn_b2", "L0_gnn_gamma", "L0_gnn_beta",
        "L1_gnn_W1", "L1_gnn_root1", "L1_gnn_b1", "L1_gnn_W2", "L1_gnn_root2", "L1_gnn_b2",
        "L1_gnn_W3", "L1_gnn_root3", "L1_gnn_b3", "L1_gnn_res_w", "L1_gnn_res_b"]


def kernel(**inputs):
    import numpy as _np
    import concourse.bacc as _bacc
    from concourse import mybir as _mybir
    from concourse.bass_utils import run_bass_kernel_spmd as _run

    nc = _bacc.Bacc("TRN2", target_bir_lowering=False, num_devices=1)
    arrays, t = {}, {}
    for name in _INS:
        a = _np.ascontiguousarray(inputs[name])
        arrays[f"in_{name}_dram"] = a
        t[name] = nc.dram_tensor(f"in_{name}_dram", a.shape, _mybir.dt.from_np(a.dtype), kind="ExternalInput").ap()
    shape = tuple(inputs["x"].shape)
    out = nc.dram_tensor("out_0_dram", shape, _mybir.dt.float32, kind="ExternalOutput").ap()
    build_gnn(nc, t["x"], t["src"], t["dst"], t["edge_type_8"], t["L0_gnn_W1"], t["L0_gnn_b1"], t["L0_gnn_W2"],
              t["L0_gnn_b2"], t["L0_gnn_gamma"], t["L0_gnn_beta"],
              [t["L1_gnn_W1"], t["L1_gnn_W2"], t["L1_gnn_W3"]],
              [t["L1_gnn_root1"], t["L1_gnn_root2"], t["L1_gnn_root3"]],
              [t["L1_gnn_b1"], t["L1_gnn_b2"], t["L1_gnn_b3"]], t["L1_gnn_res_w"], t["L1_gnn_res_b"], out)
    r = _run(nc, [arrays], core_ids=[0])
    return r.results[0]["out_0_dram"]
```

```python
from contextlib import ExitStack, nullcontext

import concourse.bass as bass
from concourse import mybir

ALU = mybir.AluOpType
ACT = mybir.ActivationFunctionType
AX = mybir.AxisListType
F32 = mybir.dt.float32
BF16 = mybir.dt.bfloat16
I32 = mybir.dt.int32
SP, DVE = mybir.EngineType.SP, mybir.EngineType.DVE

P = 128
WINDOW = 16
GROUP = 4
SLOTS = 4
CHUNK = 4 * P
BIG = 2.0 ** 100
SPLIT = 3
EPS = 1e-5
EXP_LIMIT = 30.0


def run_steps(engine, step, count, lag, unroll):
    first = 2 * unroll
    assert lag <= first
    stop = count - count % unroll
    for s in range(first):
        step(s, s % unroll)
    with engine.Fori(first // unroll, stop // unroll) as i:
        for phase in range(unroll):
            step(i * unroll + phase, phase)
    for s in range(stop, count + lag):
        step(s, s % unroll)


def active(s, lag, count):
    return not isinstance(s, int) or 0 <= s - lag < count


def later(s, n):
    return not isinstance(s, int) or s >= n


def build_gnn(nc, x, src, dst, edge_type, w1, b1, w2, b2, gamma, beta, conv_w, conv_root, conv_b, res_w, res_b, out):
    N, D = x.shape
    E = src.shape[0]
    R = conv_w[0].shape[0]
    LAYERS = len(conv_w)
    assert D == P and R * WINDOW == P
    UNIT = P * GROUP * SLOTS
    GROUPS = -(-E // UNIT) * SLOTS
    TILES = GROUPS * GROUP
    BLOCKS = -(-(TILES + GROUP * SLOTS) // P)
    COLS = BLOCKS * P
    CHUNKS = -(-N // CHUNK)
    NP = -(-N // P) * P
    LAST = NP - (CHUNKS - 1) * CHUNK
    assert NP >= N + WINDOW and LAST % P == 0 and CHUNKS % 2 == 1
    PAD_DST = 2 * N
    MAX_STEPS = (N - 1) // WINDOW
    STAT = next(n for n in range(512, 0, -1) if N % n == 0)
    SIDE = 16 * (1 + GROUP)

    def width(c):
        return (LAST if c == CHUNKS - 1 else CHUNK) if isinstance(c, int) else CHUNK

    with ExitStack() as ctx:
        sems = []

        def sb(name, shape, dt=F32):
            return ctx.enter_context(nc.sbuf_tensor(name, shape, dt))

        def sem(name):
            s = ctx.enter_context(nc.semaphore(name))
            sems.append(s)
            return s

        def dram(name, shape, dt=F32):
            return nc.dram_tensor(name, shape, dt).ap()

        p_tab = dram("p_tab", [NP * SPLIT, P], BF16)
        q_tab = dram("q_tab", [NP, P])
        h_tab = dram("h_tab", [NP, P])
        x1_tab = dram("x1_tab", [NP, P])
        rel_tab = dram("rel_tab", [COLS, P], BF16)
        reset_tab = dram("reset_tab", [COLS, P], BF16)
        fac_tab = dram("fac_tab", [NP, SPLIT * R], BF16)

        acc = sb("acc", [P, NP])
        res_buf = sb("res_buf", [P, max(NP, TILES * R)])
        type_hot = res_buf[:, 0:TILES * R].rearrange("p (t r) -> p t r", r=R)
        cnt = sb("cnt", [R, NP])
        ident = sb("ident", [P, P])
        iota_p = sb("iota_p", [P, 1])
        iota_split = sb("iota_split", [P, 1])
        iota_row = sb("iota_row", [P, P])
        big_mat = sb("big_mat", [P, P])
        negbig_row = sb("negbig_row", [1, P])
        ones_row = sb("ones_row", [1, P])
        wsteps = sb("wsteps", [1, MAX_STEPS])
        w_pq = sb("w_pq", [P, 2 * P])
        w1a = sb("w1a", [P, P])
        b1_rows = sb("b1_rows", [P, P])
        w2m = sb("w2m", [P, P])
        cols = sb("cols", [P, 4 + LAYERS + 1])
        w_all = sb("w_all", [P, (LAYERS + 1) * R * P])
        root_all = sb("root_all", [P, (LAYERS + 1) * P])
        w_cur = sb("w_cur", [P, R * P])
        root_cur = sb("root_cur", [P, P])
        b_cur = sb("b_cur", [P, 1])
        resw_sb = sb("resw_sb", [P, P])
        dst_f = sb("dst_f", [P, BLOCKS, P])
        lo = sb("lo", [P, BLOCKS])
        base_f = sb("base_f", [P, BLOCKS])
        src_c = sb("src_c", [P, COLS])
        type_c = sb("type_c", [P, COLS])
        last_c = sb("last_c", [P, COLS])
        keys = sb("keys", [P, COLS, 2])
        key_rn = sb("key_rn", [P, COLS])
        base_i = sb("base_i", [1, COLS], I32)
        facts = sb("facts", [P, 4])
        norm = sb("norm", [P, 2])
        facts_row = sb("facts_row", [1, 4])
        passes_i = sb("passes_i", [1, 2], I32)
        shift = sb("shift", [P, 4])
        rows = sb("rows", [P, SLOTS * GROUP, P])
        idx_stage = sb("idx_stage", [P, SLOTS * GROUP], I32)
        arena = sb("arena", [P, 9 * 1024])

        def carve():
            at = [0]

            def take(shape, dt=F32, parts=P):
                n = 1
                for k in shape:
                    n *= k
                words = n if dt != BF16 else n // 2
                v = arena[0:parts, at[0]:at[0] + words]
                at[0] += words
                assert at[0] <= 9 * 1024
                if dt != F32:
                    v = v.bitcast(dt)
                names = "abcd"[:len(shape)]
                if len(shape) > 1:
                    v = v.rearrange("p (" + " ".join(names) + ") -> p " + " ".join(names),
                                    **{names[k]: shape[k] for k in range(1, len(shape))})
                return v
            return take

        banks = [ctx.enter_context(nc.psum_tensor(f"bank{i}", [P, 512], F32)) for i in range(8)]

        chain = sem("chain")
        act_chain = sem("act_chain")
        landed = sem("landed")
        landed2 = [sem(f"landed2_{k}") for k in range(2)]
        landed3 = [sem(f"landed3_{k}") for k in range(2)]
        stored = [sem(f"stored_{k}") for k in range(2)]
        stored2 = [sem(f"stored2_{k}") for k in range(2)]
        filled = sem("filled")
        row_landed = [sem(f"row_landed{t}") for t in range(SLOTS * GROUP)]
        reset_landed = [sem(f"reset_landed{g}") for g in range(SLOTS // 2)]
        side_landed = [sem(f"side_landed{g}") for g in range(SLOTS)]
        idx_ready, gather_go = sem("idx_ready"), sem("gather_go")
        hot_ready, z_done, clamp_ready, recip_ready, g_ready = (sem(n) for n in (
            "hot_ready", "z_done", "clamp_ready", "recip_ready", "g_ready"))
        m_done, scan_done, turned, turned_copied, select_ready, window_done, merged = (sem(n) for n in (
            "m_done", "scan_done", "turned", "turned_copied", "select_ready", "window_done", "merged"))
        stood = sem("stood")
        spread_ready, spread_done, z_copied, scaled = (sem(n) for n in (
            "spread_ready", "spread_done", "z_copied", "scaled"))

        def block_end():
            numbers = [s.num for s in sems]
            span = range(min(numbers), max(numbers) + 1)
            assert len(span) == len(sems)
            nc.gpsimd.dma_reset(span)
            nc.gpsimd.sem_clear(span)
            nc.all_engine_barrier()

        def stand(engine):
            engine.sem_inc(stood, 1)

        def linker(engine, semaphore):
            count = [0]

            def link(instruction):
                count[0] += 1
                instruction.then_inc(semaphore, 1)
                engine.wait_ge(semaphore, count[0])
            return link

        take = carve()
        dst_i, src_i, type_i = (take([BLOCKS, P], I32) for _ in range(3))
        src_f, type_f, starts, lasts, tmp_r = (take([BLOCKS, P]) for _ in range(5))
        reset_bf = take([BLOCKS, P], BF16)
        hi, pair, top = take([BLOCKS]), take([2]), take([1, 8])
        hits = take([MAX_STEPS])
        FULL = E // P
        WHOLE = FULL // P
        TAIL = E - FULL * P
        with nc.Block() as block:
            @block.sync
            def _(sp):
                sp.wait_ge(filled, 1)
                for table, edges in ((dst_i, dst), (src_i, src), (type_i, edge_type)):
                    sp.dma_start(table[:, 0:WHOLE, :],
                                 edges[0:WHOLE * P * P].rearrange("(a q e) -> q a e", q=P, e=P)).then_inc(landed, 16)
                    sp.dma_start(table[0:FULL - WHOLE * P, WHOLE, :],
                                 edges[WHOLE * P * P:FULL * P].rearrange("(q e) -> q e", e=P)).then_inc(landed, 16)
                    sp.dma_start(table[FULL - WHOLE * P:FULL - WHOLE * P + 1, WHOLE, 0:TAIL],
                                 edges[FULL * P:E].rearrange("(a e) -> a e", a=1)).then_inc(landed, 16)
                sp.dma_start(w_pq[:, P:2 * P], w1[D:2 * D, :]).then_inc(landed2[0], 16)
                sp.dma_start(w1a[:, :], w1[0:D, :]).then_inc(landed2[0], 16)
                sp.dma_start(w2m[:, :], w2).then_inc(landed2[0], 16)
                sp.dma_start(b1_rows[:, :], b1.rearrange("(a n) -> a n", a=1).to_broadcast([P, P])).then_inc(landed3[0], 16)
                with nc.allow_non_contiguous_dma("one value per partition"):
                    for k, vec in enumerate([b2, gamma, beta, res_b] + list(conv_b)):
                        sp.dma_start(cols[:, k:k + 1], vec.rearrange("(n a) -> n a", a=1)).then_inc(landed3[0], 16)
                for k in range(LAYERS):
                    sp.dma_start(w_all[:, k * R * P:(k + 1) * R * P].rearrange("p (r n) -> p r n", n=P),
                                 conv_w[k].rearrange("r d n -> d r n")).then_inc(landed3[0], 16)
                    sp.dma_start(root_all[:, k * P:(k + 1) * P], conv_root[k]).then_inc(landed3[0], 16)
                sp.dma_start(resw_sb[:, :], res_w).then_inc(landed3[0], 16)
                sp.wait_ge(landed3[0], 16 * (6 + 3 * LAYERS))
                sp.wait_ge(scan_done, 1)
                with nc.allow_non_contiguous_dma("rows of 256 bytes"):
                    sp.dma_start(reset_tab.rearrange("(a q) e -> q a e", q=P), reset_bf).then_inc(stored[0], 16)
                sp.wait_ge(stored[0], 16)

            @block.gpsimd
            def _(pool):
                link = linker(pool, gather_go)
                link(pool.memset(ident[:, :], 0.0))
                link(pool.affine_select(out=ident[:, :], in_=ident[:, :], compare_op=ALU.not_equal, fill=1.0,
                                        base=0, pattern=[[-1, P]], channel_multiplier=1))
                link(pool.iota(iota_p[:, :], pattern=[[0, 1]], base=0, channel_multiplier=1,
                               allow_small_or_imprecise_dtypes=True))
                link(pool.iota(iota_row[:, :], pattern=[[1, P]], base=0, channel_multiplier=0,
                               allow_small_or_imprecise_dtypes=True))
                link(pool.iota(wsteps[:, :], pattern=[[WINDOW, MAX_STEPS]], base=WINDOW, channel_multiplier=0,
                               allow_small_or_imprecise_dtypes=True))
                pool.memset(ones_row[:, :], 1.0)
                pool.memset(negbig_row[:, :], -BIG)
                pool.memset(big_mat[:, :], BIG)
                pool.memset(shift[:, :], 0.0)
                pool.memset(cols[:, 4 + LAYERS:5 + LAYERS], 0.0)
                pool.memset(w_all[:, LAYERS * R * P:(LAYERS + 1) * R * P], 0.0)
                pool.memset(root_all[:, LAYERS * P:(LAYERS + 1) * P], 0.0)
                pool.drain().then_inc(idx_ready, 1)

            @block.vector
            def _(dve):
                link = linker(dve, chain)
                dve.memset(dst_i, PAD_DST)
                dve.memset(src_i, 0)
                dve.memset(type_i, 0)
                dve.drain().then_inc(filled, 1)
                dve.wait_ge(landed, 16 * 9)
                dve.wait_ge(idx_ready, 1)
                link(nc.vector.tensor_copy(dst_f[:, :, :], dst_i))
                link(nc.vector.tensor_copy(src_f, src_i))
                link(nc.vector.tensor_copy(type_f, type_i))
                link(nc.vector.tensor_tensor(starts[:, :, 1:P], dst_f[:, :, 1:P], dst_f[:, :, 0:P - 1], ALU.not_equal))
                link(nc.vector.memset(starts[:, :, 0:1], 1.0))
                link(nc.vector.tensor_scalar(reset_bf, starts, -BIG, None, ALU.mult))
                nc.vector.tensor_copy(lasts[:, :, 0:P - 1], starts[:, :, 1:P]).then_inc(scan_done, 1)
                link(nc.vector.memset(lasts[:, :, P - 1:P], 1.0))
                link(nc.vector.tensor_reduce(lo[:, :], dst_f[:, :, :], AX.X, ALU.min))
                link(nc.vector.scalar_tensor_tensor(out=tmp_r, in0=dst_f[:, :, :], scalar=float(N), in1=dst_f[:, :, :],
                                                    op0=ALU.is_lt, op1=ALU.mult))
                link(nc.vector.tensor_reduce(hi, tmp_r, AX.X, ALU.max))
                link(nc.vector.tensor_tensor(hi, hi, lo[:, :], ALU.subtract))
                link(nc.vector.tensor_reduce(pair[:, 0:1], hi, AX.X, ALU.max))
                link(nc.vector.tensor_tensor(tmp_r[:, :, 1:P], dst_f[:, :, 1:P], dst_f[:, :, 0:P - 1], ALU.is_lt))
                link(nc.vector.tensor_reduce(pair[:, 1:2], tmp_r[:, :, 1:P], AX.XY, ALU.max))
                nc.vector.tensor_scalar(iota_split[:, :], iota_p[:, :], 0.0, None, ALU.mult).then_inc(hot_ready, 1)
                dve.wait_ge(z_done, 1)
                link(nc.vector.tensor_reduce(top[0:1, 0, 0:2], banks[0][0:1, 0:2 * P].rearrange("a (k q) -> a k q", q=P),
                                             AX.X, ALU.max))
                link(nc.vector.tensor_scalar(hits[0:1, :], wsteps[:, :], top[0:1, 0, 0:1], None, ALU.is_le))
                link(nc.vector.tensor_reduce(top[0:1, 0, 2:3], hits[0:1, :], AX.X, ALU.add))
                link(nc.vector.tensor_scalar(facts_row[:, 0:1], top[0:1, 0, 2:3], 1.0, None, ALU.add))
                link(nc.vector.tensor_scalar(facts_row[:, 1:2], top[0:1, 0, 1:2], P - 1.0, 1.0, ALU.mult, ALU.add))
                link(nc.vector.tensor_copy(facts_row[:, 2:3], top[0:1, 0, 1:2]))
                link(nc.vector.reciprocal(facts_row[:, 3:4], facts_row[:, 1:2]))
                link(nc.vector.tensor_tensor(top[0:1, 0, 4:5], facts_row[:, 0:1], facts_row[:, 1:2], ALU.mult))
                link(nc.vector.tensor_copy(passes_i[:, 0:1], top[0:1, 0, 4:5]))
                nc.vector.tensor_copy(passes_i[:, 1:2], facts_row[:, 0:1]).then_inc(hot_ready, 1)
                dve.wait_ge(z_done, 2)
                nc.vector.tensor_copy(facts[:, :], banks[0][:, 0:4])
                for k in range(1, WINDOW):
                    link(nc.vector.scalar_tensor_tensor(out=iota_split[:, :], in0=iota_p[:, :], scalar=float(SPLIT * k),
                                                        in1=iota_split[:, :], op0=ALU.is_ge, op1=ALU.add))
                dve.wait_ge(landed2[0], 48)
                nc.vector.tensor_tensor(w_pq[:, 0:P], w1a[:, :], w_pq[:, P:2 * P], ALU.subtract)
                nc.vector.tensor_scalar(w2m[:, :], w2m[:, :], -2.0, None, ALU.mult)
                for n, table in enumerate((src_c, type_c, last_c)):
                    for half in range(2):
                        dve.wait_ge(m_done, 2 * n + half + 1)
                        a, b = half * GROUP * P, min((half + 1) * GROUP * P, COLS)
                        ins = nc.vector.tensor_copy(table[:, a:b], banks[1 + half + 2 * n][:, 0:b - a])
                        if (n, half) == (1, 1):
                            ins.then_inc(hot_ready, 1)
                dve.wait_ge(hot_ready, 3)
                nc.vector.tensor_tensor(type_hot, iota_row[:, None, 0:R].to_broadcast([P, TILES, R]),
                                        type_c[:, 0:TILES, None].to_broadcast([P, TILES, R]), ALU.is_equal)

            @block.tensor
            def _(pe):
                pe.wait_ge(hot_ready, 1)
                for k in range(2):
                    last = nc.tensor.transpose(banks[0][0:1, k * P:(k + 1) * P], pair[:, k:k + 1], ident[:, :])
                last.then_inc(z_done, 1)
                pe.wait_ge(hot_ready, 2)
                nc.tensor.matmul(banks[0][:, 0:4], ones_row[0:1, :], facts_row[:, :], start=True, stop=True).then_inc(z_done, 1)
                for n, table in enumerate((src_f, type_f, lasts)):
                    for a in range(BLOCKS):
                        last = nc.tensor.transpose(banks[1 + 2 * n + a // GROUP][:, (a % GROUP) * P:(a % GROUP + 1) * P],
                                                   table[:, a, :], ident[:, :])
                        if a in (GROUP - 1, BLOCKS - 1):
                            last.then_inc(m_done, 1)
        block_end()

        take = carve()
        rel = take([BLOCKS, P])
        rel_bf = take([BLOCKS, P], BF16)
        rel_c, lastw, inside, work = (take([COLS]) for _ in range(4))
        picks = take([4])

        def window_tables(sweeps=None, by_edge=False):
            def guard(engine):
                return engine.If(sweeps > 1) if sweeps is not None else nullcontext()

            with nc.Block() as block:
                @block.sync
                def _(sp):
                    with guard(sp):
                        sp.wait_ge(scan_done, 1)
                        with nc.allow_non_contiguous_dma("rows of 256 bytes"):
                            sp.dma_start(rel_tab.rearrange("(a q) e -> q a e", q=P), rel_bf).then_inc(stored[0], 16)
                        sp.wait_ge(stored[0], 16)
                        stand(sp)

                @block.vector
                def _(dve):
                    with guard(dve):
                        link = linker(dve, chain)
                        if sweeps is not None:
                            step = 1.0 if by_edge else facts[:, 1:2]
                            link(nc.vector.tensor_scalar(shift[:, 2:3], shift[:, 2:3], step, None, ALU.add))
                            link(nc.vector.tensor_tensor(shift[:, 3:4], shift[:, 2:3], facts[:, 1:2], ALU.is_ge))
                            link(nc.vector.tensor_tensor(shift[:, 1:2], shift[:, 1:2], shift[:, 3:4], ALU.add))
                            link(nc.vector.tensor_tensor(shift[:, 3:4], shift[:, 3:4], facts[:, 1:2], ALU.mult))
                            link(nc.vector.tensor_tensor(shift[:, 2:3], shift[:, 2:3], shift[:, 3:4], ALU.subtract))
                            link(nc.vector.tensor_tensor(shift[:, 3:4], shift[:, 1:2], facts[:, 0:1], ALU.is_lt))
                            link(nc.vector.tensor_tensor(shift[:, 1:2], shift[:, 1:2], shift[:, 3:4], ALU.mult))
                            link(nc.vector.tensor_scalar(shift[:, 0:1], shift[:, 1:2], float(WINDOW), None, ALU.mult))
                        link(nc.vector.tensor_scalar(base_f[:, :], lo[:, :], shift[:, 0:1], None, ALU.add))
                        link(nc.vector.tensor_scalar(base_f[:, :], base_f[:, :], float(N), None, ALU.min))
                        nc.vector.tensor_tensor(rel, dst_f[:, :, :], base_f[:, :, None].to_broadcast([P, BLOCKS, P]),
                                                ALU.subtract).then_inc(hot_ready, 1)
                        dve.wait_ge(hot_ready, 1)
                        nc.vector.tensor_scalar(rel_bf, rel, -1.0, float(WINDOW), ALU.max, ALU.min).then_inc(scan_done, 1)
                        link(nc.vector.tensor_scalar(picks[:, 0:1], facts[:, 2:3], -1.0, 1.0, ALU.mult, ALU.add))
                        link(nc.vector.tensor_tensor(picks[:, 1:2], iota_p[:, :], shift[:, 2:3], ALU.is_equal))
                        link(nc.vector.tensor_tensor(picks[:, 2:3], picks[:, 1:2], facts[:, 2:3], ALU.mult))
                        link(nc.vector.tensor_scalar(lastw, last_c[:, :], picks[:, 0:1], picks[:, 2:3], ALU.mult, ALU.add))
                        dve.wait_ge(m_done, 1)
                        for a in range(0, BLOCKS, GROUP):
                            b = min(a + GROUP, BLOCKS)
                            link(nc.vector.tensor_copy(rel_c[:, a * P:b * P], banks[a // GROUP][:, 0:(b - a) * P]))
                            nc.vector.tensor_copy(base_i[:, a * P:b * P], banks[2 + a // GROUP][0:1, 0:(b - a) * P])
                        link(nc.vector.scalar_tensor_tensor(out=work, in0=rel_c, scalar=1.0, in1=lastw,
                                                            op0=ALU.add, op1=ALU.mult))
                        nc.vector.tensor_scalar(keys[:, :, 0], work, -1.0, None, ALU.add)
                        nc.vector.tensor_copy(keys[:, :, 1], rel_c)
                        link(nc.vector.tensor_scalar(inside, rel_c, 0.0, None, ALU.is_ge))
                        link(nc.vector.scalar_tensor_tensor(out=inside, in0=rel_c, scalar=WINDOW - 1.0, in1=inside,
                                                            op0=ALU.is_le, op1=ALU.mult))
                        link(nc.vector.scalar_tensor_tensor(out=work, in0=type_c[:, :], scalar=float(WINDOW), in1=rel_c,
                                                            op0=ALU.mult, op1=ALU.add))
                        link(nc.vector.scalar_tensor_tensor(out=work, in0=work, scalar=1.0, in1=inside,
                                                            op0=ALU.add, op1=ALU.mult))
                        nc.vector.tensor_scalar(key_rn[:, :], work, -1.0, None, ALU.add)

                @block.tensor
                def _(pe):
                    with guard(pe):
                        pe.wait_ge(hot_ready, 1)
                        for a in range(BLOCKS):
                            nc.tensor.transpose(banks[a // GROUP][:, (a % GROUP) * P:(a % GROUP + 1) * P], rel[:, a, :],
                                                ident[:, :])
                            last = nc.tensor.transpose(banks[2 + a // GROUP][0:1, (a % GROUP) * P:(a % GROUP + 1) * P],
                                                       base_f[:, a:a + 1], ident[:, :])
                        last.then_inc(m_done, 1)
            block_end()

        window_tables()

        take = carve()
        x_ring = take([2, GROUP, P])
        xt = take([2, CHUNK])
        p_f = take([2, GROUP, P])
        p_parts = take([2, GROUP, SPLIT, P], BF16)
        q_rows = take([2, GROUP, P])
        with nc.Block() as block:
            @block.sync
            def _(sp):
                def step(c, k):
                    if active(c, 0, CHUNKS):
                        n = width(c) // P
                        if later(c, 2):
                            sp.wait_ge(turned, c - 1)
                        if isinstance(c, int) and c == CHUNKS - 1:
                            sp.wait_ge(filled, 1)
                            sp.dma_start(x_ring[0:N - c * CHUNK, k, 0, :], x[c * CHUNK:N, :]).then_inc(landed2[k], 16)
                        else:
                            sp.dma_start(x_ring[:, k, :, :],
                                         x[bass.ds(c * CHUNK, CHUNK), :].rearrange("(t p) d -> p t d", p=P)).then_inc(landed2[k], 16)
                    if active(c, 2, CHUNKS):
                        d = c - 2
                        n = width(d) // P
                        sp.wait_ge(m_done, d + 1)
                        sp.dma_start(p_tab[bass.ds(d * (CHUNK * SPLIT), n * P * SPLIT), :].rearrange("(t p c) d -> p t c d", p=P, c=SPLIT),
                                     p_parts[:, k, 0:n, :, :]).then_inc(stored[k], 16)
                        sp.wait_ge(z_copied, d + 1)
                        sp.dma_start(q_tab[bass.ds(d * CHUNK, n * P), :].rearrange("(t p) d -> p t d", p=P),
                                     q_rows[:, k, 0:n, :]).then_inc(stored2[k], 16)
                run_steps(sp, step, CHUNKS, 2, 2)
                for k in range(2):
                    sp.wait_ge(stored[k], 16 * ((CHUNKS + 1 - k) // 2))
                    sp.wait_ge(stored2[k], 16 * ((CHUNKS + 1 - k) // 2))

            @block.tensor
            def _(pe):
                def step(c, k):
                    if active(c, 0, CHUNKS):
                        n = width(c) // P
                        pe.wait_ge(landed2[k], (c // 2 + 1) * 16 if isinstance(c, int) else (c - k) * 8 + 16)
                        if later(c, 2):
                            pe.wait_ge(turned_copied, c - 1)
                        for t in range(n):
                            last = nc.tensor.transpose(banks[k][:, t * P:(t + 1) * P], x_ring[:, k, t, :], ident[:, :])
                        last.then_inc(turned, 1)
                    if active(c, 1, CHUNKS):
                        d, j = c - 1, (k + 1) % 2
                        n = width(d) // P
                        pe.wait_ge(turned_copied, d + 1)
                        if later(d, 2):
                            pe.wait_ge(chain, d * 5 - 9)
                            pe.wait_ge(z_copied, d - 1)
                        for t in range(n):
                            nc.tensor.matmul(banks[2 + j][:, t * P:(t + 1) * P], xt[:, j, t * P:(t + 1) * P],
                                             w_pq[:, 0:P], start=(t == 0), stop=True, skip_group_check=True)
                            last = nc.tensor.matmul(banks[4 + j][:, t * P:(t + 1) * P], xt[:, j, t * P:(t + 1) * P],
                                                    w_pq[:, P:2 * P], start=(t == 0), stop=True, skip_group_check=True)
                        last.then_inc(z_done, 1)
                run_steps(pe, step, CHUNKS, 1, 2)

            @block.scalar
            def _(act):
                def step(c, k):
                    if active(c, 0, CHUNKS):
                        w = width(c)
                        act.wait_ge(turned, c + 1)
                        if later(c, 2):
                            act.wait_ge(z_done, c - 1)
                        nc.scalar.copy(xt[:, k, 0:w], banks[k][:, 0:w]).then_inc(turned_copied, 1)
                    if active(c, 1, CHUNKS):
                        d, j = c - 1, (k + 1) % 2
                        n = width(d) // P
                        act.wait_ge(z_done, d + 1)
                        if later(d, 2):
                            act.wait_ge(stored2[j], (d // 2) * 16 if isinstance(d, int) else (d - j) * 8)
                        nc.scalar.copy(q_rows[:, j, 0:n, :], banks[4 + j][:, 0:n * P].rearrange("p (t d) -> p t d", d=P)).then_inc(z_copied, 1)
                run_steps(act, step, CHUNKS, 1, 2)

            @block.gpsimd
            def _(pool):
                pool.wait_ge(turned, CHUNKS - 2)
                pool.memset(x_ring[:, (CHUNKS - 1) % 2, 0, :], 0.0).then_inc(filled, 1)

            @block.vector
            def _(dve):
                dve.memset(acc[:, :], -BIG)
                dve.memset(cnt[:, :], 0.0)

                def step(c, k):
                    n = width(c) // P
                    left, parts = p_f[:, k, 0:n, :], p_parts[:, k, 0:n, :, :]
                    dve.wait_ge(z_done, c + 1)
                    if later(c, 2):
                        dve.wait_ge(stored[k], (c // 2) * 16 if isinstance(c, int) else (c - k) * 8)
                    link_at = c * 5
                    nc.vector.tensor_tensor(left, banks[2 + k][:, 0:n * P].rearrange("p (t d) -> p t d", d=P),
                                            b1_rows[:, None, :].to_broadcast([P, n, P]), ALU.add).then_inc(chain, 1)
                    dve.wait_ge(chain, link_at + 1)
                    nc.vector.tensor_copy(parts[:, :, 0, :], left).then_inc(chain, 1)
                    dve.wait_ge(chain, link_at + 2)
                    nc.vector.tensor_tensor(left, left, parts[:, :, 0, :], ALU.subtract).then_inc(chain, 1)
                    dve.wait_ge(chain, link_at + 3)
                    nc.vector.tensor_copy(parts[:, :, 1, :], left).then_inc(chain, 1)
                    dve.wait_ge(chain, link_at + 4)
                    nc.vector.tensor_tensor(left, left, parts[:, :, 1, :], ALU.subtract).then_inc(chain, 1)
                    dve.wait_ge(chain, link_at + 5)
                    nc.vector.tensor_copy(parts[:, :, 2, :], left).then_inc(m_done, 1)
                run_steps(dve, step, CHUNKS, 0, 2)
        block_end()

        take = carve()
        rel_ring = take([SLOTS, GROUP * P], BF16, WINDOW * SPLIT)
        reset_ring = take([SLOTS, GROUP * P], BF16)
        p_ring = take([SLOTS * GROUP, P], BF16, WINDOW * SPLIT)
        hot = take([2, GROUP * P], BF16, WINDOW * SPLIT)
        zc = take([2, GROUP * P])
        er = take([2, GROUP * P])
        g_t = take([2, GROUP * P])
        scanned = take([2, GROUP * P])
        scanned_t = take([2, GROUP, P])
        select = take([2, GROUP, 2, WINDOW])
        rel_flat = rel_tab.rearrange("t e -> (t e)")
        reset_flat = reset_tab.rearrange("t e -> (t e)")

        def gather_rows(pool, table, reader_done):
            def body(i):
                for g in range(SLOTS):
                    pool.wait_ge(idx_ready, i * SLOTS + g + 1)
                    if not isinstance(i, int):
                        pool.wait_ge(reader_done, (i - 1) * SLOTS + g + 1)
                    stand(pool)
                    for t in range(g * GROUP, (g + 1) * GROUP):
                        pool.indirect_dma_start(rows[:, t, :], None, table,
                                                bass.IndirectOffsetOnAxis(ap=idx_stage[:, t:t + 1], axis=0)
                                                ).then_inc(row_landed[t], 16)
            body(0)
            with pool.Fori(1, GROUPS // SLOTS) as i:
                body(i)

        def stage_indices(act, s, k):
            stand(act)
            nc.scalar.copy(idx_stage[:, k * GROUP:(k + 1) * GROUP],
                           src_c[:, bass.ds(s * GROUP, GROUP)]).then_inc(idx_ready, 1)

        def rows_here(pe, s, k, t):
            pe.wait_ge(row_landed[k * GROUP + t], (s // SLOTS + 1) * 16 if isinstance(s, int) else (s - k) * 4 + 16)

        def tile_bases(engine, s):
            _, values = nc.values_load_multi_w_load_instructions(
                base_i[0:1, bass.ds(s * GROUP, GROUP)], engines=[engine], min_val=0, max_val=N,
                skip_runtime_bounds_check_because="the tables hold no base above N")
            return values

        def edge_sweep():
            with nc.Block() as block:
                @block.gpsimd
                def _(pool):
                    gather_rows(pool, q_tab, z_done)

                @block.sync
                def _(sp):
                    def step(s, k):
                        if active(s, 0, GROUPS):
                            if later(s, SLOTS):
                                sp.wait_ge(z_done, s - SLOTS + 1)
                            sp.dma_start(rel_ring[:, k, :], rel_flat[None, bass.ds(s * (GROUP * P), GROUP * P)]
                                         .to_broadcast([WINDOW * SPLIT, GROUP * P])).then_inc(side_landed[k], 16)
                            for t, b in enumerate(tile_bases(SP, s)):
                                sp.dma_start(p_ring[:, k * GROUP + t, :], p_tab[bass.ds(b * SPLIT, WINDOW * SPLIT), :]
                                             ).then_inc(side_landed[k], 16)
                        if k % 2 == 0 and active(s, 2, GROUPS):
                            j, q = s - 2, 1 - k // 2
                            if later(j, SLOTS):
                                sp.wait_ge(scan_done, j - 2)
                            sp.dma_start(reset_ring[:, 2 * q:2 * q + 2, :], reset_flat[None, bass.ds(j * (GROUP * P), 2 * GROUP * P)]
                                         .rearrange("a (g e) -> a g e", g=2).to_broadcast([P, 2, GROUP * P])
                                         ).then_inc(reset_landed[q], 16)
                    run_steps(sp, step, GROUPS, 2, SLOTS)

                def side_here(engine, s, k):
                    engine.wait_ge(side_landed[k], (s // SLOTS + 1) * SIDE if isinstance(s, int) else (s - k) * (SIDE // SLOTS) + SIDE)

                @block.tensor
                def _(pe):
                    def step(s, k):
                        b, c = k % 2, (k + 1) % 2
                        if active(s, 5, GROUPS):
                            j = s - 5
                            pe.wait_ge(scan_done, j + 1)
                            if later(j, 1):
                                pe.wait_ge(turned_copied, j)
                            for t in range(GROUP):
                                last = nc.tensor.transpose(banks[5][:, t * P:(t + 1) * P],
                                                           scanned[:, c, t * P:(t + 1) * P], ident[:, :])
                            last.then_inc(turned, 1)
                        if active(s, 6, GROUPS):
                            j = s - 6
                            pe.wait_ge(select_ready, j + 1)
                            pe.wait_ge(turned_copied, j + 1)
                            if later(j, 2):
                                pe.wait_ge(merged, (j - 1) * (2 * GROUP))
                            best = banks[6 + b][:, 0:GROUP * WINDOW]
                            nc.tensor.matmul(best.rearrange("p (t n) -> p t n", n=WINDOW), big_mat[:, :], select[:, b, :, 0, :],
                                             start=True, stop=False, skip_group_check=True)
                            nc.tensor.matmul(best, negbig_row[:, :], ones_row[0:1, 0:GROUP * WINDOW], start=False,
                                             stop=False, skip_group_check=True)
                            for t in range(GROUP):
                                nc.tensor.matmul(best[:, t * WINDOW:(t + 1) * WINDOW], scanned_t[:, b, t, :],
                                                 select[:, b, t, 0, :], start=False, stop=True, skip_group_check=True)
                                last = nc.tensor.matmul(
                                    banks[6 + b][0:R, (GROUP + t) * WINDOW:(GROUP + t + 1) * WINDOW],
                                    type_now[:, b, t, :], select[:, b, t, 1, :], start=False, stop=True,
                                    skip_group_check=True)
                            last.then_inc(window_done, 1)
                        if active(s, 1, GROUPS):
                            j, slot = s - 1, (k + 3) % SLOTS
                            side_here(pe, j, slot)
                            pe.wait_ge(hot_ready, j + 1)
                            if later(j, SLOTS):
                                pe.wait_ge(g_ready, j - 3)
                            for t in range(GROUP):
                                rows_here(pe, j, slot, t)
                                nc.tensor.matmul(banks[slot][:, t * P:(t + 1) * P], rows[:, slot * GROUP + t, :], ident[:, :],
                                                 start=(t == 0), stop=False, is_transpose=True, skip_group_check=True)
                                last = nc.tensor.matmul(banks[slot][:, t * P:(t + 1) * P], p_ring[:, slot * GROUP + t, :],
                                                        hot[:, c, t * P:(t + 1) * P], start=False, stop=True,
                                                        skip_group_check=True)
                            last.then_inc(z_done, 1)
                        if active(s, 3, GROUPS):
                            j = s - 3
                            pe.wait_ge(g_ready, j + 1)
                            if later(j, 1):
                                pe.wait_ge(scan_done, j)
                            nc.tensor.matmul(banks[4][:, :], w2m[:, :], g_t[:, c, :], start=True, stop=True).then_inc(m_done, 1)
                    run_steps(pe, step, GROUPS, 6, SLOTS)

                @block.scalar
                def _(act):
                    nc.scalar.preload_act_table_set("natural_log_exp_and_others")
                    for k in range(SLOTS):
                        stage_indices(act, k, k)

                    def step(s, k):
                        b, c = k % 2, (k + 1) % 2
                        if active(s, 2, GROUPS):
                            act.wait_ge(z_done, s - 1)
                            stage_indices(act, s - 2 + SLOTS, (k + 2) % SLOTS)
                        if active(s, 5, GROUPS):
                            j = s - 5
                            act.wait_ge(turned, j + 1)
                            if later(j, 2):
                                act.wait_ge(window_done, j - 1)
                            nc.scalar.copy(scanned_t[:, c, :, :], banks[5][:, :].rearrange("p (t d) -> p t d", d=P)
                                           ).then_inc(turned_copied, 1)
                        if active(s, 2, GROUPS):
                            j = s - 2
                            act.wait_ge(clamp_ready, j + 1)
                            if later(j, 2):
                                act.wait_ge(g_ready, j - 1)
                            now = er[:, b, :]
                            nc.scalar.activation(now, zc[:, b, :], ACT.Exp).then_inc(act_chain, 1)
                            act.wait_ge(act_chain, j * 3 + 1)
                            nc.scalar.activation(now, now, ACT.Square, bias=1.0).then_inc(act_chain, 1)
                            act.wait_ge(act_chain, j * 3 + 2)
                            nc.scalar.activation(now, now, ACT.Ln, bias=1.0).then_inc(act_chain, 1)
                            act.wait_ge(act_chain, j * 3 + 3)
                            nc.scalar.activation(now, now, ACT.Exp, scale=-1.0).then_inc(recip_ready, 1)
                    run_steps(act, step, GROUPS, 5, SLOTS)

                @block.vector
                def _(dve):
                    def step(s, k):
                        b, c = k % 2, (k + 1) % 2
                        if active(s, 2, GROUPS):
                            j = s - 2
                            dve.wait_ge(z_done, j + 1)
                            if later(j, 2):
                                dve.wait_ge(recip_ready, j - 1)
                            nc.vector.tensor_scalar(zc[:, b, :], banks[(k + 2) % SLOTS][:, :], EXP_LIMIT, None, ALU.min
                                                    ).then_inc(clamp_ready, 1)
                        if active(s, 3, GROUPS):
                            j = s - 3
                            dve.wait_ge(recip_ready, j + 1)
                            if later(j, 2):
                                dve.wait_ge(m_done, j - 1)
                            nc.vector.scalar_tensor_tensor(out=g_t[:, c, :], in0=er[:, c, :], scalar=-0.5,
                                                           in1=banks[(k + 1) % SLOTS][:, :], op0=ALU.add, op1=ALU.mult
                                                           ).then_inc(g_ready, 1)
                        if active(s, 4, GROUPS):
                            j, q = s - 4, k // 2
                            dve.wait_ge(m_done, j + 1)
                            dve.wait_ge(reset_landed[q], (j // SLOTS + 1) * 16 if isinstance(j, int) else (j - k) * 4 + 16)
                            if later(j, 2):
                                dve.wait_ge(turned, j - 1)
                            nc.vector.tensor_tensor_scan(scanned[:, b, :], reset_ring[:, k, :], banks[4][:, :],
                                                         0.0, ALU.add, ALU.max).then_inc(scan_done, 1)
                        if active(s, 0, GROUPS):
                            side_here(dve, s, k)
                            if later(s, 2):
                                dve.wait_ge(z_done, s - 1)
                            nc.vector.tensor_scalar(hot[:, b, :], rel_ring[:, k, :], iota_split[0:WINDOW * SPLIT, :], None,
                                                    ALU.is_equal).then_inc(hot_ready, 1)
                        if active(s, 5, GROUPS):
                            j = s - 5
                            if later(j, 2):
                                dve.wait_ge(window_done, j - 1)
                            nc.vector.tensor_copy(type_now[:, c, :, :], type_hot[:, bass.ds(j * GROUP, GROUP), :])
                            nc.vector.tensor_tensor(
                                select[:, c, :, :, :],
                                iota_row[:, None, None, 0:WINDOW].to_broadcast([P, GROUP, 2, WINDOW]),
                                keys[:, bass.ds(j * GROUP, GROUP), :, None].to_broadcast([P, GROUP, 2, WINDOW]),
                                ALU.is_equal).then_inc(select_ready, 1)
                        if active(s, 7, GROUPS):
                            j = s - 7
                            dve.wait_ge(window_done, j + 1)
                            at = j * (2 * GROUP)
                            for t, w in enumerate(tile_bases(DVE, j)):
                                if later(j, 1) or t:
                                    dve.wait_ge(merged, at + 2 * t)
                                nc.vector.tensor_tensor(acc[:, bass.ds(w, WINDOW)], acc[:, bass.ds(w, WINDOW)],
                                                        banks[6 + c][:, t * WINDOW:(t + 1) * WINDOW], ALU.max).then_inc(merged, 1)
                                nc.vector.tensor_tensor(cnt[:, bass.ds(w, WINDOW)], cnt[:, bass.ds(w, WINDOW)],
                                                        banks[6 + c][0:R, (GROUP + t) * WINDOW:(GROUP + t + 1) * WINDOW],
                                                        ALU.add).then_inc(merged, 1)
                    run_steps(dve, step, GROUPS, 7, SLOTS)
            block_end()

        type_now = take([2, GROUP, R])
        sweeps = nc.values_load(passes_i[0:1, 0:1], min_val=1, max_val=P * (MAX_STEPS + 1),
                                skip_runtime_bounds_check_because="the kernel works it out from spans of at most N")
        with nc.Fori(0, sweeps):
            edge_sweep()
            window_tables(sweeps, True)

        take = carve()
        nodes_ok = take([STAT])
        stats = take([N // STAT, 6])
        mv = take([8])
        factor = take([NP // P, R])
        factor_parts = take([NP // P, SPLIT, R], BF16)
        with nc.Block() as block:
            @block.sync
            def _(sp):
                sp.wait_ge(spread_ready, 1)
                with nc.allow_non_contiguous_dma("rows of 48 bytes"):
                    sp.dma_start(fac_tab.rearrange("(t p) m -> p t m", p=P),
                                 factor_parts.rearrange("p t c r -> p t (c r)")).then_inc(stored[0], 16)
                sp.wait_ge(stored[0], 16)

            @block.tensor
            def _(pe):
                for t in range(NP // P):
                    last = nc.tensor.transpose(banks[0][:, t * R:(t + 1) * R], cnt[:, t * P:(t + 1) * P], ident[0:R, 0:R])
                last.then_inc(turned, 1)

            @block.vector
            def _(dve):
                link = linker(dve, chain)
                dve.wait_ge(turned, 1)
                link(nc.vector.tensor_scalar(factor, banks[0][:, 0:NP // P * R].rearrange("p (t r) -> p t r", r=R),
                                             facts[:, 3:4], 1.0, ALU.mult, ALU.max))
                link(nc.vector.reciprocal(factor, factor))
                link(nc.vector.tensor_copy(factor_parts[:, :, 0, :], factor))
                link(nc.vector.tensor_tensor(factor, factor, factor_parts[:, :, 0, :], ALU.subtract))
                link(nc.vector.tensor_copy(factor_parts[:, :, 1, :], factor))
                link(nc.vector.tensor_tensor(factor, factor, factor_parts[:, :, 1, :], ALU.subtract))
                nc.vector.tensor_copy(factor_parts[:, :, 2, :], factor).then_inc(spread_ready, 1)
                nc.vector.memset(acc[:, N:NP], 0.0)

                def part(s, k):
                    here = acc[:, bass.ds(s * STAT, STAT)]
                    at = 2 * s
                    if later(s, 1):
                        dve.wait_ge(scaled, at + s)
                    nc.vector.tensor_scalar(nodes_ok, here, -BIG / 2, None, ALU.is_gt).then_inc(scaled, 1)
                    dve.wait_ge(scaled, at + s + 1)
                    nc.vector.scalar_tensor_tensor(out=here, in0=here, scalar=cols[:, 0:1], in1=nodes_ok, op0=ALU.add,
                                                   op1=ALU.mult).then_inc(scaled, 1)
                    dve.wait_ge(scaled, at + s + 2)
                    nc.vector.bn_stats(stats[:, bass.ds(s, 1), :], here).then_inc(scaled, 1)
                part(0, 0)
                with dve.Fori(1, N // STAT) as i:
                    part(i, 0)
                dve.wait_ge(scaled, 3 * (N // STAT))
                link(nc.vector.bn_aggr(mv[:, 0:2], stats))
                nc.vector.tensor_scalar(mv[:, 2:3], mv[:, 1:2], EPS, None, ALU.add).then_inc(hot_ready, 1)
                dve.wait_ge(z_copied, 1)
                link(nc.vector.reciprocal(mv[:, 4:5], mv[:, 3:4]))
                link(nc.vector.tensor_tensor(norm[:, 0:1], mv[:, 4:5], cols[:, 1:2], ALU.mult))
                link(nc.vector.tensor_tensor(mv[:, 5:6], mv[:, 0:1], norm[:, 0:1], ALU.mult))
                nc.vector.tensor_tensor(norm[:, 1:2], cols[:, 2:3], mv[:, 5:6], ALU.subtract)

            @block.scalar
            def _(act):
                act.wait_ge(hot_ready, 1)
                nc.scalar.activation(mv[:, 3:4], mv[:, 2:3], ACT.Sqrt).then_inc(z_copied, 1)
                link = linker(act, act_chain)
                link(nc.scalar.copy(w_cur[:, :], w_all[:, 0:R * P]))
                link(nc.scalar.copy(b_cur[:, :], cols[:, 4:5]))
        block_end()

        take = carve()
        y_t = take([2, CHUNK])
        x_rows = take([2, GROUP, P])
        v_rows = take([2, GROUP, P])
        x1_rows = take([2, GROUP, P])
        x1_t = take([2, CHUNK])
        ln_stats = take([2, GROUP, 6])
        ln_mv = take([2, GROUP, 2])
        ln_sd = take([2, GROUP])
        y_rows = take([2, GROUP, P])

        def ln_stats_of(dve, k, n, at):
            for t in range(n):
                last = nc.vector.bn_stats(ln_stats[:, k, t, :], v_rows[:, k, t, :])
            last.then_inc(chain, 1)
            dve.wait_ge(chain, at + 1)
            stand(dve)
            for t in range(n):
                last = nc.vector.bn_aggr(ln_mv[:, k, t, :], ln_stats[:, k, t, :])
            last.then_inc(chain, 1)
            dve.wait_ge(chain, at + 2)
            nc.vector.tensor_scalar(ln_sd[:, k, 0:n], ln_mv[:, k, 0:n, 1], EPS, None, ALU.add).then_inc(hot_ready, 1)

        def ln_apply(dve, k, n, at):
            nc.vector.reciprocal(ln_sd[:, k, 0:n], ln_sd[:, k, 0:n]).then_inc(chain, 1)
            dve.wait_ge(chain, at)
            for t in range(n):
                last = nc.vector.tensor_scalar(x1_rows[:, k, t, :], v_rows[:, k, t, :], ln_mv[:, k, t, 0:1],
                                               ln_sd[:, k, t:t + 1], ALU.subtract, ALU.mult)
            last.then_inc(scaled, 1)

        def ln_root(act, k, n):
            nc.scalar.activation(ln_sd[:, k, 0:n], ln_sd[:, k, 0:n], ACT.Sqrt).then_inc(recip_ready, 1)

        def half16(c, k):
            return (c // 2) * 16 if isinstance(c, int) else (c - k) * 8

        with nc.Block() as block:
            @block.sync
            def _(sp):
                def step(c, k):
                    if active(c, 0, CHUNKS):
                        if later(c, 2):
                            sp.wait_ge(filled, c - 1)
                        if isinstance(c, int) and c == CHUNKS - 1:
                            sp.wait_ge(spread_ready, 1)
                            sp.dma_start(x_rows[0:N - c * CHUNK, k, 0, :], x[c * CHUNK:N, :]).then_inc(landed2[k], 16)
                        else:
                            sp.dma_start(x_rows[:, k, :, :],
                                         x[bass.ds(c * CHUNK, CHUNK), :].rearrange("(t p) d -> p t d", p=P)).then_inc(landed2[k], 16)
                    if active(c, 2, CHUNKS):
                        d = c - 2
                        n = width(d) // P
                        sp.wait_ge(scaled, d + 1)
                        for table, done in ((h_tab, stored), (x1_tab, stored2)):
                            sp.dma_start(table[bass.ds(d * CHUNK, n * P), :].rearrange("(t p) d -> p t d", p=P),
                                         x1_rows[:, k, 0:n, :]).then_inc(done[k], 16)
                run_steps(sp, step, CHUNKS, 2, 2)
                for k in range(2):
                    sp.wait_ge(stored[k], 16 * ((CHUNKS + 1 - k) // 2))
                    sp.wait_ge(stored2[k], 16 * ((CHUNKS + 1 - k) // 2))

            @block.scalar
            def _(act):
                def step(c, k):
                    if active(c, 0, CHUNKS):
                        w = width(c)
                        if later(c, 2):
                            act.wait_ge(turned, c - 1)
                        nc.scalar.activation(y_t[:, k, 0:w], acc[:, bass.ds(c * CHUNK, w)], ACT.Identity,
                                             bias=norm[:, 1:2], scale=norm[:, 0:1]).then_inc(clamp_ready, 1)
                        act.wait_ge(hot_ready, c + 1)
                        ln_root(act, k, w // P)
                    if active(c, 1, CHUNKS):
                        d, j = c - 1, (k + 1) % 2
                        w = width(d)
                        act.wait_ge(m_done, d + 1)
                        if later(d, 2):
                            act.wait_ge(window_done, d - 1)
                        nc.scalar.copy(x1_t[:, j, 0:w], banks[2 + j][:, 0:w]).then_inc(turned_copied, 1)
                        act.wait_ge(window_done, d + 1)
                        stand(act)
                        nc.scalar.copy(acc[:, bass.ds(d * CHUNK, w)], banks[4 + j][:, 0:w]).then_inc(z_copied, 1)
                        nc.scalar.activation(res_buf[:, bass.ds(d * CHUNK, w)], banks[6 + j][:, 0:w], ACT.Identity,
                                             bias=cols[:, 3:4]).then_inc(z_copied, 1)
                run_steps(act, step, CHUNKS, 1, 2)

            @block.tensor
            def _(pe):
                def step(c, k):
                    if active(c, 0, CHUNKS):
                        n = width(c) // P
                        pe.wait_ge(clamp_ready, c + 1)
                        if later(c, 2):
                            pe.wait_ge(filled, c - 1)
                        for t in range(n):
                            last = nc.tensor.transpose(banks[k][:, t * P:(t + 1) * P], y_t[:, k, t * P:(t + 1) * P], ident[:, :])
                        last.then_inc(turned, 1)
                    if active(c, 1, CHUNKS):
                        d, j = c - 1, (k + 1) % 2
                        w = width(d)
                        pe.wait_ge(scaled, d + 1)
                        if later(d, 2):
                            pe.wait_ge(turned_copied, d - 1)
                        for t in range(w // P):
                            last = nc.tensor.transpose(banks[2 + j][:, t * P:(t + 1) * P], x1_rows[:, j, t, :], ident[:, :])
                        last.then_inc(m_done, 1)
                        pe.wait_ge(turned_copied, d + 1)
                        if later(d, 2):
                            pe.wait_ge(z_copied, 2 * d - 2)
                        nc.tensor.matmul(banks[4 + j][:, 0:w], root_all[:, 0:P], x1_t[:, j, 0:w], start=True, stop=True)
                        nc.tensor.matmul(banks[6 + j][:, 0:w], resw_sb[:, :], x1_t[:, j, 0:w], start=True, stop=True
                                         ).then_inc(window_done, 1)
                run_steps(pe, step, CHUNKS, 1, 2)

            @block.vector
            def _(dve):
                def step(c, k):
                    n = width(c) // P
                    dve.wait_ge(turned, c + 1)
                    dve.wait_ge(landed2[k], half16(c, k) + 16)
                    if later(c, 2):
                        dve.wait_ge(scaled, c - 1)
                    nc.vector.tensor_tensor(v_rows[:, k, 0:n, :], banks[k][:, 0:n * P].rearrange("p (t d) -> p t d", d=P),
                                            x_rows[:, k, 0:n, :], ALU.add).then_inc(filled, 1)
                    dve.wait_ge(filled, c + 1)
                    ln_stats_of(dve, k, n, c * 3)
                    dve.wait_ge(recip_ready, c + 1)
                    if later(c, 2):
                        dve.wait_ge(stored[k], half16(c, k))
                        dve.wait_ge(stored2[k], half16(c, k))
                        dve.wait_ge(m_done, c - 1)
                    ln_apply(dve, k, n, c * 3 + 3)
                run_steps(dve, step, CHUNKS, 0, 2)

            @block.gpsimd
            def _(pool):
                pool.wait_ge(filled, CHUNKS - 2)
                pool.memset(x_rows[:, (CHUNKS - 1) % 2, 0, :], 0.0).then_inc(spread_ready, 1)
        block_end()

        take = carve()
        rel_ring16 = take([SLOTS, GROUP * P], BF16, WINDOW)
        fac_ring = take([SLOTS * GROUP, SPLIT * R], BF16, WINDOW)
        hot16 = take([2, GROUP * P], BF16, WINDOW)
        type_sel = take([2, GROUP, 1, R])
        fac_sel = take([2, GROUP, SPLIT * R])
        edge_fac = take([2, GROUP])
        key_now = take([2, GROUP])
        onehot = take([2, GROUP, P])
        z_sb = take([2, 2 * GROUP, R, WINDOW])

        def conv_sweep():
            with nc.Block() as block:
                @block.gpsimd
                def _(pool):
                    gather_rows(pool, h_tab, z_done)

                @block.sync
                def _(sp):
                    def step(s, k):
                        if later(s, SLOTS):
                            sp.wait_ge(m_done, s - SLOTS + 1)
                        sp.dma_start(rel_ring16[:, k, :], rel_flat[None, bass.ds(s * (GROUP * P), GROUP * P)]
                                     .to_broadcast([WINDOW, GROUP * P])).then_inc(side_landed[k], 16)
                        for t, b in enumerate(tile_bases(SP, s)):
                            sp.dma_start(fac_ring[:, k * GROUP + t, :], fac_tab[bass.ds(b, WINDOW), :]
                                         ).then_inc(side_landed[k], 16)
                    run_steps(sp, step, GROUPS, 0, SLOTS)

                def side_here(engine, s, k):
                    engine.wait_ge(side_landed[k], (s // SLOTS + 1) * SIDE if isinstance(s, int)
                                   else (s - k) * (SIDE // SLOTS) + SIDE)

                @block.tensor
                def _(pe):
                    def step(s, k):
                        b, c = k % 2, (k + 1) % 2
                        if active(s, 3, GROUPS):
                            j, slot = s - 3, (k + 1) % SLOTS
                            pe.wait_ge(select_ready, j + 1)
                            if later(j, 2):
                                pe.wait_ge(z_copied, j - 1)
                            for t in range(GROUP):
                                rows_here(pe, j, slot, t)
                                last = nc.tensor.matmul(banks[c][:, t * P:(t + 1) * P], rows[:, slot * GROUP + t, :],
                                                        onehot[:, c, t, :], start=(t == 0), stop=True, skip_group_check=True)
                            last.then_inc(z_done, 1)
                        if active(s, 1, GROUPS):
                            j, slot = s - 1, (k + 3) % SLOTS
                            side_here(pe, j, slot)
                            pe.wait_ge(hot_ready, j + 1)
                            if later(j, 2):
                                pe.wait_ge(scaled, j - 1)
                            for t in range(GROUP):
                                last = nc.tensor.matmul(banks[6 + c][:, t * SPLIT * R:(t + 1) * SPLIT * R],
                                                        hot16[:, c, t * P:(t + 1) * P], fac_ring[:, slot * GROUP + t, :],
                                                        start=(t == 0), stop=True, skip_group_check=True)
                            last.then_inc(m_done, 1)
                        if k % 2 == 0 and active(s, 5, GROUPS):
                            j, q = s - 5, 1 - k // 2
                            pe.wait_ge(z_copied, j + 1)
                            if later(j, 4):
                                pe.wait_ge(merged, (j - 3) * GROUP)
                            for r in range(R):
                                last = nc.tensor.matmul(banks[4 + q][:, 0:2 * GROUP * WINDOW].rearrange("p (t n) -> p t n", n=WINDOW),
                                                        w_cur[:, r * P:(r + 1) * P],
                                                        z_sb[:, q, :, r, :], start=(r == 0), stop=(r == R - 1))
                            last.then_inc(window_done, 2)
                    run_steps(pe, step, GROUPS, 5, SLOTS)

                @block.scalar
                def _(act):
                    for k in range(SLOTS):
                        stage_indices(act, k, k)

                    def step(s, k):
                        if active(s, 3, GROUPS):
                            j, slot = s - 3, (k + 1) % SLOTS
                            q, half = slot // 2, slot % 2
                            act.wait_ge(z_done, j + 1)
                            stage_indices(act, j + SLOTS, slot)
                            if later(j, 4):
                                act.wait_ge(window_done, j - 3 if half else j - 2)
                            nc.scalar.copy(z_sb[:, q, half * GROUP:(half + 1) * GROUP, :, :],
                                           banks[half][:, :].rearrange("p (t r n) -> p t r n", r=R, n=WINDOW)
                                           ).then_inc(z_copied, 1)
                    run_steps(act, step, GROUPS, 3, SLOTS)

                @block.vector
                def _(dve):
                    def step(s, k):
                        b, c = k % 2, (k + 1) % 2
                        if active(s, 2, GROUPS):
                            j = s - 2
                            if later(j, 2):
                                dve.wait_ge(z_done, j - 1)
                            nc.vector.tensor_tensor(type_sel[:, b, :, 0, :], iota_row[:, None, 0:R].to_broadcast([P, GROUP, R]),
                                                    type_c[:, bass.ds(j * GROUP, GROUP), None].to_broadcast([P, GROUP, R]),
                                                    ALU.is_equal).then_inc(chain, 1)
                            nc.vector.tensor_copy(key_now[:, b, :], key_rn[:, bass.ds(j * GROUP, GROUP)])
                            dve.wait_ge(chain, j * 2 + 1)
                            dve.wait_ge(m_done, j + 1)
                            nc.vector.tensor_tensor(fac_sel[:, b, :, :].rearrange("p t (c r) -> p t c r", r=R),
                                                    banks[6 + b][:, 0:GROUP * SPLIT * R].rearrange("p (t c r) -> p t c r", c=SPLIT, r=R),
                                                    type_sel[:, b, :, :, :].to_broadcast([P, GROUP, SPLIT, R]),
                                                    ALU.mult).then_inc(scaled, 1)
                            dve.wait_ge(scaled, j + 1)
                            nc.vector.tensor_reduce(edge_fac[:, b, :], fac_sel[:, b, :, :], AX.X, ALU.add).then_inc(chain, 1)
                            dve.wait_ge(chain, j * 2 + 2)
                            for t in range(GROUP):
                                last = nc.vector.tensor_scalar(onehot[:, b, t, :], iota_row[:, :],
                                                               key_now[:, b, t:t + 1], edge_fac[:, b, t:t + 1],
                                                               ALU.is_equal, ALU.mult)
                            last.then_inc(select_ready, 1)
                        if active(s, 0, GROUPS):
                            side_here(dve, s, k)
                            if later(s, 2):
                                dve.wait_ge(m_done, s - 1)
                            nc.vector.tensor_scalar(hot16[:, b, :], rel_ring16[:, k, :], iota_p[0:WINDOW, :], None,
                                                    ALU.is_equal).then_inc(hot_ready, 1)
                        if active(s, 7, GROUPS):
                            j, slot = s - 7, (k + 1) % SLOTS
                            q, half = slot // 2, slot % 2
                            dve.wait_ge(window_done, j + 1 if half else j + 2)
                            for t, w in enumerate(tile_bases(DVE, j)):
                                if later(j, 1) or t:
                                    dve.wait_ge(merged, j * GROUP + t)
                                col = (half * GROUP + t) * WINDOW
                                nc.vector.tensor_tensor(acc[:, bass.ds(w, WINDOW)], acc[:, bass.ds(w, WINDOW)],
                                                        banks[4 + q][:, col:col + WINDOW], ALU.add).then_inc(merged, 1)
                    run_steps(dve, step, GROUPS, 7, SLOTS)
            block_end()

        take = carve()
        relu_t = take([2, CHUNK])
        h_t = take([2, CHUNK])
        h_rows = take([2, GROUP, P])

        def node_update(layer):
            with nc.Block() as block:
                @block.scalar
                def _(act):
                    nc.scalar.copy(root_cur[:, :], root_all[:, bass.ds((layer + 1) * P, P)]).then_inc(act_chain, 1)

                    def step(c, k):
                        if active(c, 0, CHUNKS):
                            w = width(c)
                            if later(c, 2):
                                act.wait_ge(g_ready, c - 1)
                            nc.scalar.activation(relu_t[:, k, 0:w], acc[:, bass.ds(c * CHUNK, w)], ACT.Relu,
                                                 bias=b_cur[:, :]).then_inc(clamp_ready, 1)
                        if active(c, 1, CHUNKS):
                            d, j = c - 1, (k + 1) % 2
                            w = width(d)
                            act.wait_ge(z_done, d + 1)
                            act.wait_ge(clamp_ready, d + 1)
                            stand(act)
                            nc.scalar.copy(acc[:, bass.ds(d * CHUNK, w)], banks[2 + j][:, 0:w]).then_inc(z_copied, 1)
                    run_steps(act, step, CHUNKS, 1, 2)
                    act.wait_ge(clamp_ready, CHUNKS)
                    nc.scalar.copy(w_cur[:, :], w_all[:, bass.ds((layer + 1) * (R * P), R * P)])
                    nc.scalar.copy(b_cur[:, :], cols[:, bass.ds(layer + 5, 1)])

                @block.vector
                def _(dve):
                    def step(c, k):
                        if active(c, 0, CHUNKS):
                            w = width(c)
                            dve.wait_ge(clamp_ready, c + 1)
                            if later(c, 2):
                                dve.wait_ge(z_done, c - 1)
                            nc.vector.tensor_tensor(h_t[:, k, 0:w], relu_t[:, k, 0:w], res_buf[:, bass.ds(c * CHUNK, w)],
                                                    ALU.add).then_inc(g_ready, 1)
                        if active(c, 1, CHUNKS):
                            d, j = c - 1, (k + 1) % 2
                            n = width(d) // P
                            dve.wait_ge(turned, d + 1)
                            if later(d, 2):
                                dve.wait_ge(stored[j], half16(d, j))
                            nc.vector.tensor_copy(h_rows[:, j, 0:n, :], banks[j][:, 0:n * P].rearrange("p (t d) -> p t d", d=P)
                                                  ).then_inc(turned_copied, 1)
                    run_steps(dve, step, CHUNKS, 1, 2)

                @block.tensor
                def _(pe):
                    pe.wait_ge(act_chain, 1)

                    def step(c, k):
                        w = width(c)
                        pe.wait_ge(g_ready, c + 1)
                        if later(c, 2):
                            pe.wait_ge(turned_copied, c - 1)
                        for t in range(w // P):
                            last = nc.tensor.transpose(banks[k][:, t * P:(t + 1) * P], h_t[:, k, t * P:(t + 1) * P], ident[:, :])
                        last.then_inc(turned, 1)
                        if later(c, 2):
                            pe.wait_ge(z_copied, c - 1)
                        nc.tensor.matmul(banks[2 + k][:, 0:w], root_cur[:, :], h_t[:, k, 0:w], start=True, stop=True
                                         ).then_inc(z_done, 1)
                    run_steps(pe, step, CHUNKS, 0, 2)

                @block.sync
                def _(sp):
                    def step(c, k):
                        n = width(c) // P
                        sp.wait_ge(turned_copied, c + 1)
                        sp.dma_start(h_tab[bass.ds(c * CHUNK, n * P), :].rearrange("(t p) d -> p t d", p=P),
                                     h_rows[:, k, 0:n, :]).then_inc(stored[k], 16)
                    run_steps(sp, step, CHUNKS, 0, 2)
                    for k in range(2):
                        sp.wait_ge(stored[k], 16 * ((CHUNKS + 1 - k) // 2))
            block_end()

        with nc.Fori(0, LAYERS) as layer:
            windows = nc.values_load(passes_i[0:1, 1:2], min_val=1, max_val=MAX_STEPS + 1,
                                     skip_runtime_bounds_check_because="the kernel works it out from spans of at most N")
            with nc.Fori(0, windows):
                conv_sweep()
                window_tables(windows, False)
            node_update(layer)

        with nc.Block() as block:
            @block.sync
            def _(sp):
                def step(c, k):
                    if active(c, 0, CHUNKS):
                        n = width(c) // P
                        if later(c, 2):
                            sp.wait_ge(filled, c - 1)
                        for table, ring, done in ((x1_tab, y_rows, landed2), (h_tab, x_rows, landed3)):
                            sp.dma_start(ring[:, k, 0:n, :], table[bass.ds(c * CHUNK, n * P), :].rearrange("(t p) d -> p t d", p=P)
                                         ).then_inc(done[k], 16)
                    if active(c, 1, CHUNKS):
                        d, j = c - 1, (k + 1) % 2
                        sp.wait_ge(scaled, d + 1)
                        if isinstance(d, int) and d == CHUNKS - 1:
                            sp.dma_start(out[d * CHUNK:N, :], x1_rows[0:N - d * CHUNK, j, 0, :]).then_inc(stored[j], 16)
                        else:
                            sp.dma_start(out[bass.ds(d * CHUNK, CHUNK), :].rearrange("(t p) d -> p t d", p=P),
                                         x1_rows[:, j, :, :]).then_inc(stored[j], 16)
                run_steps(sp, step, CHUNKS, 1, 2)
                for k in range(2):
                    sp.wait_ge(stored[k], 16 * ((CHUNKS + 1 - k) // 2))

            @block.scalar
            def _(act):
                def step(c, k):
                    act.wait_ge(hot_ready, c + 1)
                    ln_root(act, k, width(c) // P)
                run_steps(act, step, CHUNKS, 0, 2)

            @block.vector
            def _(dve):
                def step(c, k):
                    n = width(c) // P
                    dve.wait_ge(landed2[k], half16(c, k) + 16)
                    dve.wait_ge(landed3[k], half16(c, k) + 16)
                    if later(c, 2):
                        dve.wait_ge(scaled, c - 1)
                    nc.vector.tensor_tensor(v_rows[:, k, 0:n, :], y_rows[:, k, 0:n, :], x_rows[:, k, 0:n, :],
                                            ALU.add).then_inc(filled, 1)
                    dve.wait_ge(filled, c + 1)
                    ln_stats_of(dve, k, n, c * 3)
                    dve.wait_ge(recip_ready, c + 1)
                    if later(c, 2):
                        dve.wait_ge(stored[k], half16(c, k))
                    ln_apply(dve, k, n, c * 3 + 3)
                run_steps(dve, step, CHUNKS, 0, 2)


_INS = ["x", "src", "dst", "edge_type_8",
        "L0_gnn_W1", "L0_gnn_b1", "L0_gnn_W2", "L0_gnn_b2", "L0_gnn_gamma", "L0_gnn_beta",
        "L1_gnn_W1", "L1_gnn_root1", "L1_gnn_b1", "L1_gnn_W2", "L1_gnn_root2", "L1_gnn_b2",
        "L1_gnn_W3", "L1_gnn_root3", "L1_gnn_b3", "L1_gnn_res_w", "L1_gnn_res_b"]


def kernel(**inputs):
    import numpy as _np
    import concourse.bacc as _bacc
    from concourse import mybir as _mybir
    from concourse.bass_utils import run_bass_kernel_spmd as _run

    nc = _bacc.Bacc("TRN2", target_bir_lowering=False, num_devices=1)
    arrays, t = {}, {}
    for name in _INS:
        a = _np.ascontiguousarray(inputs[name])
        arrays[f"in_{name}_dram"] = a
        t[name] = nc.dram_tensor(f"in_{name}_dram", a.shape, _mybir.dt.from_np(a.dtype), kind="ExternalInput").ap()
    shape = tuple(inputs["x"].shape)
    out = nc.dram_tensor("out_0_dram", shape, _mybir.dt.float32, kind="ExternalOutput").ap()
    build_gnn(nc, t["x"], t["src"], t["dst"], t["edge_type_8"], t["L0_gnn_W1"], t["L0_gnn_b1"], t["L0_gnn_W2"],
              t["L0_gnn_b2"], t["L0_gnn_gamma"], t["L0_gnn_beta"],
              [t["L1_gnn_W1"], t["L1_gnn_W2"], t["L1_gnn_W3"]],
              [t["L1_gnn_root1"], t["L1_gnn_root2"], t["L1_gnn_root3"]],
              [t["L1_gnn_b1"], t["L1_gnn_b2"], t["L1_gnn_b3"]], t["L1_gnn_res_w"], t["L1_gnn_res_b"], out)
    r = _run(nc, [arrays], core_ids=[0])
    return r.results[0]["out_0_dram"]
```

```python
from contextlib import ExitStack, nullcontext

import concourse.bass as bass
from concourse import mybir

ALU = mybir.AluOpType
ACT = mybir.ActivationFunctionType
AX = mybir.AxisListType
F32 = mybir.dt.float32
BF16 = mybir.dt.bfloat16
I32 = mybir.dt.int32
SP, DVE = mybir.EngineType.SP, mybir.EngineType.DVE

P = 128
WINDOW = 16
GROUP = 4
SLOTS = 4
CHUNK = 4 * P
BIG = 2.0 ** 100
SPLIT = 3
ROUND = 1.5 * 2.0 ** 23
EPS = 1e-5
EXP_LIMIT = 30.0


def run_steps(engine, step, count, lag, unroll):
    first = 2 * unroll
    assert lag <= first
    stop = count - count % unroll
    for s in range(first):
        step(s, s % unroll)
    with engine.Fori(first // unroll, stop // unroll) as i:
        for phase in range(unroll):
            step(i * unroll + phase, phase)
    for s in range(stop, count + lag):
        step(s, s % unroll)


def active(s, lag, count):
    return not isinstance(s, int) or 0 <= s - lag < count


def later(s, n):
    return not isinstance(s, int) or s >= n


def build_gnn(nc, x, src, dst, edge_type, w1, b1, w2, b2, gamma, beta, conv_w, conv_root, conv_b, res_w, res_b, out):
    N, D = x.shape
    E = src.shape[0]
    R = conv_w[0].shape[0]
    LAYERS = len(conv_w)
    assert D == P and R * WINDOW == P
    UNIT = P * GROUP * SLOTS
    GROUPS = -(-E // UNIT) * SLOTS
    TILES = GROUPS * GROUP
    BLOCKS = -(-(TILES + GROUP * SLOTS) // P)
    COLS = BLOCKS * P
    HALVES = -(-BLOCKS // GROUP)
    assert HALVES <= 2
    CHUNKS = -(-N // CHUNK)
    NP = -(-N // P) * P
    LAST = NP - (CHUNKS - 1) * CHUNK
    assert NP >= N + WINDOW and LAST % P == 0 and CHUNKS % 2 == 1
    PAD_DST = 2 * N
    MAX_STEPS = (N - 1) // WINDOW
    STAT = next(n for n in range(512, 0, -1) if N % n == 0)
    STATS = N // STAT
    WIDE = next(n for n in range(5, 0, -1) if STATS % n == 0)
    SIDE = 16 * (1 + GROUP)

    def width(c):
        return (LAST if c == CHUNKS - 1 else CHUNK) if isinstance(c, int) else CHUNK

    with ExitStack() as ctx:
        sems = []

        def sb(name, shape, dt=F32):
            return ctx.enter_context(nc.sbuf_tensor(name, shape, dt))

        def sem(name):
            s = ctx.enter_context(nc.semaphore(name))
            sems.append(s)
            return s

        def dram(name, shape, dt=F32):
            return nc.dram_tensor(name, shape, dt).ap()

        p_tab = dram("p_tab", [NP * SPLIT, P], BF16)
        q_tab = dram("q_tab", [NP, P])
        h_tab = dram("h_tab", [NP, P])
        x1_tab = dram("x1_tab", [NP, P])
        rel_tab = dram("rel_tab", [COLS, P], BF16)
        reset_tab = dram("reset_tab", [COLS, P], BF16)
        fac_tab = dram("fac_tab", [NP, SPLIT * R], BF16)

        acc = sb("acc", [P, NP])
        res_buf = sb("res_buf", [P, NP])
        x_all = res_buf[:, :].rearrange("p (t d) -> p t d", d=P)
        cnt = sb("cnt", [R, NP])
        ident = sb("ident", [P, P])
        iota_p = sb("iota_p", [P, 1])
        iota_split = sb("iota_split", [P, 1])
        iota_row = sb("iota_row", [P, P])
        big_mat = sb("big_mat", [P, P], BF16)
        negbig_row = sb("negbig_row", [1, P], BF16)
        ones_bf = sb("ones_bf", [1, P], BF16)
        ones_row = sb("ones_row", [1, P])
        wsteps = sb("wsteps", [1, MAX_STEPS])
        w_pq = sb("w_pq", [P, 2 * P])
        w1a = sb("w1a", [P, P])
        b1_rows = sb("b1_rows", [P, P])
        w2m = sb("w2m", [P, P])
        cols = sb("cols", [P, 4 + LAYERS])
        w_all = sb("w_all", [P, LAYERS * R * P])
        root_all = sb("root_all", [P, LAYERS * P])
        w_cur = sb("w_cur", [P, R * P])
        root_cur = sb("root_cur", [P, P])
        b_cur = sb("b_cur", [P, 1])
        resw_sb = sb("resw_sb", [P, P])
        dst_f = sb("dst_f", [P, BLOCKS, P])
        lo = sb("lo", [P, BLOCKS])
        base_f = sb("base_f", [P, BLOCKS])
        src_c = sb("src_c", [P, COLS])
        last_c = sb("last_c", [P, COLS])
        keys = sb("keys", [P, COLS, 3])
        type_c = keys[:, :, 2]
        key_rn = sb("key_rn", [P, COLS])
        base_i = sb("base_i", [1, COLS], I32)
        facts = sb("facts", [P, 4])
        norm = sb("norm", [P, 2])
        facts_row = sb("facts_row", [1, 4])
        passes_i = sb("passes_i", [1, 2], I32)
        shift = sb("shift", [P, 4])
        rows = sb("rows", [P, SLOTS * GROUP, P])
        idx_stage = sb("idx_stage", [P, SLOTS * GROUP], I32)
        arena = sb("arena", [P, 9 * 1024])

        def carve():
            at = [0]

            def take(shape, dt=F32, parts=P):
                n = 1
                for k in shape:
                    n *= k
                words = n if dt != BF16 else n // 2
                v = arena[0:parts, at[0]:at[0] + words]
                at[0] += words
                assert at[0] <= 9 * 1024
                if dt != F32:
                    v = v.bitcast(dt)
                names = "abcd"[:len(shape)]
                if len(shape) > 1:
                    v = v.rearrange("p (" + " ".join(names) + ") -> p " + " ".join(names),
                                    **{names[k]: shape[k] for k in range(1, len(shape))})
                return v
            return take

        banks = [ctx.enter_context(nc.psum_tensor(f"bank{i}", [P, 512], F32)) for i in range(8)]

        chain = sem("chain")
        act_chain = sem("act_chain")
        landed = sem("landed")
        landed2 = [sem(f"landed2_{k}") for k in range(2)]
        landed3 = [sem(f"landed3_{k}") for k in range(2)]
        stored = [sem(f"stored_{k}") for k in range(2)]
        stored2 = [sem(f"stored2_{k}") for k in range(2)]
        filled = sem("filled")
        row_landed = [sem(f"row_landed{t}") for t in range(SLOTS * GROUP)]
        reset_landed = [sem(f"reset_landed{g}") for g in range(SLOTS // 2)]
        side_landed = [sem(f"side_landed{g}") for g in range(SLOTS)]
        idx_ready = sem("idx_ready")
        pool_chain = sem("pool_chain")
        hot_ready, z_done, clamp_ready, recip_ready, g_ready = (sem(n) for n in (
            "hot_ready", "z_done", "clamp_ready", "recip_ready", "g_ready"))
        m_done, scan_done, turned, turned_copied, select_ready, window_done, merged = (sem(n) for n in (
            "m_done", "scan_done", "turned", "turned_copied", "select_ready", "window_done", "merged"))
        stood = sem("stood")
        spread_ready, z_copied, scaled = (sem(n) for n in ("spread_ready", "z_copied", "scaled"))

        def block_end():
            numbers = [s.num for s in sems]
            span = range(min(numbers), max(numbers) + 1)
            assert len(span) == len(sems)
            nc.gpsimd.dma_reset(span)
            nc.gpsimd.sem_clear(span)
            nc.all_engine_barrier()

        def stand(engine):
            engine.sem_inc(stood, 1)

        def linker(engine, semaphore):
            count = [0]

            def link(instruction):
                count[0] += 1
                instruction.then_inc(semaphore, 1)
                engine.wait_ge(semaphore, count[0])
            return link

        take = carve()
        dst_i, src_i, type_i = (take([BLOCKS, P], I32) for _ in range(3))
        src_f, type_f, starts, lasts, tmp_r = (take([BLOCKS, P]) for _ in range(5))
        reset_bf = take([BLOCKS, P], BF16)
        hi, pair, top = take([BLOCKS]), take([2]), take([1, 8])
        hits = take([MAX_STEPS])
        FULL = E // P
        WHOLE = FULL // P
        TAIL = E - FULL * P
        with nc.Block() as block:
            @block.sync
            def _(sp):
                sp.wait_ge(filled, 1)
                for table, edges in ((dst_i, dst), (src_i, src), (type_i, edge_type)):
                    sp.dma_start(table[:, 0:WHOLE, :],
                                 edges[0:WHOLE * P * P].rearrange("(a q e) -> q a e", q=P, e=P)).then_inc(landed, 16)
                    sp.dma_start(table[0:FULL - WHOLE * P, WHOLE, :],
                                 edges[WHOLE * P * P:FULL * P].rearrange("(q e) -> q e", e=P)).then_inc(landed, 16)
                    sp.dma_start(table[FULL - WHOLE * P:FULL - WHOLE * P + 1, WHOLE, 0:TAIL],
                                 edges[FULL * P:E].rearrange("(a e) -> a e", a=1)).then_inc(landed, 16)
                sp.dma_start(w_pq[:, P:2 * P], w1[D:2 * D, :]).then_inc(landed2[0], 16)
                sp.dma_start(w1a[:, :], w1[0:D, :]).then_inc(landed2[0], 16)
                sp.dma_start(w2m[:, :], w2).then_inc(landed2[0], 16)
                sp.dma_start(b1_rows[:, :], b1.rearrange("(a n) -> a n", a=1).to_broadcast([P, P])).then_inc(landed3[0], 16)
                with nc.allow_non_contiguous_dma("one value per partition"):
                    for k, vec in enumerate([b2, gamma, beta, res_b] + list(conv_b)):
                        sp.dma_start(cols[:, k:k + 1], vec.rearrange("(n a) -> n a", a=1)).then_inc(landed3[0], 16)
                for k in range(LAYERS):
                    sp.dma_start(w_all[:, k * R * P:(k + 1) * R * P].rearrange("p (r n) -> p r n", n=P),
                                 conv_w[k].rearrange("r d n -> d r n")).then_inc(landed3[0], 16)
                    sp.dma_start(root_all[:, k * P:(k + 1) * P], conv_root[k]).then_inc(landed3[0], 16)
                sp.dma_start(resw_sb[:, :], res_w).then_inc(landed3[0], 16)
                sp.wait_ge(landed3[0], 16 * (6 + 3 * LAYERS))
                sp.wait_ge(scan_done, 1)
                with nc.allow_non_contiguous_dma("rows of 256 bytes"):
                    sp.dma_start(reset_tab.rearrange("(a q) e -> q a e", q=P), reset_bf).then_inc(stored[0], 16)
                sp.wait_ge(stored[0], 16)

            @block.gpsimd
            def _(pool):
                link = linker(pool, pool_chain)
                pool.memset(x_all[:, NP // P - 1, :], 0.0).then_inc(spread_ready, 1)
                link(pool.memset(ident[:, :], 0.0))
                link(pool.affine_select(out=ident[:, :], in_=ident[:, :], compare_op=ALU.not_equal, fill=1.0,
                                        base=0, pattern=[[-1, P]], channel_multiplier=1))
                link(pool.iota(iota_p[:, :], pattern=[[0, 1]], base=0, channel_multiplier=1,
                               allow_small_or_imprecise_dtypes=True))
                link(pool.iota(iota_row[:, :], pattern=[[1, P]], base=0, channel_multiplier=0,
                               allow_small_or_imprecise_dtypes=True))
                link(pool.iota(wsteps[:, :], pattern=[[WINDOW, MAX_STEPS]], base=WINDOW, channel_multiplier=0,
                               allow_small_or_imprecise_dtypes=True))
                pool.memset(ones_row[:, :], 1.0)
                pool.memset(ones_bf[:, :], 1.0)
                pool.memset(negbig_row[:, :], -BIG)
                pool.memset(big_mat[:, :], BIG)
                pool.memset(shift[:, :], 0.0)
                pool.drain().then_inc(idx_ready, 1)
                pool.memset(acc[:, :], -BIG)
                pool.memset(cnt[:, :], 0.0)

            @block.vector
            def _(dve):
                link = linker(dve, chain)
                dve.memset(dst_i, PAD_DST)
                dve.memset(src_i, 0)
                dve.memset(type_i, 0)
                dve.drain().then_inc(filled, 1)
                dve.wait_ge(landed, 16 * 9)
                dve.wait_ge(idx_ready, 1)
                link(nc.vector.tensor_copy(dst_f[:, :, :], dst_i))
                link(nc.vector.tensor_copy(src_f, src_i))
                link(nc.vector.tensor_copy(type_f, type_i))
                link(nc.vector.tensor_tensor(starts[:, :, 1:P], dst_f[:, :, 1:P], dst_f[:, :, 0:P - 1], ALU.not_equal))
                link(nc.vector.memset(starts[:, :, 0:1], 1.0))
                link(nc.vector.tensor_scalar(reset_bf, starts, -BIG, None, ALU.mult))
                nc.vector.tensor_copy(lasts[:, :, 0:P - 1], starts[:, :, 1:P]).then_inc(scan_done, 1)
                link(nc.vector.memset(lasts[:, :, P - 1:P], 1.0))
                link(nc.vector.tensor_reduce(lo[:, :], dst_f[:, :, :], AX.X, ALU.min))
                link(nc.vector.scalar_tensor_tensor(out=tmp_r, in0=dst_f[:, :, :], scalar=float(N), in1=dst_f[:, :, :],
                                                    op0=ALU.is_lt, op1=ALU.mult))
                link(nc.vector.tensor_reduce(hi, tmp_r, AX.X, ALU.max))
                link(nc.vector.tensor_tensor(hi, hi, lo[:, :], ALU.subtract))
                link(nc.vector.tensor_reduce(pair[:, 0:1], hi, AX.X, ALU.max))
                link(nc.vector.tensor_tensor(tmp_r[:, :, 1:P], dst_f[:, :, 1:P], dst_f[:, :, 0:P - 1], ALU.is_lt))
                link(nc.vector.tensor_reduce(pair[:, 1:2], tmp_r[:, :, 1:P], AX.XY, ALU.max))
                dve.drain().then_inc(hot_ready, 1)
                dve.wait_ge(z_done, 1)
                link(nc.vector.tensor_reduce(top[0:1, 0, 0:2], banks[0][0:1, 0:2 * P].rearrange("a (k q) -> a k q", q=P),
                                             AX.X, ALU.max))
                link(nc.vector.tensor_scalar(hits[0:1, :], wsteps[:, :], top[0:1, 0, 0:1], None, ALU.is_le))
                link(nc.vector.tensor_reduce(top[0:1, 0, 2:3], hits[0:1, :], AX.X, ALU.add))
                link(nc.vector.tensor_scalar(facts_row[:, 0:1], top[0:1, 0, 2:3], 1.0, None, ALU.add))
                link(nc.vector.tensor_scalar(facts_row[:, 1:2], top[0:1, 0, 1:2], P - 1.0, 1.0, ALU.mult, ALU.add))
                link(nc.vector.tensor_copy(facts_row[:, 2:3], top[0:1, 0, 1:2]))
                link(nc.vector.reciprocal(facts_row[:, 3:4], facts_row[:, 1:2]))
                link(nc.vector.tensor_tensor(top[0:1, 0, 4:5], facts_row[:, 0:1], facts_row[:, 1:2], ALU.mult))
                link(nc.vector.tensor_copy(passes_i[:, 0:1], top[0:1, 0, 4:5]))
                nc.vector.tensor_copy(passes_i[:, 1:2], facts_row[:, 0:1]).then_inc(hot_ready, 1)
                dve.wait_ge(z_done, 2)
                nc.vector.tensor_copy(facts[:, :], banks[0][:, 0:4])
                link(nc.vector.tensor_scalar(iota_split[:, :], iota_p[:, :], -(SPLIT - 1) / 2, 1.0 / SPLIT, ALU.add, ALU.mult))
                link(nc.vector.tensor_scalar(iota_split[:, :], iota_split[:, :], ROUND, None, ALU.add))
                link(nc.vector.tensor_scalar(iota_split[:, :], iota_split[:, :], -ROUND, None, ALU.add))
                dve.wait_ge(landed2[0], 48)
                nc.vector.tensor_tensor(w_pq[:, 0:P], w1a[:, :], w_pq[:, P:2 * P], ALU.subtract)
                nc.vector.tensor_scalar(w2m[:, :], w2m[:, :], -2.0, None, ALU.mult)
                for n, table in enumerate((src_c[:, :], type_c, last_c[:, :])):
                    for half in range(HALVES):
                        dve.wait_ge(m_done, HALVES * n + half + 1)
                        a, b = half * GROUP * P, min((half + 1) * GROUP * P, COLS)
                        nc.vector.tensor_copy(table[:, a:b], banks[1 + half + 2 * n][:, 0:b - a])

            @block.scalar
            def _(act):
                whole = N // P
                act.wait_ge(landed, 16 * 9)
                for a, b in ((0, whole // 2), (whole // 2, whole)):
                    act.dma_start(x_all[:, a:b, :], x[a * P:b * P, :].rearrange("(t p) d -> p t d", p=P)
                                  ).then_inc(landed3[1], 16)
                act.wait_ge(spread_ready, 1)
                act.dma_start(x_all[0:N - whole * P, whole, :], x[whole * P:N, :]).then_inc(landed3[1], 16)
                act.wait_ge(landed3[1], 48)

            @block.tensor
            def _(pe):
                pe.wait_ge(hot_ready, 1)
                for k in range(2):
                    last = nc.tensor.transpose(banks[0][0:1, k * P:(k + 1) * P], pair[:, k:k + 1], ident[:, :])
                last.then_inc(z_done, 1)
                pe.wait_ge(hot_ready, 2)
                nc.tensor.matmul(banks[0][:, 0:4], ones_row[0:1, :], facts_row[:, :], start=True, stop=True).then_inc(z_done, 1)
                for n, table in enumerate((src_f, type_f, lasts)):
                    for a in range(BLOCKS):
                        last = nc.tensor.transpose(banks[1 + 2 * n + a // GROUP][:, (a % GROUP) * P:(a % GROUP + 1) * P],
                                                   table[:, a, :], ident[:, :])
                        if a % GROUP == GROUP - 1 or a == BLOCKS - 1:
                            last.then_inc(m_done, 1)
        block_end()

        take = carve()
        rel = take([BLOCKS, P])
        rel_bf = take([BLOCKS, P], BF16)
        rel_c, lastw, inside, work = (take([COLS]) for _ in range(4))
        picks = take([4])

        def window_tables(sweeps=None, by_edge=False):
            def guard(engine):
                return engine.If(sweeps > 1) if sweeps is not None else nullcontext()

            with nc.Block() as block:
                @block.sync
                def _(sp):
                    with guard(sp):
                        sp.wait_ge(scan_done, 1)
                        with nc.allow_non_contiguous_dma("rows of 256 bytes"):
                            sp.dma_start(rel_tab.rearrange("(a q) e -> q a e", q=P), rel_bf).then_inc(stored[0], 16)
                        sp.wait_ge(stored[0], 16)
                        stand(sp)

                @block.vector
                def _(dve):
                    with guard(dve):
                        link = linker(dve, chain)
                        if sweeps is not None:
                            step = 1.0 if by_edge else facts[:, 1:2]
                            link(nc.vector.tensor_scalar(shift[:, 2:3], shift[:, 2:3], step, None, ALU.add))
                            link(nc.vector.tensor_tensor(shift[:, 3:4], shift[:, 2:3], facts[:, 1:2], ALU.is_ge))
                            link(nc.vector.tensor_tensor(shift[:, 1:2], shift[:, 1:2], shift[:, 3:4], ALU.add))
                            link(nc.vector.tensor_tensor(shift[:, 3:4], shift[:, 3:4], facts[:, 1:2], ALU.mult))
                            link(nc.vector.tensor_tensor(shift[:, 2:3], shift[:, 2:3], shift[:, 3:4], ALU.subtract))
                            link(nc.vector.tensor_tensor(shift[:, 3:4], shift[:, 1:2], facts[:, 0:1], ALU.is_lt))
                            link(nc.vector.tensor_tensor(shift[:, 1:2], shift[:, 1:2], shift[:, 3:4], ALU.mult))
                            link(nc.vector.tensor_scalar(shift[:, 0:1], shift[:, 1:2], float(WINDOW), None, ALU.mult))
                        link(nc.vector.tensor_scalar(base_f[:, :], lo[:, :], shift[:, 0:1], None, ALU.add))
                        link(nc.vector.tensor_scalar(base_f[:, :], base_f[:, :], float(N), None, ALU.min))
                        nc.vector.tensor_tensor(rel, dst_f[:, :, :], base_f[:, :, None].to_broadcast([P, BLOCKS, P]),
                                                ALU.subtract).then_inc(hot_ready, 1)
                        dve.wait_ge(hot_ready, 1)
                        nc.vector.tensor_scalar(rel_bf, rel, -1.0, float(WINDOW), ALU.max, ALU.min).then_inc(scan_done, 1)
                        link(nc.vector.tensor_scalar(picks[:, 0:1], facts[:, 2:3], -1.0, 1.0, ALU.mult, ALU.add))
                        link(nc.vector.tensor_tensor(picks[:, 1:2], iota_p[:, :], shift[:, 2:3], ALU.is_equal))
                        link(nc.vector.tensor_tensor(picks[:, 2:3], picks[:, 1:2], facts[:, 2:3], ALU.mult))
                        link(nc.vector.tensor_scalar(lastw, last_c[:, :], picks[:, 0:1], picks[:, 2:3], ALU.mult, ALU.add))
                        dve.wait_ge(m_done, 1)
                        for a in range(0, BLOCKS, GROUP):
                            b = min(a + GROUP, BLOCKS)
                            link(nc.vector.tensor_copy(rel_c[:, a * P:b * P], banks[a // GROUP][:, 0:(b - a) * P]))
                            nc.vector.tensor_copy(base_i[:, a * P:b * P], banks[2 + a // GROUP][0:1, 0:(b - a) * P])
                        link(nc.vector.scalar_tensor_tensor(out=work, in0=rel_c, scalar=1.0, in1=lastw,
                                                            op0=ALU.add, op1=ALU.mult))
                        nc.vector.tensor_scalar(keys[:, :, 0], work, -1.0, None, ALU.add)
                        nc.vector.tensor_copy(keys[:, :, 1], rel_c)
                        link(nc.vector.tensor_scalar(inside, rel_c, 0.0, None, ALU.is_ge))
                        link(nc.vector.scalar_tensor_tensor(out=inside, in0=rel_c, scalar=WINDOW - 1.0, in1=inside,
                                                            op0=ALU.is_le, op1=ALU.mult))
                        link(nc.vector.scalar_tensor_tensor(out=work, in0=type_c, scalar=float(WINDOW), in1=rel_c,
                                                            op0=ALU.mult, op1=ALU.add))
                        link(nc.vector.scalar_tensor_tensor(out=work, in0=work, scalar=1.0, in1=inside,
                                                            op0=ALU.add, op1=ALU.mult))
                        nc.vector.tensor_scalar(key_rn[:, :], work, -1.0, None, ALU.add)

                @block.tensor
                def _(pe):
                    with guard(pe):
                        pe.wait_ge(hot_ready, 1)
                        for a in range(BLOCKS):
                            nc.tensor.transpose(banks[a // GROUP][:, (a % GROUP) * P:(a % GROUP + 1) * P], rel[:, a, :],
                                                ident[:, :])
                            last = nc.tensor.transpose(banks[2 + a // GROUP][0:1, (a % GROUP) * P:(a % GROUP + 1) * P],
                                                       base_f[:, a:a + 1], ident[:, :])
                        last.then_inc(m_done, 1)
            block_end()

        window_tables()

        take = carve()
        x_now = take([2, GROUP, P])
        xt = take([2, CHUNK])
        p_f = take([2, GROUP, P])
        p_parts = take([2, GROUP, SPLIT, P], BF16)
        q_rows = take([2, GROUP, P])

        def half16(c, k):
            return (c // 2) * 16 if isinstance(c, int) else (c - k) * 8

        with nc.Block() as block:
            @block.sync
            def _(sp):
                def step(c, k):
                    n = width(c) // P
                    sp.wait_ge(z_copied, c + 1)
                    sp.dma_start(q_tab[bass.ds(c * CHUNK, n * P), :].rearrange("(t p) d -> p t d", p=P),
                                 q_rows[:, k, 0:n, :]).then_inc(stored2[k], 16)
                    sp.wait_ge(m_done, c + 1)
                    sp.dma_start(p_tab[bass.ds(c * (CHUNK * SPLIT), n * P * SPLIT), :].rearrange("(t p c) d -> p t c d", p=P, c=SPLIT),
                                 p_parts[:, k, 0:n, :, :]).then_inc(stored[k], 16)
                run_steps(sp, step, CHUNKS, 0, 2)
                for k in range(2):
                    sp.wait_ge(stored[k], 16 * ((CHUNKS + 1 - k) // 2))
                    sp.wait_ge(stored2[k], 16 * ((CHUNKS + 1 - k) // 2))

            @block.tensor
            def _(pe):
                def step(c, k):
                    if active(c, 0, CHUNKS):
                        n = width(c) // P
                        pe.wait_ge(filled, c + 1)
                        if later(c, 2):
                            pe.wait_ge(turned_copied, c - 1)
                        for t in range(n):
                            last = nc.tensor.transpose(banks[k][:, t * P:(t + 1) * P], x_now[:, k, t, :], ident[:, :])
                        last.then_inc(turned, 1)
                    if active(c, 1, CHUNKS):
                        d, j = c - 1, (k + 1) % 2
                        n = width(d) // P
                        pe.wait_ge(turned_copied, d + 1)
                        if later(d, 2):
                            pe.wait_ge(chain, d * 5 - 9)
                            pe.wait_ge(z_copied, d - 1)
                        for t in range(n):
                            for half in range(2):
                                last = nc.tensor.matmul(banks[2 + 2 * half + j][:, t * P:(t + 1) * P], xt[:, j, t * P:(t + 1) * P],
                                                        w_pq[:, half * P:(half + 1) * P], start=(t == 0), stop=True,
                                                        skip_group_check=True)
                        last.then_inc(z_done, 1)
                run_steps(pe, step, CHUNKS, 1, 2)

            @block.scalar
            def _(act):
                def step(s, k):
                    j = (k + 1) % 2
                    if active(s, 0, CHUNKS):
                        w = width(s)
                        if later(s, 2):
                            act.wait_ge(turned, s - 1)
                        stand(act)
                        nc.scalar.copy(x_now[:, k, 0:w // P, :], res_buf[:, bass.ds(s * CHUNK, w)].rearrange("p (t d) -> p t d", d=P)
                                       ).then_inc(filled, 1)
                    if active(s, 1, CHUNKS):
                        c = s - 1
                        w = width(c)
                        act.wait_ge(turned, c + 1)
                        if later(c, 2):
                            act.wait_ge(z_done, c - 1)
                        nc.scalar.copy(xt[:, j, 0:w], banks[j][:, 0:w]).then_inc(turned_copied, 1)
                    if active(s, 2, CHUNKS):
                        c = s - 2
                        n = width(c) // P
                        act.wait_ge(z_done, c + 1)
                        if later(c, 2):
                            act.wait_ge(stored2[k], half16(c, k))
                        nc.scalar.copy(q_rows[:, k, 0:n, :], banks[4 + k][:, 0:n * P].rearrange("p (t d) -> p t d", d=P)
                                       ).then_inc(z_copied, 1)
                        act.wait_ge(chain, c * 5 + 5)
                        nc.scalar.copy(p_parts[:, k, 0:n, 2, :], p_f[:, k, 0:n, :]).then_inc(m_done, 1)
                run_steps(act, step, CHUNKS, 2, 2)

            @block.vector
            def _(dve):
                def step(c, k):
                    n = width(c) // P
                    left, parts = p_f[:, k, 0:n, :], p_parts[:, k, 0:n, :, :]
                    dve.wait_ge(z_done, c + 1)
                    if later(c, 2):
                        dve.wait_ge(stored[k], half16(c, k))
                        dve.wait_ge(m_done, c - 1)
                    nc.vector.tensor_tensor(left, banks[2 + k][:, 0:n * P].rearrange("p (t d) -> p t d", d=P),
                                            b1_rows[:, None, :].to_broadcast([P, n, P]), ALU.add).then_inc(chain, 1)
                    dve.wait_ge(chain, c * 5 + 1)
                    nc.vector.tensor_copy(parts[:, :, 0, :], left).then_inc(chain, 1)
                    dve.wait_ge(chain, c * 5 + 2)
                    nc.vector.tensor_tensor(left, left, parts[:, :, 0, :], ALU.subtract).then_inc(chain, 1)
                    dve.wait_ge(chain, c * 5 + 3)
                    nc.vector.tensor_copy(parts[:, :, 1, :], left).then_inc(chain, 1)
                    dve.wait_ge(chain, c * 5 + 4)
                    nc.vector.tensor_tensor(left, left, parts[:, :, 1, :], ALU.subtract).then_inc(chain, 1)
                run_steps(dve, step, CHUNKS, 0, 2)
        block_end()

        take = carve()
        rel_ring = take([SLOTS, GROUP * P], BF16, WINDOW * SPLIT)
        reset_ring = take([SLOTS, GROUP * P], BF16)
        p_ring = take([SLOTS * GROUP, P], BF16, WINDOW * SPLIT)
        hot = take([2, GROUP * P], BF16, WINDOW * SPLIT)
        zc = take([2, GROUP * P])
        er = take([2, GROUP * P])
        g_t = take([2, GROUP * P])
        scanned = take([2, GROUP * P])
        scanned_t = take([2, GROUP, P])
        select = take([2, GROUP, 3, WINDOW], BF16)
        select_f = take([2, GROUP, WINDOW])
        rel_flat = rel_tab.rearrange("t e -> (t e)")
        reset_flat = reset_tab.rearrange("t e -> (t e)")

        def gather_rows(pool, table, reader_done):
            def body(i):
                for g in range(SLOTS):
                    pool.wait_ge(idx_ready, i * SLOTS + g + 1)
                    if not isinstance(i, int):
                        pool.wait_ge(reader_done, (i - 1) * SLOTS + g + 1)
                    stand(pool)
                    for t in range(g * GROUP, (g + 1) * GROUP):
                        pool.indirect_dma_start(rows[:, t, :], None, table,
                                                bass.IndirectOffsetOnAxis(ap=idx_stage[:, t:t + 1], axis=0)
                                                ).then_inc(row_landed[t], 16)
            body(0)
            with pool.Fori(1, GROUPS // SLOTS) as i:
                body(i)

        def stage_indices(act, s, k):
            stand(act)
            nc.scalar.copy(idx_stage[:, k * GROUP:(k + 1) * GROUP],
                           src_c[:, bass.ds(s * GROUP, GROUP)]).then_inc(idx_ready, 1)

        def rows_here(pe, s, k, t):
            pe.wait_ge(row_landed[k * GROUP + t], (s // SLOTS + 1) * 16 if isinstance(s, int) else (s - k) * 4 + 16)

        def tile_bases(engine, s):
            _, values = nc.values_load_multi_w_load_instructions(
                base_i[0:1, bass.ds(s * GROUP, GROUP)], engines=[engine], min_val=0, max_val=N,
                skip_runtime_bounds_check_because="the tables hold no base above N")
            return values

        def edge_sweep():
            with nc.Block() as block:
                @block.gpsimd
                def _(pool):
                    gather_rows(pool, q_tab, z_done)

                @block.sync
                def _(sp):
                    def step(s, k):
                        if active(s, 0, GROUPS):
                            if later(s, SLOTS):
                                sp.wait_ge(z_done, s - SLOTS + 1)
                            sp.dma_start(rel_ring[:, k, :], rel_flat[None, bass.ds(s * (GROUP * P), GROUP * P)]
                                         .to_broadcast([WINDOW * SPLIT, GROUP * P])).then_inc(side_landed[k], 16)
                            for t, b in enumerate(tile_bases(SP, s)):
                                sp.dma_start(p_ring[:, k * GROUP + t, :], p_tab[bass.ds(b * SPLIT, WINDOW * SPLIT), :]
                                             ).then_inc(side_landed[k], 16)
                        if k % 2 == 0 and active(s, 2, GROUPS):
                            j, q = s - 2, 1 - k // 2
                            if later(j, SLOTS):
                                sp.wait_ge(scan_done, j - 2)
                            sp.dma_start(reset_ring[:, 2 * q:2 * q + 2, :], reset_flat[None, bass.ds(j * (GROUP * P), 2 * GROUP * P)]
                                         .rearrange("a (g e) -> a g e", g=2).to_broadcast([P, 2, GROUP * P])
                                         ).then_inc(reset_landed[q], 16)
                    run_steps(sp, step, GROUPS, 2, SLOTS)

                def side_here(engine, s, k):
                    engine.wait_ge(side_landed[k], (s // SLOTS + 1) * SIDE if isinstance(s, int) else (s - k) * (SIDE // SLOTS) + SIDE)

                @block.tensor
                def _(pe):
                    def step(s, k):
                        b, c = k % 2, (k + 1) % 2
                        if active(s, 5, GROUPS):
                            j = s - 5
                            pe.wait_ge(scan_done, j + 1)
                            if later(j, 1):
                                pe.wait_ge(turned_copied, j)
                            for t in range(GROUP):
                                last = nc.tensor.transpose(banks[5][:, t * P:(t + 1) * P],
                                                           scanned[:, c, t * P:(t + 1) * P], ident[:, :])
                            last.then_inc(turned, 1)
                        if active(s, 6, GROUPS):
                            j = s - 6
                            pe.wait_ge(select_ready, j + 1)
                            pe.wait_ge(turned_copied, j + 1)
                            pe.wait_ge(spread_ready, j + 1)
                            if later(j, 2):
                                pe.wait_ge(merged, (j - 1) * (2 * GROUP))
                            best = banks[6 + b][:, 0:GROUP * WINDOW]
                            nc.tensor.matmul(best.rearrange("p (t n) -> p t n", n=WINDOW), big_mat[:, :], select[:, b, :, 0, :],
                                             start=True, stop=False, skip_group_check=True)
                            nc.tensor.matmul(best, negbig_row[:, :], ones_bf[:, 0:GROUP * WINDOW], start=False,
                                             stop=False, skip_group_check=True)
                            for t in range(GROUP):
                                nc.tensor.matmul(best[:, t * WINDOW:(t + 1) * WINDOW], scanned_t[:, b, t, :],
                                                 select_f[:, b, t, :], start=False, stop=True, skip_group_check=True)
                                last = nc.tensor.matmul(
                                    banks[6 + b][0:R, (GROUP + t) * WINDOW:(GROUP + t + 1) * WINDOW],
                                    select[:, b, t, 2, 0:R], select[:, b, t, 1, :], start=False, stop=True,
                                    skip_group_check=True)
                            last.then_inc(window_done, 1)
                        if active(s, 1, GROUPS):
                            j, slot = s - 1, (k + 3) % SLOTS
                            side_here(pe, j, slot)
                            pe.wait_ge(hot_ready, j + 1)
                            if later(j, SLOTS):
                                pe.wait_ge(g_ready, j - 3)
                            for t in range(GROUP):
                                rows_here(pe, j, slot, t)
                                nc.tensor.matmul(banks[slot][:, t * P:(t + 1) * P], rows[:, slot * GROUP + t, :], ident[:, :],
                                                 start=(t == 0), stop=False, is_transpose=True, skip_group_check=True)
                                last = nc.tensor.matmul(banks[slot][:, t * P:(t + 1) * P], p_ring[:, slot * GROUP + t, :],
                                                        hot[:, c, t * P:(t + 1) * P], start=False, stop=True,
                                                        skip_group_check=True)
                            last.then_inc(z_done, 1)
                        if active(s, 3, GROUPS):
                            j = s - 3
                            pe.wait_ge(g_ready, j + 1)
                            if later(j, 1):
                                pe.wait_ge(scan_done, j)
                            nc.tensor.matmul(banks[4][:, :], w2m[:, :], g_t[:, c, :], start=True, stop=True).then_inc(m_done, 1)
                    run_steps(pe, step, GROUPS, 6, SLOTS)

                @block.scalar
                def _(act):
                    nc.scalar.preload_act_table_set("natural_log_exp_and_others")
                    for k in range(SLOTS):
                        stage_indices(act, k, k)

                    def step(s, k):
                        b, c = k % 2, (k + 1) % 2
                        if active(s, 2, GROUPS):
                            act.wait_ge(z_done, s - 1)
                            stage_indices(act, s - 2 + SLOTS, (k + 2) % SLOTS)
                        if active(s, 5, GROUPS):
                            j = s - 5
                            act.wait_ge(turned, j + 1)
                            if later(j, 2):
                                act.wait_ge(window_done, j - 1)
                            nc.scalar.copy(scanned_t[:, c, :, :], banks[5][:, :].rearrange("p (t d) -> p t d", d=P)
                                           ).then_inc(turned_copied, 1)
                        if active(s, 2, GROUPS):
                            j = s - 2
                            act.wait_ge(clamp_ready, j + 1)
                            if later(j, 2):
                                act.wait_ge(g_ready, j - 1)
                            now = er[:, b, :]
                            nc.scalar.activation(now, zc[:, b, :], ACT.Exp).then_inc(act_chain, 1)
                            act.wait_ge(act_chain, j * 3 + 1)
                            nc.scalar.activation(now, now, ACT.Square, bias=1.0).then_inc(act_chain, 1)
                            act.wait_ge(act_chain, j * 3 + 2)
                            nc.scalar.activation(now, now, ACT.Ln, bias=1.0).then_inc(act_chain, 1)
                            act.wait_ge(act_chain, j * 3 + 3)
                            nc.scalar.activation(now, now, ACT.Exp, scale=-1.0).then_inc(recip_ready, 1)
                        if active(s, 5, GROUPS):
                            j = s - 5
                            act.wait_ge(select_ready, j + 1)
                            nc.scalar.copy(select_f[:, c, :, :], select[:, c, :, 0, :]).then_inc(spread_ready, 1)
                    run_steps(act, step, GROUPS, 5, SLOTS)

                @block.vector
                def _(dve):
                    def step(s, k):
                        b, c = k % 2, (k + 1) % 2
                        if active(s, 2, GROUPS):
                            j = s - 2
                            dve.wait_ge(z_done, j + 1)
                            if later(j, 2):
                                dve.wait_ge(recip_ready, j - 1)
                            nc.vector.tensor_scalar(zc[:, b, :], banks[(k + 2) % SLOTS][:, :], EXP_LIMIT, None, ALU.min
                                                    ).then_inc(clamp_ready, 1)
                        if active(s, 3, GROUPS):
                            j = s - 3
                            dve.wait_ge(recip_ready, j + 1)
                            if later(j, 2):
                                dve.wait_ge(m_done, j - 1)
                            nc.vector.scalar_tensor_tensor(out=g_t[:, c, :], in0=er[:, c, :], scalar=-0.5,
                                                           in1=banks[(k + 1) % SLOTS][:, :], op0=ALU.add, op1=ALU.mult
                                                           ).then_inc(g_ready, 1)
                        if active(s, 4, GROUPS):
                            j, q = s - 4, k // 2
                            dve.wait_ge(m_done, j + 1)
                            dve.wait_ge(reset_landed[q], (j // SLOTS + 1) * 16 if isinstance(j, int) else (j - k) * 4 + 16)
                            if later(j, 2):
                                dve.wait_ge(turned, j - 1)
                            nc.vector.tensor_tensor_scan(scanned[:, b, :], reset_ring[:, k, :], banks[4][:, :],
                                                         0.0, ALU.add, ALU.max).then_inc(scan_done, 1)
                        if active(s, 0, GROUPS):
                            side_here(dve, s, k)
                            if later(s, 2):
                                dve.wait_ge(z_done, s - 1)
                            nc.vector.tensor_scalar(hot[:, b, :], rel_ring[:, k, :], iota_split[0:WINDOW * SPLIT, :], None,
                                                    ALU.is_equal).then_inc(hot_ready, 1)
                        if active(s, 5, GROUPS):
                            j = s - 5
                            if later(j, 2):
                                dve.wait_ge(window_done, j - 1)
                            nc.vector.tensor_tensor(
                                select[:, c, :, :, :],
                                iota_row[:, None, None, 0:WINDOW].to_broadcast([P, GROUP, 3, WINDOW]),
                                keys[:, bass.ds(j * GROUP, GROUP), :, None].to_broadcast([P, GROUP, 3, WINDOW]),
                                ALU.is_equal).then_inc(select_ready, 1)
                        if active(s, 7, GROUPS):
                            j = s - 7
                            dve.wait_ge(window_done, j + 1)
                            at = j * (2 * GROUP)
                            for t, w in enumerate(tile_bases(DVE, j)):
                                if later(j, 1) or t:
                                    dve.wait_ge(merged, at + 2 * t)
                                nc.vector.tensor_tensor(acc[:, bass.ds(w, WINDOW)], acc[:, bass.ds(w, WINDOW)],
                                                        banks[6 + c][:, t * WINDOW:(t + 1) * WINDOW], ALU.max).then_inc(merged, 1)
                                nc.vector.tensor_tensor(cnt[:, bass.ds(w, WINDOW)], cnt[:, bass.ds(w, WINDOW)],
                                                        banks[6 + c][0:R, (GROUP + t) * WINDOW:(GROUP + t + 1) * WINDOW],
                                                        ALU.add).then_inc(merged, 1)
                    run_steps(dve, step, GROUPS, 7, SLOTS)
            block_end()

        sweeps = nc.values_load(passes_i[0:1, 0:1], min_val=1, max_val=P * (MAX_STEPS + 1),
                                skip_runtime_bounds_check_because="the kernel works it out from spans of at most N")
        with nc.Fori(0, sweeps):
            edge_sweep()
            window_tables(sweeps, True)

        take = carve()
        nodes_ok = take([2, WIDE * STAT])
        stats = take([STATS, 6])
        mv = take([8])
        factor = take([NP // P, R])
        factor_parts = take([NP // P, SPLIT, R], BF16)
        with nc.Block() as block:
            @block.sync
            def _(sp):
                sp.wait_ge(spread_ready, 1)
                with nc.allow_non_contiguous_dma("rows of 48 bytes"):
                    sp.dma_start(fac_tab.rearrange("(t p) m -> p t m", p=P),
                                 factor_parts.rearrange("p t c r -> p t (c r)")).then_inc(stored[0], 16)
                sp.wait_ge(stored[0], 16)

            @block.tensor
            def _(pe):
                for t in range(NP // P):
                    last = nc.tensor.transpose(banks[0][:, t * R:(t + 1) * R], cnt[:, t * P:(t + 1) * P], ident[0:R, 0:R])
                last.then_inc(turned, 1)

            @block.vector
            def _(dve):
                link = linker(dve, chain)
                dve.wait_ge(turned, 1)
                link(nc.vector.tensor_scalar(factor, banks[0][:, 0:NP // P * R].rearrange("p (t r) -> p t r", r=R),
                                             facts[:, 3:4], 1.0, ALU.mult, ALU.max))
                link(nc.vector.reciprocal(factor, factor))
                link(nc.vector.tensor_copy(factor_parts[:, :, 0, :], factor))
                link(nc.vector.tensor_tensor(factor, factor, factor_parts[:, :, 0, :], ALU.subtract))
                link(nc.vector.tensor_copy(factor_parts[:, :, 1, :], factor))
                link(nc.vector.tensor_tensor(factor, factor, factor_parts[:, :, 1, :], ALU.subtract))
                nc.vector.tensor_copy(factor_parts[:, :, 2, :], factor).then_inc(spread_ready, 1)
                nc.vector.memset(acc[:, N:NP], 0.0)

                def part(s, k):
                    here = acc[:, bass.ds(s * (WIDE * STAT), WIDE * STAT)]
                    ok = nodes_ok[:, k, :]
                    nc.vector.tensor_scalar(ok, here, -BIG / 2, None, ALU.is_gt).then_inc(scaled, 1)
                    dve.wait_ge(scaled, s * 2 + 1)
                    nc.vector.scalar_tensor_tensor(out=here, in0=here, scalar=cols[:, 0:1], in1=ok, op0=ALU.add,
                                                   op1=ALU.mult).then_inc(scaled, 1)
                    dve.wait_ge(scaled, s * 2 + 2)
                    for g in range(WIDE):
                        last = nc.vector.bn_stats(stats[:, bass.ds(s * WIDE + g, 1), :],
                                                  acc[:, bass.ds((s * WIDE + g) * STAT, STAT)])
                    last.then_inc(m_done, 1)
                for s in range(STATS // WIDE):
                    if s > 1:
                        dve.wait_ge(scaled, s * 2 - 2)
                    part(s, s % 2)
                dve.wait_ge(m_done, STATS // WIDE)
                link(nc.vector.bn_aggr(mv[:, 0:2], stats))
                nc.vector.tensor_scalar(mv[:, 2:3], mv[:, 1:2], EPS, None, ALU.add).then_inc(hot_ready, 1)
                dve.wait_ge(z_copied, 1)
                link(nc.vector.reciprocal(mv[:, 4:5], mv[:, 3:4]))
                link(nc.vector.tensor_tensor(norm[:, 0:1], mv[:, 4:5], cols[:, 1:2], ALU.mult))
                link(nc.vector.tensor_tensor(mv[:, 5:6], mv[:, 0:1], norm[:, 0:1], ALU.mult))
                nc.vector.tensor_tensor(norm[:, 1:2], cols[:, 2:3], mv[:, 5:6], ALU.subtract)

            @block.scalar
            def _(act):
                act.wait_ge(hot_ready, 1)
                nc.scalar.activation(mv[:, 3:4], mv[:, 2:3], ACT.Sqrt).then_inc(z_copied, 1)
                link = linker(act, act_chain)
                link(nc.scalar.copy(w_cur[:, :], w_all[:, 0:R * P]))
                link(nc.scalar.copy(b_cur[:, :], cols[:, 4:5]))
        block_end()

        take = carve()
        y_t = take([2, CHUNK])
        v_rows = take([2, GROUP, P])
        x1_rows = take([2, GROUP, P])
        x1_t = take([2, CHUNK])
        ln_stats = take([2, GROUP, 6])
        ln_mv = take([2, GROUP, 2])
        ln_sd = take([2, GROUP])
        y_rows = take([2, GROUP, P])
        ln_shift = take([2, GROUP])

        def ln_stats_of(dve, c, k, n):
            for t in range(n):
                last = nc.vector.bn_stats(ln_stats[:, k, t, :], v_rows[:, k, t, :])
            last.then_inc(chain, 1)
            dve.wait_ge(chain, c * 2 + 1)
            stand(dve)
            for t in range(n):
                last = nc.vector.bn_aggr(ln_mv[:, k, t, :], ln_stats[:, k, t, :])
            last.then_inc(chain, 1)
            dve.wait_ge(chain, c * 2 + 2)
            nc.vector.tensor_scalar(ln_sd[:, k, 0:n], ln_mv[:, k, 0:n, 1], EPS, None, ALU.add).then_inc(hot_ready, 1)

        def ln_apply(dve, c, k, n):
            nc.vector.reciprocal(ln_sd[:, k, 0:n], ln_sd[:, k, 0:n]).then_inc(g_ready, 1)
            dve.wait_ge(g_ready, c + 1)
            for t in range(n):
                last = nc.vector.tensor_scalar(x1_rows[:, k, t, :], v_rows[:, k, t, :], ln_mv[:, k, t, 0:1],
                                               ln_sd[:, k, t:t + 1], ALU.subtract, ALU.mult)
            last.then_inc(scaled, 1)

        def ln_root(act, k, n):
            nc.scalar.activation(ln_sd[:, k, 0:n], ln_sd[:, k, 0:n], ACT.Sqrt).then_inc(recip_ready, 1)

        with nc.Block() as block:
            @block.sync
            def _(sp):
                def step(c, k):
                    if active(c, 2, CHUNKS):
                        d = c - 2
                        n = width(d) // P
                        sp.wait_ge(scaled, d + 1)
                        for table, done in ((h_tab, stored), (x1_tab, stored2)):
                            sp.dma_start(table[bass.ds(d * CHUNK, n * P), :].rearrange("(t p) d -> p t d", p=P),
                                         x1_rows[:, k, 0:n, :]).then_inc(done[k], 16)
                run_steps(sp, step, CHUNKS, 2, 2)
                for k in range(2):
                    sp.wait_ge(stored[k], 16 * ((CHUNKS + 1 - k) // 2))
                    sp.wait_ge(stored2[k], 16 * ((CHUNKS + 1 - k) // 2))

            @block.scalar
            def _(act):
                def step(s, k):
                    j = (k + 1) % 2
                    if active(s, 3, CHUNKS):
                        c = s - 3
                        w = width(c)
                        act.wait_ge(m_done, c + 1)
                        if later(c, 2):
                            act.wait_ge(window_done, c - 1)
                        nc.scalar.copy(x1_t[:, j, 0:w], banks[2 + j][:, 0:w]).then_inc(turned_copied, 1)
                    if active(s, 0, CHUNKS):
                        w = width(s)
                        if later(s, 2):
                            act.wait_ge(turned, s - 1)
                        nc.scalar.activation(y_t[:, k, 0:w], acc[:, bass.ds(s * CHUNK, w)], ACT.Identity,
                                             bias=norm[:, 1:2], scale=norm[:, 0:1]).then_inc(clamp_ready, 1)
                    if active(s, 4, CHUNKS):
                        c = s - 4
                        w = width(c)
                        act.wait_ge(window_done, c + 1)
                        act.wait_ge(filled, c + 1)
                        stand(act)
                        nc.scalar.copy(acc[:, bass.ds(c * CHUNK, w)], banks[4 + k][:, 0:w]).then_inc(z_copied, 1)
                        nc.scalar.activation(res_buf[:, bass.ds(c * CHUNK, w)], banks[6 + k][:, 0:w], ACT.Identity,
                                             bias=cols[:, 3:4]).then_inc(z_copied, 1)
                    if active(s, 1, CHUNKS):
                        act.wait_ge(hot_ready, s)
                        ln_root(act, j, width(s - 1) // P)
                run_steps(act, step, CHUNKS, 4, 2)

            @block.tensor
            def _(pe):
                def step(s, k):
                    j = (k + 1) % 2
                    if active(s, 3, CHUNKS):
                        c = s - 3
                        w = width(c)
                        pe.wait_ge(turned_copied, c + 1)
                        if later(c, 2):
                            pe.wait_ge(z_copied, 2 * c - 2)
                        nc.tensor.matmul(banks[4 + j][:, 0:w], root_all[:, 0:P], x1_t[:, j, 0:w], start=True, stop=True)
                        nc.tensor.matmul(banks[6 + j][:, 0:w], resw_sb[:, :], x1_t[:, j, 0:w], start=True, stop=True
                                         ).then_inc(window_done, 1)
                    if active(s, 0, CHUNKS):
                        pe.wait_ge(clamp_ready, s + 1)
                        if later(s, 2):
                            pe.wait_ge(filled, s - 1)
                        for t in range(width(s) // P):
                            last = nc.tensor.transpose(banks[k][:, t * P:(t + 1) * P], y_t[:, k, t * P:(t + 1) * P], ident[:, :])
                        last.then_inc(turned, 1)
                    if active(s, 2, CHUNKS):
                        c = s - 2
                        pe.wait_ge(scaled, c + 1)
                        if later(c, 2):
                            pe.wait_ge(turned_copied, c - 1)
                        for t in range(width(c) // P):
                            last = nc.tensor.transpose(banks[2 + k][:, t * P:(t + 1) * P], x1_rows[:, k, t, :], ident[:, :])
                        last.then_inc(m_done, 1)
                run_steps(pe, step, CHUNKS, 3, 2)

            @block.vector
            def _(dve):
                def step(s, k):
                    j = (k + 1) % 2
                    if active(s, 2, CHUNKS):
                        c = s - 2
                        dve.wait_ge(recip_ready, c + 1)
                        if later(c, 2):
                            dve.wait_ge(stored[k], half16(c, k))
                            dve.wait_ge(stored2[k], half16(c, k))
                            dve.wait_ge(m_done, c - 1)
                        ln_apply(dve, c, k, width(c) // P)
                    if active(s, 1, CHUNKS):
                        c = s - 1
                        n = width(c) // P
                        dve.wait_ge(turned, c + 1)
                        if later(c, 2):
                            dve.wait_ge(scaled, c - 1)
                        nc.vector.tensor_tensor(v_rows[:, j, 0:n, :], banks[j][:, 0:n * P].rearrange("p (t d) -> p t d", d=P),
                                                res_buf[:, bass.ds(c * CHUNK, n * P)].rearrange("p (t d) -> p t d", d=P),
                                                ALU.add).then_inc(filled, 1)
                        dve.wait_ge(filled, c + 1)
                        ln_stats_of(dve, c, j, n)
                run_steps(dve, step, CHUNKS, 2, 2)

        block_end()

        take = carve()
        rel_ring16 = take([SLOTS, GROUP * P], BF16, WINDOW)
        fac_ring = take([SLOTS * GROUP, SPLIT * R], BF16, WINDOW)
        hot16 = take([2, GROUP * P], BF16, WINDOW)
        type_sel = take([2, GROUP, 1, R])
        fac_sel = take([2, GROUP, SPLIT * R])
        edge_fac = take([2, GROUP])
        key_now = take([2, GROUP])
        onehot = take([2, GROUP, P])
        z_sb = take([2, 2 * GROUP, R, WINDOW])

        def conv_sweep():
            with nc.Block() as block:
                @block.gpsimd
                def _(pool):
                    gather_rows(pool, h_tab, z_done)

                @block.sync
                def _(sp):
                    def step(s, k):
                        if later(s, SLOTS):
                            sp.wait_ge(m_done, s - SLOTS + 1)
                        sp.dma_start(rel_ring16[:, k, :], rel_flat[None, bass.ds(s * (GROUP * P), GROUP * P)]
                                     .to_broadcast([WINDOW, GROUP * P])).then_inc(side_landed[k], 16)
                        for t, b in enumerate(tile_bases(SP, s)):
                            sp.dma_start(fac_ring[:, k * GROUP + t, :], fac_tab[bass.ds(b, WINDOW), :]
                                         ).then_inc(side_landed[k], 16)
                    run_steps(sp, step, GROUPS, 0, SLOTS)

                def side_here(engine, s, k):
                    engine.wait_ge(side_landed[k], (s // SLOTS + 1) * SIDE if isinstance(s, int)
                                   else (s - k) * (SIDE // SLOTS) + SIDE)

                @block.tensor
                def _(pe):
                    def step(s, k):
                        b, c = k % 2, (k + 1) % 2
                        if active(s, 3, GROUPS):
                            j, slot = s - 3, (k + 1) % SLOTS
                            pe.wait_ge(select_ready, j + 1)
                            if later(j, 2):
                                pe.wait_ge(z_copied, j - 1)
                            for t in range(GROUP):
                                rows_here(pe, j, slot, t)
                                last = nc.tensor.matmul(banks[c][:, t * P:(t + 1) * P], rows[:, slot * GROUP + t, :],
                                                        onehot[:, c, t, :], start=(t == 0), stop=True, skip_group_check=True)
                            last.then_inc(z_done, 1)
                        if active(s, 1, GROUPS):
                            j, slot = s - 1, (k + 3) % SLOTS
                            side_here(pe, j, slot)
                            pe.wait_ge(hot_ready, j + 1)
                            if later(j, 2):
                                pe.wait_ge(scaled, j - 1)
                            for t in range(GROUP):
                                last = nc.tensor.matmul(banks[6 + c][:, t * SPLIT * R:(t + 1) * SPLIT * R],
                                                        hot16[:, c, t * P:(t + 1) * P], fac_ring[:, slot * GROUP + t, :],
                                                        start=(t == 0), stop=True, skip_group_check=True)
                            last.then_inc(m_done, 1)
                        if k % 2 == 0 and active(s, 5, GROUPS):
                            j, q = s - 5, 1 - k // 2
                            pe.wait_ge(z_copied, j + 1)
                            if later(j, 4):
                                pe.wait_ge(merged, (j - 3) * GROUP)
                            for r in range(R):
                                last = nc.tensor.matmul(banks[4 + q][:, 0:2 * GROUP * WINDOW].rearrange("p (t n) -> p t n", n=WINDOW),
                                                        w_cur[:, r * P:(r + 1) * P],
                                                        z_sb[:, q, :, r, :], start=(r == 0), stop=(r == R - 1))
                            last.then_inc(window_done, 2)
                    run_steps(pe, step, GROUPS, 5, SLOTS)

                @block.scalar
                def _(act):
                    for k in range(SLOTS):
                        stage_indices(act, k, k)

                    def step(s, k):
                        if active(s, 3, GROUPS):
                            j, slot = s - 3, (k + 1) % SLOTS
                            q, half = slot // 2, slot % 2
                            act.wait_ge(z_done, j + 1)
                            stage_indices(act, j + SLOTS, slot)
                            if later(j, 4):
                                act.wait_ge(window_done, j - 3 if half else j - 2)
                            nc.scalar.copy(z_sb[:, q, half * GROUP:(half + 1) * GROUP, :, :],
                                           banks[half][:, :].rearrange("p (t r n) -> p t r n", r=R, n=WINDOW)
                                           ).then_inc(z_copied, 1)
                    run_steps(act, step, GROUPS, 3, SLOTS)

                @block.vector
                def _(dve):
                    def step(s, k):
                        b, c = k % 2, (k + 1) % 2
                        if active(s, 2, GROUPS):
                            j = s - 2
                            if later(j, 2):
                                dve.wait_ge(z_done, j - 1)
                            nc.vector.tensor_tensor(type_sel[:, b, :, 0, :], iota_row[:, None, 0:R].to_broadcast([P, GROUP, R]),
                                                    type_c[:, bass.ds(j * GROUP, GROUP), None].to_broadcast([P, GROUP, R]),
                                                    ALU.is_equal).then_inc(chain, 1)
                            nc.vector.tensor_copy(key_now[:, b, :], key_rn[:, bass.ds(j * GROUP, GROUP)])
                            dve.wait_ge(chain, j * 2 + 1)
                            dve.wait_ge(m_done, j + 1)
                            nc.vector.tensor_tensor(fac_sel[:, b, :, :].rearrange("p t (c r) -> p t c r", r=R),
                                                    banks[6 + b][:, 0:GROUP * SPLIT * R].rearrange("p (t c r) -> p t c r", c=SPLIT, r=R),
                                                    type_sel[:, b, :, :, :].to_broadcast([P, GROUP, SPLIT, R]),
                                                    ALU.mult).then_inc(scaled, 1)
                            dve.wait_ge(scaled, j + 1)
                            nc.vector.tensor_reduce(edge_fac[:, b, :], fac_sel[:, b, :, :], AX.X, ALU.add).then_inc(chain, 1)
                            dve.wait_ge(chain, j * 2 + 2)
                            for t in range(GROUP):
                                last = nc.vector.tensor_scalar(onehot[:, b, t, :], iota_row[:, :],
                                                               key_now[:, b, t:t + 1], edge_fac[:, b, t:t + 1],
                                                               ALU.is_equal, ALU.mult)
                            last.then_inc(select_ready, 1)
                        if active(s, 0, GROUPS):
                            side_here(dve, s, k)
                            if later(s, 2):
                                dve.wait_ge(m_done, s - 1)
                            nc.vector.tensor_scalar(hot16[:, b, :], rel_ring16[:, k, :], iota_p[0:WINDOW, :], None,
                                                    ALU.is_equal).then_inc(hot_ready, 1)
                        if active(s, 7, GROUPS):
                            j, slot = s - 7, (k + 1) % SLOTS
                            q, half = slot // 2, slot % 2
                            dve.wait_ge(window_done, j + 1 if half else j + 2)
                            for t, w in enumerate(tile_bases(DVE, j)):
                                if later(j, 1) or t:
                                    dve.wait_ge(merged, j * GROUP + t)
                                col = (half * GROUP + t) * WINDOW
                                nc.vector.tensor_tensor(acc[:, bass.ds(w, WINDOW)], acc[:, bass.ds(w, WINDOW)],
                                                        banks[4 + q][:, col:col + WINDOW], ALU.add).then_inc(merged, 1)
                    run_steps(dve, step, GROUPS, 7, SLOTS)
            block_end()

        take = carve()
        relu_t = take([2, CHUNK])
        h_t = take([2, CHUNK])
        h_rows = take([2, GROUP, P])

        def node_update(layer):
            with nc.Block() as block:
                @block.scalar
                def _(act):
                    nc.scalar.copy(root_cur[:, :], root_all[:, bass.ds((layer + 1) * P, P)]).then_inc(act_chain, 1)

                    def step(c, k):
                        if active(c, 0, CHUNKS):
                            w = width(c)
                            if later(c, 2):
                                act.wait_ge(g_ready, c - 1)
                            nc.scalar.activation(relu_t[:, k, 0:w], acc[:, bass.ds(c * CHUNK, w)], ACT.Relu,
                                                 bias=b_cur[:, :]).then_inc(clamp_ready, 1)
                        if active(c, 2, CHUNKS):
                            d = c - 2
                            w = width(d)
                            act.wait_ge(z_done, d + 1)
                            act.wait_ge(clamp_ready, d + 1)
                            stand(act)
                            nc.scalar.copy(acc[:, bass.ds(d * CHUNK, w)], banks[2 + k][:, 0:w]).then_inc(z_copied, 1)
                    run_steps(act, step, CHUNKS, 2, 2)
                    act.wait_ge(clamp_ready, CHUNKS)
                    nc.scalar.copy(w_cur[:, :], w_all[:, bass.ds((layer + 1) * (R * P), R * P)])
                    nc.scalar.copy(b_cur[:, :], cols[:, bass.ds(layer + 5, 1)])

                @block.vector
                def _(dve):
                    def step(c, k):
                        if active(c, 0, CHUNKS):
                            w = width(c)
                            dve.wait_ge(clamp_ready, c + 1)
                            if later(c, 2):
                                dve.wait_ge(z_done, c - 1)
                            nc.vector.tensor_tensor(h_t[:, k, 0:w], relu_t[:, k, 0:w], res_buf[:, bass.ds(c * CHUNK, w)],
                                                    ALU.add).then_inc(g_ready, 1)
                        if active(c, 1, CHUNKS):
                            d, j = c - 1, (k + 1) % 2
                            n = width(d) // P
                            dve.wait_ge(turned, d + 1)
                            if later(d, 2):
                                dve.wait_ge(stored[j], half16(d, j))
                            nc.vector.tensor_copy(h_rows[:, j, 0:n, :], banks[j][:, 0:n * P].rearrange("p (t d) -> p t d", d=P)
                                                  ).then_inc(turned_copied, 1)
                    run_steps(dve, step, CHUNKS, 1, 2)

                @block.tensor
                def _(pe):
                    pe.wait_ge(act_chain, 1)

                    def step(c, k):
                        w = width(c)
                        pe.wait_ge(g_ready, c + 1)
                        if later(c, 2):
                            pe.wait_ge(turned_copied, c - 1)
                        for t in range(w // P):
                            last = nc.tensor.transpose(banks[k][:, t * P:(t + 1) * P], h_t[:, k, t * P:(t + 1) * P], ident[:, :])
                        last.then_inc(turned, 1)
                        if later(c, 2):
                            pe.wait_ge(z_copied, c - 1)
                        nc.tensor.matmul(banks[2 + k][:, 0:w], root_cur[:, :], h_t[:, k, 0:w], start=True, stop=True
                                         ).then_inc(z_done, 1)
                    run_steps(pe, step, CHUNKS, 0, 2)

                @block.sync
                def _(sp):
                    def step(c, k):
                        n = width(c) // P
                        sp.wait_ge(turned_copied, c + 1)
                        sp.dma_start(h_tab[bass.ds(c * CHUNK, n * P), :].rearrange("(t p) d -> p t d", p=P),
                                     h_rows[:, k, 0:n, :]).then_inc(stored[k], 16)
                    run_steps(sp, step, CHUNKS, 0, 2)
                    for k in range(2):
                        sp.wait_ge(stored[k], 16 * ((CHUNKS + 1 - k) // 2))
            block_end()

        def conv_windows():
            windows = nc.values_load(passes_i[0:1, 1:2], min_val=1, max_val=MAX_STEPS + 1,
                                     skip_runtime_bounds_check_because="the kernel works it out from spans of at most N")
            with nc.Fori(0, windows):
                conv_sweep()
                window_tables(windows, False)

        with nc.Fori(0, LAYERS - 1) as layer:
            conv_windows()
            node_update(layer)
        conv_windows()

        relu_l, h_l = x1_t, y_t
        with nc.Block() as block:
            @block.sync
            def _(sp):
                def step(s, k):
                    if active(s, 0, CHUNKS):
                        n = width(s) // P
                        if later(s, 2):
                            sp.wait_ge(filled, s - 1)
                        sp.dma_start(y_rows[:, k, 0:n, :], x1_tab[bass.ds(s * CHUNK, n * P), :].rearrange("(t p) d -> p t d", p=P)
                                     ).then_inc(landed2[k], 16)
                    if active(s, 3, CHUNKS):
                        c, j = s - 3, (k + 1) % 2
                        sp.wait_ge(scaled, c + 1)
                        if isinstance(c, int) and c == CHUNKS - 1:
                            sp.dma_start(out[c * CHUNK:N, :], x1_rows[0:N - c * CHUNK, j, 0, :]).then_inc(stored[j], 16)
                        else:
                            sp.dma_start(out[bass.ds(c * CHUNK, CHUNK), :].rearrange("(t p) d -> p t d", p=P),
                                         x1_rows[:, j, :, :]).then_inc(stored[j], 16)
                run_steps(sp, step, CHUNKS, 3, 2)
                for k in range(2):
                    sp.wait_ge(stored[k], 16 * ((CHUNKS + 1 - k) // 2))

            @block.tensor
            def _(pe):
                def step(c, k):
                    pe.wait_ge(select_ready, c + 1)
                    if later(c, 2):
                        pe.wait_ge(filled, c - 1)
                    for t in range(width(c) // P):
                        last = nc.tensor.transpose(banks[k][:, t * P:(t + 1) * P], h_l[:, k, t * P:(t + 1) * P], ident[:, :])
                    last.then_inc(turned, 1)
                run_steps(pe, step, CHUNKS, 0, 2)

            @block.scalar
            def _(act):
                def step(s, k):
                    j = (k + 1) % 2
                    if active(s, 0, CHUNKS):
                        w = width(s)
                        if later(s, 2):
                            act.wait_ge(select_ready, s - 1)
                        nc.scalar.activation(relu_l[:, k, 0:w], acc[:, bass.ds(s * CHUNK, w)], ACT.Relu,
                                             bias=b_cur[:, :]).then_inc(clamp_ready, 1)
                    if active(s, 2, CHUNKS):
                        c = s - 2
                        act.wait_ge(g_ready, 2 * c + 2)
                        if later(c, 2):
                            act.wait_ge(stored[k], half16(c, k))
                        for t in range(width(c) // P):
                            last = nc.scalar.activation(x1_rows[:, k, t, :], v_rows[:, k, t, :], ACT.Identity,
                                                        bias=ln_shift[:, k, t:t + 1], scale=ln_sd[:, k, t:t + 1])
                        last.then_inc(scaled, 1)
                    if active(s, 1, CHUNKS):
                        act.wait_ge(hot_ready, s)
                        ln_root(act, j, width(s - 1) // P)
                run_steps(act, step, CHUNKS, 2, 2)

            @block.vector
            def _(dve):
                def step(s, k):
                    j = (k + 1) % 2
                    if active(s, 2, CHUNKS):
                        c = s - 2
                        n = width(c) // P
                        dve.wait_ge(recip_ready, c + 1)
                        nc.vector.reciprocal(ln_sd[:, k, 0:n], ln_sd[:, k, 0:n]).then_inc(g_ready, 1)
                        dve.wait_ge(g_ready, 2 * c + 1)
                        nc.vector.scalar_tensor_tensor(out=ln_shift[:, k, 0:n], in0=ln_mv[:, k, 0:n, 0], scalar=-1.0,
                                                       in1=ln_sd[:, k, 0:n], op0=ALU.mult, op1=ALU.mult).then_inc(g_ready, 1)
                    if active(s, 0, CHUNKS):
                        w = width(s)
                        dve.wait_ge(clamp_ready, s + 1)
                        if later(s, 2):
                            dve.wait_ge(turned, s - 1)
                        nc.vector.tensor_tensor(h_l[:, k, 0:w], relu_l[:, k, 0:w], res_buf[:, bass.ds(s * CHUNK, w)],
                                                ALU.add).then_inc(select_ready, 1)
                    if active(s, 1, CHUNKS):
                        c = s - 1
                        n = width(c) // P
                        dve.wait_ge(turned, c + 1)
                        dve.wait_ge(landed2[j], half16(c, j) + 16)
                        if later(c, 2):
                            dve.wait_ge(scaled, c - 1)
                        nc.vector.tensor_tensor(v_rows[:, j, 0:n, :], banks[j][:, 0:n * P].rearrange("p (t d) -> p t d", d=P),
                                                y_rows[:, j, 0:n, :], ALU.add).then_inc(filled, 1)
                        dve.wait_ge(filled, c + 1)
                        ln_stats_of(dve, c, j, n)
                run_steps(dve, step, CHUNKS, 2, 2)


_INS = ["x", "src", "dst", "edge_type_8",
        "L0_gnn_W1", "L0_gnn_b1", "L0_gnn_W2", "L0_gnn_b2", "L0_gnn_gamma", "L0_gnn_beta",
        "L1_gnn_W1", "L1_gnn_root1", "L1_gnn_b1", "L1_gnn_W2", "L1_gnn_root2", "L1_gnn_b2",
        "L1_gnn_W3", "L1_gnn_root3", "L1_gnn_b3", "L1_gnn_res_w", "L1_gnn_res_b"]


def kernel(**inputs):
    import numpy as _np
    import concourse.bacc as _bacc
    from concourse import mybir as _mybir
    from concourse.bass_utils import run_bass_kernel_spmd as _run

    nc = _bacc.Bacc("TRN2", target_bir_lowering=False, num_devices=1)
    arrays, t = {}, {}
    for name in _INS:
        a = _np.ascontiguousarray(inputs[name])
        arrays[f"in_{name}_dram"] = a
        t[name] = nc.dram_tensor(f"in_{name}_dram", a.shape, _mybir.dt.from_np(a.dtype), kind="ExternalInput").ap()
    shape = tuple(inputs["x"].shape)
    out = nc.dram_tensor("out_0_dram", shape, _mybir.dt.float32, kind="ExternalOutput").ap()
    build_gnn(nc, t["x"], t["src"], t["dst"], t["edge_type_8"], t["L0_gnn_W1"], t["L0_gnn_b1"], t["L0_gnn_W2"],
              t["L0_gnn_b2"], t["L0_gnn_gamma"], t["L0_gnn_beta"],
              [t["L1_gnn_W1"], t["L1_gnn_W2"], t["L1_gnn_W3"]],
              [t["L1_gnn_root1"], t["L1_gnn_root2"], t["L1_gnn_root3"]],
              [t["L1_gnn_b1"], t["L1_gnn_b2"], t["L1_gnn_b3"]], t["L1_gnn_res_w"], t["L1_gnn_res_b"], out)
    r = _run(nc, [arrays], core_ids=[0])
    return r.results[0]["out_0_dram"]
```
